# Optimizing a Trainium2 kernel written in Bass

```python
import numpy as np
import jax
import jax.numpy as jnp

def _softmax(x, axis=-1):
    return jax.nn.softmax(x, axis=axis)

def _gelu(x):
    return jax.nn.gelu(x, approximate=True)

def _silu(x):
    return jax.nn.silu(x)

def _sigmoid(x):
    return jax.nn.sigmoid(x)

def _layernorm(x, axis=-1, eps=1e-05):
    m = jnp.mean(x, axis=axis, keepdims=True)
    v = jnp.var(x, axis=axis, keepdims=True)
    return (x - m) / jnp.sqrt(v + eps)

def _scatter_add(tgt, idx, src, axis=0):
    return tgt.at[idx].add(src)

def _segment_sum(src, seg, n):
    return jax.ops.segment_sum(src, seg, n)
kernel_name = 'mk_decoder_preln_d2_seqx_r8_7065a0'

def setup_inputs(seed: int=0):
    np.random.seed(seed)
    _w = jnp.asarray

    def _rec_inputs():
        import jax
        import jax.numpy as jnp
        _rk = jax.random.key(seed)
        x = -0.0003929 + 0.9999 * jax.random.normal(jax.random.fold_in(_rk, 1), (32, 100, 128), jnp.float32)
        _lenS = 100 - jax.random.randint(jax.random.fold_in(_rk, 7), (32,), 0, max(1, 100 // 4) + 1, jnp.int32)
        _lenS2 = 1444 - jax.random.randint(jax.random.fold_in(_rk, 8), (32,), 0, max(1, 1444 // 4) + 1, jnp.int32)
        _ctx_1024P = jax.random.normal(jax.random.fold_in(_rk, 11), (32, 16, 128), jnp.float32)
        _ctx_1024c = jax.random.dirichlet(jax.random.fold_in(_rk, 511), 0.3 * jnp.ones((16,), jnp.float32), (32, 1444))
        _ctx_1024t = jnp.einsum('bsk,bkd->bsd', _ctx_1024c, _ctx_1024P)
        _ctx_1024t = _ctx_1024t * jax.lax.rsqrt(jnp.mean(jnp.square(_ctx_1024t)) + 1e-12) * 0.953939
        ctx_1024 = -1.39393e-06 + 0.999914 * (_ctx_1024t + 0.3 * jax.random.normal(jax.random.fold_in(_rk, 611), (32, 1444, 128), jnp.float32))
        _validS = jnp.arange(100)[None, :] < _lenS[:, None]
        _validS2 = jnp.arange(1444)[None, :] < _lenS2[:, None]
        _causal = jnp.tril(jnp.ones((100, 100), dtype=bool))
        mask_BxS2_bk0 = jnp.logical_not(jnp.broadcast_to(_validS2[:, :], (32, 1444)))
        return (x, ctx_1024, mask_BxS2_bk0)
    x, ctx_1024, mask_BxS2_bk0 = _rec_inputs()

    def _L0_attn_setup():
        import jax, jax.numpy as jnp
        import numpy as np
        H = 16
        ROPE_BASE = 10000.0

        def _rotate_half(x):
            d = x.shape[-1]
            return jnp.concatenate((-x[..., d // 2:], x[..., :d // 2]), axis=-1)
        key = jax.random.key(seed)
        ks = jax.random.split(key, 9)
        B, S, E = (4, 256, 128)
        s = 0.02
        return {'x': jax.random.normal(ks[0], (B, S, E), dtype=jnp.float32), 'wq': jax.random.normal(ks[1], (E, E), dtype=jnp.float32) * s, 'bq': jax.random.normal(ks[2], (E,), dtype=jnp.float32) * s, 'wk': jax.random.normal(ks[3], (E, E), dtype=jnp.float32) * s, 'bk': jax.random.normal(ks[4], (E,), dtype=jnp.float32) * s, 'wv': jax.random.normal(ks[5], (E, E), dtype=jnp.float32) * s, 'bv': jax.random.normal(ks[6], (E,), dtype=jnp.float32) * s, 'wo': jax.random.normal(ks[7], (E, E), dtype=jnp.float32) * s, 'bo': jax.random.normal(ks[8], (E,), dtype=jnp.float32) * s}
    _L0_attn_all = _L0_attn_setup()
    _L0_attn_in = {k: v for k, v in _L0_attn_all.items() if k in ('wq', 'bq', 'wk', 'bk', 'wv', 'bv', 'wo', 'bo')}
    del _L0_attn_all

    def _L0_xattn_setup():
        import jax, jax.numpy as jnp
        import numpy as np
        DIM = 128
        DIM_MEDIA = 128
        DIM_HEAD = 64
        HEADS = 8
        INNER = DIM_HEAD * HEADS
        B, N_TOK, N_LAT = (4, 512, 128)
        LN_EPS = 1e-05
        key = jax.random.key(seed)
        ks = jax.random.split(key, 6)
        x = jax.random.normal(ks[0], (B, N_TOK, DIM), dtype=jnp.float32)
        media = jax.random.normal(ks[1], (B, N_LAT, DIM_MEDIA), dtype=jnp.float32)
        media_mask = jax.random.randint(ks[2], (B, N_LAT), 0, 2).astype(bool)
        media_mask = media_mask.at[:, 0].set(True)
        ln_gamma = jnp.ones((DIM,), jnp.float32)
        ln_beta = jnp.zeros((DIM,), jnp.float32)
        Wq = jax.random.normal(ks[3], (DIM, INNER), jnp.float32) * DIM ** (-0.5)
        Wkv = jax.random.normal(ks[4], (DIM_MEDIA, 2 * INNER), jnp.float32) * DIM_MEDIA ** (-0.5)
        Wout = jax.random.normal(ks[5], (INNER, DIM), jnp.float32) * INNER ** (-0.5)
        return {'x': x, 'media': media, 'media_mask': media_mask, 'ln_gamma': ln_gamma, 'ln_beta': ln_beta, 'Wq': Wq, 'Wkv': Wkv, 'Wout': Wout}
    _L0_xattn_all = _L0_xattn_setup()
    _L0_xattn_in = {k: v for k, v in _L0_xattn_all.items() if k in ('ln_gamma', 'ln_beta', 'Wq', 'Wkv', 'Wout')}
    del _L0_xattn_all

    def _L0_ffn_setup():
        import jax, jax.numpy as jnp
        import numpy as np
        B, S, D, F, E = (4, 256, 128, 512, 8)
        key = jax.random.key(seed)
        ks = jax.random.split(key, 7)
        s1 = 1.0 / np.sqrt(D)
        s2 = 1.0 / np.sqrt(F)
        x = jax.random.normal(ks[0], (B, S, D), dtype=jnp.float32)
        W1 = jax.random.uniform(ks[1], (E, D, F), jnp.float32, -s1, s1)
        b1 = jax.random.uniform(ks[2], (E, F), jnp.float32, -s1, s1)
        W2 = jax.random.uniform(ks[3], (E, F, D), jnp.float32, -s2, s2)
        b2 = jax.random.uniform(ks[4], (E, D), jnp.float32, -s2, s2)
        Wr = jax.random.uniform(ks[5], (D, E), jnp.float32, -s1, s1)
        br = jax.random.uniform(ks[6], (E,), jnp.float32, -s1, s1)
        return {'x': x, 'W1': W1, 'b1': b1, 'W2': W2, 'b2': b2, 'Wr': Wr, 'br': br}
    _L0_ffn_all = _L0_ffn_setup()
    _L0_ffn_in = {k: v for k, v in _L0_ffn_all.items() if k in ('W1', 'b1', 'W2', 'b2', 'Wr', 'br')}
    del _L0_ffn_all

    def _L1_attn_setup():
        import jax, jax.numpy as jnp
        import numpy as np
        import math
        N_EMBD = 128
        N_HEAD = 16
        HEAD_DIM = N_EMBD // N_HEAD
        key = jax.random.key(seed)
        k1, k2, k3, k4, k5 = jax.random.split(key, 5)
        s = 1.0 / math.sqrt(N_EMBD)
        x = jax.random.normal(k1, (4, 256, N_EMBD), dtype=jnp.float32)
        W_qkv = jax.random.normal(k2, (N_EMBD, 3 * N_EMBD), dtype=jnp.float32) * s
        b_qkv = jnp.zeros((3 * N_EMBD,), dtype=jnp.float32)
        W_proj = jax.random.normal(k3, (N_EMBD, N_EMBD), dtype=jnp.float32) * s
        b_proj = jnp.zeros((N_EMBD,), dtype=jnp.float32)
        return {'x': x, 'W_qkv': W_qkv, 'b_qkv': b_qkv, 'W_proj': W_proj, 'b_proj': b_proj}
    _L1_attn_all = _L1_attn_setup()
    _L1_attn_in = {k: v for k, v in _L1_attn_all.items() if k in ('W_qkv', 'b_qkv', 'W_proj', 'b_proj')}
    del _L1_attn_all

    def _L1_xattn_setup():
        import jax, jax.numpy as jnp
        import numpy as np
        B, L_ENC, L_DEC, D = (16, 64, 128, 128)
        key = jax.random.key(seed)
        k1, k2, k3, k4, k5, k6 = jax.random.split(key, 6)
        encoder_hc = jax.random.normal(k1, (B, L_ENC, D), dtype=jnp.float32)
        decoder_hq = jax.random.normal(k2, (B, L_DEC, D), dtype=jnp.float32)
        w_sim = jax.random.normal(k3, (3 * D,), dtype=jnp.float32) * 0.02
        b_sim = jax.random.normal(k4, (1,), dtype=jnp.float32) * 0.02
        W_qv = jax.random.normal(k5, (4 * D, D), dtype=jnp.float32) * 0.02
        b_qv = jax.random.normal(k6, (D,), dtype=jnp.float32) * 0.02
        return {'encoder_hc': encoder_hc, 'decoder_hq': decoder_hq, 'w_sim': w_sim, 'b_sim': b_sim, 'W_qv': W_qv, 'b_qv': b_qv}
    _L1_xattn_all = _L1_xattn_setup()
    _L1_xattn_in = {k: v for k, v in _L1_xattn_all.items() if k in ('w_sim', 'b_sim', 'W_qv', 'b_qv')}
    del _L1_xattn_all

    def _L1_ffn_setup():
        import jax, jax.numpy as jnp
        import numpy as np
        QMAX = 127.0

        def _ste_round(v):
            return v + jax.lax.stop_gradient(jnp.round(v) - v)

        def _act_fake_quant(x, clip_factor):
            scale = jax.nn.sigmoid(clip_factor) * jnp.max(jnp.abs(x)) / QMAX
            return jnp.clip(_ste_round(x / scale), -QMAX - 1.0, QMAX) * scale

        def _weight_fake_quant(w):
            scale = jnp.max(jnp.abs(w), axis=1, keepdims=True) / QMAX
            return jnp.clip(_ste_round(w / scale), -QMAX - 1.0, QMAX) * scale
        key = jax.random.key(seed)
        k1, k2, k3, k4 = jax.random.split(key, 4)
        B, S, H, I = (8, 1024, 128, 352)
        return {'x': jax.random.normal(k1, (B, S, H), dtype=jnp.float32), 'clip_x': jnp.full((1,), 4.0, dtype=jnp.float32), 'clip_down': jnp.full((1,), 4.0, dtype=jnp.float32), 'w_gate': jax.random.normal(k2, (I, H), dtype=jnp.float32) * 0.02, 'w_up': jax.random.normal(k3, (I, H), dtype=jnp.float32) * 0.02, 'w_down': jax.random.normal(k4, (H, I), dtype=jnp.float32) * 0.02}
    _L1_ffn_all = _L1_ffn_setup()
    _L1_ffn_in = {k: v for k, v in _L1_ffn_all.items() if k in ('clip_x', 'clip_down', 'w_gate', 'w_up', 'w_down')}
    del _L1_ffn_all
    return {'x': x, 'ctx_1024': ctx_1024, 'mask_BxS2_bk0': mask_BxS2_bk0, 'L0_attn_wq': _L0_attn_in['wq'], 'L0_attn_bq': _L0_attn_in['bq'], 'L0_attn_wk': _L0_attn_in['wk'], 'L0_attn_bk': _L0_attn_in['bk'], 'L0_attn_wv': _L0_attn_in['wv'], 'L0_attn_bv': _L0_attn_in['bv'], 'L0_attn_wo': _L0_attn_in['wo'], 'L0_attn_bo': _L0_attn_in['bo'], 'L0_xattn_ln_gamma': _L0_xattn_in['ln_gamma'], 'L0_xattn_ln_beta': _L0_xattn_in['ln_beta'], 'L0_xattn_Wq': _L0_xattn_in['Wq'], 'L0_xattn_Wkv': _L0_xattn_in['Wkv'], 'L0_xattn_Wout': _L0_xattn_in['Wout'], 'L0_ffn_W1': _L0_ffn_in['W1'], 'L0_ffn_b1': _L0_ffn_in['b1'], 'L0_ffn_W2': _L0_ffn_in['W2'], 'L0_ffn_b2': _L0_ffn_in['b2'], 'L0_ffn_Wr': _L0_ffn_in['Wr'], 'L0_ffn_br': _L0_ffn_in['br'], 'L1_attn_W_qkv': _L1_attn_in['W_qkv'], 'L1_attn_b_qkv': _L1_attn_in['b_qkv'], 'L1_attn_W_proj': _L1_attn_in['W_proj'], 'L1_attn_b_proj': _L1_attn_in['b_proj'], 'L1_xattn_w_sim': _L1_xattn_in['w_sim'], 'L1_xattn_b_sim': _L1_xattn_in['b_sim'], 'L1_xattn_W_qv': _L1_xattn_in['W_qv'], 'L1_xattn_b_qv': _L1_xattn_in['b_qv'], 'L1_ffn_clip_x': _L1_ffn_in['clip_x'], 'L1_ffn_clip_down': _L1_ffn_in['clip_down'], 'L1_ffn_w_gate': _L1_ffn_in['w_gate'], 'L1_ffn_w_up': _L1_ffn_in['w_up'], 'L1_ffn_w_down': _L1_ffn_in['w_down']}

def reference(x, ctx_1024, mask_BxS2_bk0, L0_attn_wq, L0_attn_bq, L0_attn_wk, L0_attn_bk, L0_attn_wv, L0_attn_bv, L0_attn_wo, L0_attn_bo, L0_xattn_ln_gamma, L0_xattn_ln_beta, L0_xattn_Wq, L0_xattn_Wkv, L0_xattn_Wout, L0_ffn_W1, L0_ffn_b1, L0_ffn_W2, L0_ffn_b2, L0_ffn_Wr, L0_ffn_br, L1_attn_W_qkv, L1_attn_b_qkv, L1_attn_W_proj, L1_attn_b_proj, L1_xattn_w_sim, L1_xattn_b_sim, L1_xattn_W_qv, L1_xattn_b_qv, L1_ffn_clip_x, L1_ffn_clip_down, L1_ffn_w_gate, L1_ffn_w_up, L1_ffn_w_down):
    import jax
    import jax.numpy as jnp

    def _L0_attn_ref(x, wq, bq, wk, bk, wv, bv, wo, bo):
        import jax, jax.numpy as jnp
        import numpy as np
        H = 16
        ROPE_BASE = 10000.0

        def _rotate_half(x):
            d = x.shape[-1]
            return jnp.concatenate((-x[..., d // 2:], x[..., :d // 2]), axis=-1)
        B, S, E = x.shape
        D = E // H

        def proj(w, b):
            return (x @ w.T + b).reshape(B, S, H, D).transpose(0, 2, 1, 3)
        q = proj(wq, bq)
        k = proj(wk, bk)
        v = proj(wv, bv)
        inv_freq = 1.0 / ROPE_BASE ** (jnp.arange(0, D, 2, dtype=jnp.float32) / D)
        freqs = jnp.arange(S, dtype=jnp.float32)[:, None] * inv_freq[None, :]
        cos = jnp.repeat(jnp.cos(freqs), 2, axis=-1)[None, None]
        sin = jnp.repeat(jnp.sin(freqs), 2, axis=-1)[None, None]
        q = q * cos + _rotate_half(q) * sin
        k = k * cos + _rotate_half(k) * sin
        scale = D ** (-0.5)
        scores = jnp.einsum('bhqd,bhkd->bhqk', q, k) * scale
        attn = jax.nn.softmax(scores, axis=-1)
        out = jnp.einsum('bhqk,bhkd->bhqd', attn, v)
        out = out.transpose(0, 2, 1, 3).reshape(B, S, E)
        return out @ wo.T + bo

    def _L0_xattn_ref(x, media, media_mask, ln_gamma, ln_beta, Wq, Wkv, Wout):
        import jax, jax.numpy as jnp
        import numpy as np
        DIM = 128
        DIM_MEDIA = 128
        DIM_HEAD = 64
        HEADS = 8
        INNER = DIM_HEAD * HEADS
        B, N_TOK, N_LAT = (4, 512, 128)
        LN_EPS = 1e-05
        scale = DIM_HEAD ** (-0.5)
        mu = jnp.mean(x, axis=-1, keepdims=True)
        var = jnp.mean(jnp.square(x - mu), axis=-1, keepdims=True)
        xn = (x - mu) * jax.lax.rsqrt(var + LN_EPS) * ln_gamma + ln_beta
        q = xn @ Wq * scale
        kv = media @ Wkv
        k, v = jnp.split(kv, 2, axis=-1)

        def to_heads(t):
            b, n, _ = t.shape
            return t.reshape(b, n, HEADS, DIM_HEAD).transpose(0, 2, 1, 3)
        q, k, v = (to_heads(q), to_heads(k), to_heads(v))
        sim = jnp.einsum('bhid,bhjd->bhij', q, k)
        neg_inf = jnp.float32(-jnp.inf)
        sim = jnp.where(media_mask[:, None, None, :], sim, neg_inf)
        sim = sim - jax.lax.stop_gradient(jnp.max(sim, axis=-1, keepdims=True))
        attn = jax.nn.softmax(sim, axis=-1)
        out = jnp.einsum('bhij,bhjd->bhid', attn, v)
        out = out.transpose(0, 2, 1, 3).reshape(out.shape[0], out.shape[2], INNER)
        return out @ Wout

    def _L0_ffn_ref(x, W1, b1, W2, b2, Wr, br):
        import jax, jax.numpy as jnp
        import numpy as np
        B, S, D, F, E = (4, 256, 128, 512, 8)
        b, s, d = x.shape
        e = Wr.shape[1]
        logits = x @ Wr + br
        idx = jnp.argmax(logits, axis=-1)
        probs = jax.nn.softmax(logits, axis=-1)
        gates = jnp.take_along_axis(probs, idx[..., None], axis=-1)[..., 0]
        xf = x.reshape(-1, d)
        idxf = idx.reshape(-1)
        gf = gates.reshape(-1)
        out = jnp.zeros_like(xf)
        for ei in range(e):
            h = jax.nn.gelu(xf @ W1[ei] + b1[ei], approximate=False)
            y = h @ W2[ei] + b2[ei]
            mask = (idxf == ei).astype(xf.dtype)
            out = out + y * (gf * mask)[:, None]
        return out.reshape(b, s, d)

    def _L1_attn_ref(x, W_qkv, b_qkv, W_proj, b_proj):
        import jax, jax.numpy as jnp
        import numpy as np
        import math
        N_EMBD = 128
        N_HEAD = 16
        HEAD_DIM = N_EMBD // N_HEAD
        B, T, C = x.shape
        H, D = (N_HEAD, HEAD_DIM)
        qkv = x @ W_qkv + b_qkv
        qkv = qkv.reshape(B, T, 3, H, D)
        q = jnp.transpose(qkv[:, :, 0], (0, 2, 1, 3))
        k = jnp.transpose(qkv[:, :, 1], (0, 2, 1, 3))
        v = jnp.transpose(qkv[:, :, 2], (0, 2, 1, 3))
        scale = 1.0 / math.sqrt(D)
        att = jnp.einsum('bhtd,bhsd->bhts', q, k) * scale
        causal = jnp.tril(jnp.ones((T, T), dtype=bool))
        att = jnp.where(causal[None, None], att, -jnp.inf)
        att = jax.nn.softmax(att, axis=-1)
        out = jnp.einsum('bhts,bhsd->bhtd', att, v)
        out = jnp.transpose(out, (0, 2, 1, 3)).reshape(B, T, C)
        return out @ W_proj + b_proj

    def _L1_xattn_ref(encoder_hc, decoder_hq, w_sim, b_sim, W_qv, b_qv):
        import jax, jax.numpy as jnp
        import numpy as np
        B, L_ENC, L_DEC, D = (16, 64, 128, 128)
        d = encoder_hc.shape[-1]
        w1, w2, w3 = (w_sim[:d], w_sim[d:2 * d], w_sim[2 * d:])
        Sim = (encoder_hc @ w1)[:, :, None] + (decoder_hq @ w2)[:, None, :] + jnp.einsum('bid,bjd->bij', encoder_hc * w3, decoder_hq) + b_sim[0]
        A = jax.nn.softmax(Sim, axis=2)
        hq_hat = jnp.einsum('bij,bjd->bid', A, decoder_hq)
        Batt = jax.nn.softmax(jnp.max(Sim, axis=2), axis=1)
        hc_bar = jnp.einsum('bi,bid->bd', Batt, encoder_hc)[:, None, :]
        hc_hat = jnp.broadcast_to(hc_bar, encoder_hc.shape)
        feats = jnp.concatenate([encoder_hc, hq_hat, encoder_hc * hq_hat, encoder_hc * hc_hat], axis=-1)
        hcq = feats @ W_qv + b_qv
        return hcq

    def _L1_ffn_ref(x, clip_x, clip_down, w_gate, w_up, w_down):
        import jax, jax.numpy as jnp
        import numpy as np
        QMAX = 127.0

        def _ste_round(v):
            return v + jax.lax.stop_gradient(jnp.round(v) - v)

        def _act_fake_quant(x, clip_factor):
            scale = jax.nn.sigmoid(clip_factor) * jnp.max(jnp.abs(x)) / QMAX
            return jnp.clip(_ste_round(x / scale), -QMAX - 1.0, QMAX) * scale

        def _weight_fake_quant(w):
            scale = jnp.max(jnp.abs(w), axis=1, keepdims=True) / QMAX
            return jnp.clip(_ste_round(w / scale), -QMAX - 1.0, QMAX) * scale
        xq = _act_fake_quant(x, clip_x[0])
        gate = jnp.einsum('bsh,ih->bsi', xq, _weight_fake_quant(w_gate))
        up = jnp.einsum('bsh,ih->bsi', xq, _weight_fake_quant(w_up))
        h = _act_fake_quant(jax.nn.silu(gate) * up, clip_down[0])
        return jnp.einsum('bsi,hi->bsh', h, _weight_fake_quant(w_down))
    x = x + _L0_attn_ref(_layernorm(x, axis=-1), L0_attn_wq, L0_attn_bq, L0_attn_wk, L0_attn_bk, L0_attn_wv, L0_attn_bv, L0_attn_wo, L0_attn_bo)
    x = x + _L0_xattn_ref(_layernorm(x, axis=-1), ctx_1024, mask_BxS2_bk0, L0_xattn_ln_gamma, L0_xattn_ln_beta, L0_xattn_Wq, L0_xattn_Wkv, L0_xattn_Wout)
    x = x + _L0_ffn_ref(_layernorm(x, axis=-1), L0_ffn_W1, L0_ffn_b1, L0_ffn_W2, L0_ffn_b2, L0_ffn_Wr, L0_ffn_br)
    x = x + _L1_attn_ref(_layernorm(x, axis=-1), L1_attn_W_qkv, L1_attn_b_qkv, L1_attn_W_proj, L1_attn_b_proj)
    x = x + _L1_xattn_ref(_layernorm(x, axis=-1), ctx_1024, L1_xattn_w_sim, L1_xattn_b_sim, L1_xattn_W_qv, L1_xattn_b_qv)
    x = x + _L1_ffn_ref(_layernorm(x, axis=-1), L1_ffn_clip_x, L1_ffn_clip_down, L1_ffn_w_gate, L1_ffn_w_up, L1_ffn_w_down)
    return x

_drawn_inputs = setup_inputs


def setup_inputs(seed=0):
    import zlib

    import numpy as np

    out = dict(_drawn_inputs(seed))
    spreads = {'L0_xattn_ln_gamma': (1.0, 0.2),
     'L0_xattn_ln_beta': (0.0, 0.32),
     'L1_attn_b_qkv': (0.0, 0.1),
     'L1_attn_b_proj': (0.0, 0.1)}
    factors = {'L0_attn_wq': 8.0,
     'L0_attn_bq': 8.0,
     'L0_attn_wk': 8.0,
     'L0_attn_bk': 8.0,
     'L0_attn_wv': 8.0,
     'L0_attn_bv': 8.0,
     'L0_attn_wo': 7.393,
     'L0_ffn_b1': 8.0,
     'L0_ffn_b2': 8.0,
     'L0_ffn_br': 4.543,
     'L1_xattn_w_sim': 3.556,
     'L1_xattn_b_qv': 3.167,
     'L1_ffn_w_gate': 7.265,
     'L1_ffn_w_up': 7.209,
     'L1_ffn_w_down': 7.109}
    for name, (base, spread) in spreads.items():
        noise = np.random.default_rng([zlib.crc32(name.encode()), seed]).standard_normal(out[name].shape)
        drawn = base * np.exp(spread * noise) if base else spread * noise
        out[name] = jnp.asarray(drawn.astype(out[name].dtype))
    for name, factor in factors.items():
        out[name] = (out[name] * factor).astype(out[name].dtype)
    return out
```

```python
from contextlib import ExitStack

import numpy as np

import concourse.bass as bass
from concourse import mybir

ALU = mybir.AluOpType
ACT = mybir.ActivationFunctionType
AX = mybir.AxisListType
F32 = mybir.dt.float32
BF16 = mybir.dt.bfloat16
I32 = mybir.dt.int32
U8 = mybir.dt.uint8

NB, S, D = 32, 100, 128
CTX = 1444
EPS = 1e-5
BIG = 3.0e38
ROUND = 1.5 * 2.0 ** 23


class Tick:

    def __init__(self, it, off, per):
        self.it, self.off, self.per = it, off, per

    def back(self, lag):
        return Tick(self.it, self.off - lag, self.per)

    def index(self, of=1):
        return self.it * (self.per // of) + self.off // of

    def exists(self, count):
        if not isinstance(self.it, int):
            return True
        return 0 <= self.it * self.per + self.off < count

    def phase(self, n):
        return self.off % n


def at_least(eng, sem, value):
    if isinstance(value, int) and value <= 0:
        return
    eng.wait_ge(sem, value)


def run_steps(eng, step, lead, items, drain, per, peel):
    for off in range(-lead, peel * per):
        step(Tick(0, off, per))
    last = items // per - 1
    with eng.Fori(peel, last) as it:
        for off in range(per):
            step(Tick(it, off, per))
    for off in range(per + drain):
        step(Tick(last, off, per))


class Space:

    def __init__(self, nc, ctx, tag):
        self.nc, self.ctx, self.tag = nc, ctx, tag
        self.sems = []
        ctx.callback(self.clear)

    def clear(self):
        if self.sems:
            self.nc.clear_and_free_semaphores(self.sems)
            self.nc.all_engine_barrier()

    def sb(self, name, shape, dt=F32):
        return self.ctx.enter_context(self.nc.sbuf_tensor(f"{self.tag}_{name}", shape, dt))

    def ps(self, name, shape=(128, 512), dt=F32):
        return self.ctx.enter_context(self.nc.psum_tensor(f"{self.tag}_{name}", list(shape), dt))

    def sem(self, name):
        self.sems.append(self.nc.alloc_semaphore(f"{self.tag}_{name}"))
        return self.sems[-1]


class Chain:

    def __init__(self, eng, sem):
        self.eng, self.sem, self.count = eng, sem, 0

    def __call__(self, ins):
        self.count += 1
        ins.then_inc(self.sem, 1)
        self.eng.wait_ge(self.sem, self.count)


def layernorm_moments(dve, link, st, tmp, var):
    link(dve.tensor_tensor(st.mean[:, :], st.stats[:, :, 1], st.stats[:, :, 4], ALU.add))
    link(dve.tensor_scalar(st.mean[:, :], st.mean[:, :], 0.5, None, ALU.mult))
    link(dve.tensor_tensor(tmp[:, :], st.stats[:, :, 1], st.mean[:, :], ALU.subtract))
    link(dve.tensor_tensor(tmp[:, :], tmp[:, :], tmp[:, :], ALU.mult))
    link(dve.tensor_tensor(var[:, :], st.stats[:, :, 2], st.stats[:, :, 5], ALU.add))
    link(dve.scalar_tensor_tensor(var[:, :], var[:, :], 1.0 / D, tmp[:, :], ALU.mult, ALU.add))


def attention(nc, st, tag, rotary, wts):
    H, HD, HG = 16, 8, 4
    GROUPS = H // HG
    ITEMS = NB * GROUPS
    SCALE = float(HD) ** -0.5
    PER = 2 * GROUPS
    with ExitStack() as ctx:
        sp = Space(nc, ctx, tag)
        sb, ps, sem = sp.sb, sp.ps, sp.sem
        tmp, var, std = sb("tmp", [S, NB]), sb("var", [S, NB]), sb("std", [S, NB])
        nproj = 4 if rotary else 2
        wproj = sb("wproj", [D, nproj, D])
        wv, wo = sb("wv", [D, D]), sb("wo", [D, D])
        wraw = sb("wraw", [D, 4, D])
        bcol = sb("bcol", [D, 8])
        brow = sb("brow", [S, D])
        bias_qk = sb("bias_qk", [D, 2, S])
        rowbias = sb("rowbias", [S, D])
        xn = sb("xn", [S, D])
        xnT = [sb(f"xnT{i}", [D, S]) for i in range(2)]
        turned = sb("turned", [D, 4, S])
        qk = [sb(f"qk{i}", [D, 2, S]) for i in range(2)]
        kblk = [sb(f"kblk{i}", [D, H, S]) for i in range(2)]
        ROW, HALF = S, H // 2
        vone = [sb(f"vone{i}", [D, H, ROW]) for i in range(2)]
        probs = [sb(f"probs{i}", [S, HG, S]) for i in range(4)]
        probsT = [sb(f"probsT{i}", [D, HG, S]) for i in range(2)]
        top = sb("top", [S, 4, HG])
        rsum = sb("rsum", [S, H])
        heads = [sb(f"heads{i}", [S, H, HD]) for i in range(2)]
        headsT = sb("headsT", [D, S])
        scores = [ps(f"scores{i}") for i in range(2)]
        pT = [ps(f"pT{i}") for i in range(2)]
        outp = [ps(f"outp{i}") for i in range(2)]
        front, back = ps("front"), ps("back")

        (weights_in, moments, std_ready, rstd_ready, chain, achain, setup_pe, setup_read, setup_done, ones_set,
         ln_done, xT_ready, xnT_ready, proj_ready, proj_read, v_ready, v_read, turned_read, sum_made, biased, kq_ready,
         s_ready, max_done, shifted, exp_done, pT_ready, pT_read, pv_done,
         rsum_done, heads_done, hT_ready, hT_read, y_ready, added, bias_added) = [sem(n) for n in (
            "weights_in", "moments", "std_ready", "rstd_ready", "chain", "achain", "setup_pe", "setup_read", "setup_done",
            "ones_set", "ln_done", "xT_ready", "xnT_ready", "proj_ready", "proj_read", "v_ready", "v_read",
            "turned_read", "sum_made", "biased", "kq_ready",
            "s_ready", "max_done", "shifted", "exp_done", "pT_ready", "pT_read", "pv_done",
            "rsum_done", "heads_done", "hT_ready", "hT_read", "y_ready", "added", "bias_added")]

        def v_places(v, half, lo, hi):
            flat = v[:, :, :].rearrange("p h e -> p (h e)")[:, half * HALF * ROW:(half + 1) * HALF * ROW]
            step = ROW + HD + 1
            return bass.AP(flat.tensor, flat.offset + lo, [list(flat.ap[0]), [step, HALF], [1, hi - lo]])

        def sv(t):
            return scores[t.phase(2)][0:S, 0:HG * S].rearrange("p (h k) -> p h k", h=HG)

        n_weights = 8 if rotary else 7
        block = ctx.enter_context(nc.Block())

        def load_places(eng, part):
            first, past = ((0, 8), (8, 16), (16, NB))[part]
            with eng.Fori(first // 4, past // 4) as it:
                for b in range(4):
                    p = it * 4 + b
                    n = eng.value_load(st.order[0:1, bass.ds(p, 1)], min_val=0, max_val=NB - 1)
                    eng.dma_start(st.xs[:, bass.ds(p, 1), :], st.x[bass.ds(n, 1)].rearrange("b s d -> s b d"))\
                        .then_inc(st.x_in[part], 16)

        @block.sync
        def _(sync):
            if rotary:
                for i, name in enumerate(("wq", "wk", "wv", "wo")):
                    sync.dma_start(wraw[:, i, :], wts[name]).then_inc(weights_in, 16)
                for i, name in enumerate(("bq", "bk", "bv")):
                    sync.dma_start(bcol[:, i:i + 1], wts[name].rearrange("(p a) -> p a", a=1)).then_inc(weights_in, 16)
                sync.dma_start(brow[:, :], wts["bo"].rearrange("(a n) -> a n", a=1).broadcast_to([S, D]))\
                    .then_inc(weights_in, 16)
            else:
                sync.dma_start(wproj[:, :, :], wts["W_qkv"][:, 0:2 * D].rearrange("p (w n) -> p w n", w=2))\
                    .then_inc(weights_in, 16)
                sync.dma_start(wv[:, :], wts["W_qkv"][:, 2 * D:3 * D]).then_inc(weights_in, 16)
                sync.dma_start(wo[:, :], wts["W_proj"]).then_inc(weights_in, 16)
                for i in range(3):
                    sync.dma_start(bcol[:, i:i + 1], wts["b_qkv"][i * D:(i + 1) * D].rearrange("(p a) -> p a", a=1))\
                        .then_inc(weights_in, 16)
                sync.dma_start(brow[:, :], wts["b_proj"].rearrange("(a n) -> a n", a=1).broadcast_to([S, D]))\
                    .then_inc(weights_in, 16)
            if tag == "a0":
                load_places(sync, 0)

        @block.tensor
        def _(pe):
            pe.wait_ge(weights_in, 16 * n_weights)
            pe.wait_ge(st.consts_in, 16 * st.n_consts)
            if rotary:
                for i in range(4):
                    pe.transpose(scores[0][:, i * D:(i + 1) * D], wraw[:, i, :], st.ident[:, :])
                for i in range(2):
                    pe.matmul(scores[1][:, i * D:(i + 1) * D], wraw[:, i, :], st.rotT[:, :], start=True, stop=True)
                pe.matmul(pT[0][:, 0:2], st.rotT[:, :], bcol[:, 0:2], start=True, stop=True).then_inc(setup_pe, 1)
                pe.wait_ge(setup_read, 1)
            pe.matmul(pT[1][0:S, 0:D], bcol[:, 2:3].broadcast_to([D, S]), wo[:, :], start=True, stop=True)\
                .then_inc(setup_pe, 1)

            def step(t):
                c = t.back(-GROUPS)
                if t.phase(GROUPS) == 0 and c.exists(ITEMS):
                    n = c.index(GROUPS)
                    at_least(pe, ln_done, n + 1)
                    at_least(pe, v_read, n)
                    pe.transpose(front[:, 0:S], xn[:, :], st.ident[0:S, 0:S]).then_inc(xT_ready, 1)
                if t.phase(GROUPS) == 1 and c.exists(ITEMS):
                    n = c.index(GROUPS)
                    at_least(pe, xnT_ready, n + 1)
                    for j in range(nproj):
                        ins = pe.matmul(front[:, j * S:(j + 1) * S], wproj[:, j, :], xnT[c.phase(PER) // GROUPS][:, :],
                                        start=True, stop=True)
                    ins.then_inc(proj_ready, 1)
                if t.exists(ITEMS):
                    k, n, g = t.index(), t.index(GROUPS), t.phase(GROUPS)
                    slot = t.phase(PER) // GROUPS
                    at_least(pe, kq_ready, n + 1)
                    at_least(pe, shifted, k - 1)
                    if not rotary:
                        pe.matmul(scores[t.phase(2)][0:S, 0:HG * S], st.ident_b[0:S, 0:S],
                                  st.causal[:, :, :], start=True, stop=False)
                    pe.matmul(scores[t.phase(2)][0:S, 0:HG * S], qk[slot][:, 0, :],
                              kblk[slot][:, HG * g:HG * g + HG, :], start=rotary, stop=True).then_inc(s_ready, 1)
                u = t.back(2)
                if u.exists(ITEMS):
                    k = u.index()
                    at_least(pe, exp_done, k + 1)
                    at_least(pe, pT_read, k - 1)
                    for h in range(HG):
                        ins = pe.transpose(pT[u.phase(2)][0:S, h * S:(h + 1) * S], probs[u.phase(4)][:, h, :],
                                           st.ident[0:S, 0:S])
                    ins.then_inc(pT_ready, 1)
                u = t.back(3)
                if u.exists(ITEMS):
                    k, n, g = u.index(), u.index(GROUPS), u.phase(GROUPS)
                    slot = u.phase(PER) // GROUPS
                    at_least(pe, pT_read, k + 1)
                    at_least(pe, v_read, n + 1)
                    if g == 0:
                        at_least(pe, heads_done, n - 1)
                    half = g // 2
                    for h in range(HG):
                        hh = HG * g + h
                        ins = pe.matmul(outp[slot][0:S, half * ROW:(half + 1) * ROW], probsT[u.phase(2)][:, h, :],
                                        vone[slot][:, hh, :], start=(hh % HALF == 0), stop=(hh % HALF == HALF - 1))
                    ins.then_inc(pv_done, 1)
                if t.phase(GROUPS) == 2 and c.exists(ITEMS):
                    n = c.index(GROUPS)
                    at_least(pe, proj_read, n + 1)
                    pe.matmul(front[0:S, 0:D], xnT[c.phase(PER) // GROUPS][:, :], wv[:, :], start=True, stop=True)\
                        .then_inc(v_ready, 1)
                u = t.back(8)
                if u.phase(GROUPS) == 0 and u.exists(ITEMS):
                    n = u.index(GROUPS)
                    at_least(pe, heads_done, n + 1)
                    at_least(pe, added, n)
                    pe.transpose(back[:, 0:S], heads[u.phase(PER) // GROUPS][:, :, :].rearrange("p h d -> p (h d)"),
                                 st.ident[0:S, 0:S]).then_inc(hT_ready, 1)
                u = t.back(10)
                if u.phase(GROUPS) == 0 and u.exists(ITEMS):
                    n = u.index(GROUPS)
                    at_least(pe, hT_read, n + 1)
                    pe.matmul(back[0:S, 128:128 + D], headsT[:, :], wo[:, :], start=True, stop=True)\
                        .then_inc(y_ready, 1)

            run_steps(pe, step, GROUPS, ITEMS, 12, PER, 2)

        @block.scalar
        def _(act):
            if tag == "a0":
                load_places(act, 1)
            act.wait_ge(moments, 1)
            act.wait_ge(ones_set, 1)
            act.activation(std[:, :], var[:, :], ACT.Sqrt).then_inc(std_ready, 1)

            def step(t):
                c = t.back(-GROUPS)
                if t.phase(GROUPS) == 0 and c.exists(ITEMS):
                    n = c.index(GROUPS)
                    at_least(act, xT_ready, n + 1)
                    at_least(act, v_ready, n - 1)
                    act.activation(xnT[c.phase(PER) // GROUPS][:, :], front[:, 0:S], ACT.Copy).then_inc(xnT_ready, 1)
                if not rotary and t.phase(GROUPS) == 1 and c.exists(ITEMS):
                    n, slot = c.index(GROUPS), c.phase(PER) // GROUPS
                    at_least(act, proj_ready, n + 1)
                    at_least(act, s_ready, (n - 1) * GROUPS)
                    for j in range(2):
                        ins = act.activation(qk[slot][:, j, :], front[:, j * S:(j + 1) * S], ACT.Identity,
                                             bias=bcol[:, j:j + 1])
                    ins.then_inc(proj_read, 1)
                if t.phase(GROUPS) == 3 and c.exists(ITEMS):
                    n, slot = c.index(GROUPS), c.phase(PER) // GROUPS
                    at_least(act, v_ready, n + 1)
                    at_least(act, pv_done, (n - 1) * GROUPS)
                    for half in range(2):
                        ins = act.activation(v_places(vone[slot], half, 0, HD)[0:S], front[0:S, half * 64:half * 64 + 64]
                                             .rearrange("p (h d) -> p h d", h=HALF), ACT.Copy)
                    ins.then_inc(v_read, 1)
                u = t.back(2)
                if u.exists(ITEMS):
                    k = u.index()
                    at_least(act, pT_ready, k + 1)
                    at_least(act, pv_done, k - 1)
                    act.activation(probsT[u.phase(2)][0:S, :, :], pT[u.phase(2)][0:S, 0:HG * S]
                                   .rearrange("p (h k) -> p h k", h=HG), ACT.Copy).then_inc(pT_read, 1)
                if t.exists(ITEMS):
                    k = t.index()
                    at_least(act, shifted, k + 1)
                    p = probs[t.phase(4)][0:S, :, :]
                    act.activation(p, p, ACT.Exp, scale=SCALE).then_inc(exp_done, 1)
                u = t.back(9)
                if u.phase(GROUPS) == 0 and u.exists(ITEMS):
                    n = u.index(GROUPS)
                    at_least(act, hT_ready, n + 1)
                    at_least(act, y_ready, n)
                    act.activation(headsT[:, :], back[:, 0:S], ACT.Copy).then_inc(hT_read, 1)

            run_steps(act, step, GROUPS, ITEMS, 12, PER, 2)

        @block.vector
        def _(dve):
            link = Chain(dve, chain)
            for p in probsT:
                dve.memset(p[96:D, :, :], 0.0)
            for v in vone:
                link(dve.memset(v[:, :, :], 0.0))
                for half in range(2):
                    ins = dve.memset(v_places(v, half, HD, HD + 1)[0:S], 1.0)
            ins.then_inc(ones_set, 1)
            if tag == "a0":
                for part, first, past in ((2, 16, NB), (0, 0, 8), (1, 8, 16)):
                    dve.wait_ge(st.x_in[part], 16 * (past - first))
                    for n in range(first, past):
                        ins = dve.bn_stats(st.stats[:, n, :], st.xs[:, n, :])
                link(ins)
            layernorm_moments(dve, link, st, tmp, var)
            dve.tensor_scalar(var[:, :], var[:, :], EPS, None, ALU.add).then_inc(moments, 1)
            dve.wait_ge(std_ready, 1)
            dve.reciprocal(st.rstd[:, :], std[:, :]).then_inc(rstd_ready, 1)
            dve.wait_ge(rstd_ready, 1)
            if rotary:
                dve.wait_ge(setup_pe, 1)
                dve.tensor_copy(bcol[:, 3:5], pT[0][:, 0:2])
                for i in range(2):
                    dve.tensor_copy(wproj[:, 2 * i, :], scores[0][:, i * D:(i + 1) * D])
                    dve.tensor_copy(wproj[:, 2 * i + 1, :], scores[1][:, i * D:(i + 1) * D])
                dve.tensor_copy(wv[:, :], scores[0][:, 2 * D:3 * D])
                link(dve.tensor_copy(wo[:, :], scores[0][:, 3 * D:4 * D]))
                for i in range(2):
                    link(dve.tensor_scalar(bias_qk[:, i, :], st.turn[:, 0, :], bcol[:, i:i + 1], None, ALU.mult))
                    link(dve.scalar_tensor_tensor(bias_qk[:, i, :], st.turn[:, 1, :], bcol[:, 3 + i:4 + i],
                                                  bias_qk[:, i, :], ALU.mult, ALU.add))
                dve.tensor_copy(std[:, 0:1], std[:, 0:1]).then_inc(setup_read, 1)
            dve.wait_ge(setup_pe, 2 if rotary else 1)
            dve.wait_ge(weights_in, 16 * n_weights)
            dve.tensor_tensor(rowbias[:, :], pT[1][0:S, 0:D], brow[:, :], ALU.add).then_inc(setup_done, 1)

            def step(t):
                c = t.back(-2 * GROUPS)
                if t.phase(GROUPS) == 3 and c.exists(ITEMS):
                    n = c.index(GROUPS)
                    at_least(dve, xT_ready, n)
                    dve.tensor_scalar(xn[:, :], st.xs[:, n, :], st.mean[:, bass.ds(n, 1)], st.rstd[:, bass.ds(n, 1)],
                                      ALU.subtract, ALU.mult).then_inc(ln_done, 1)
                c = t.back(-GROUPS)
                if rotary and t.phase(GROUPS) == 1 and c.exists(ITEMS):
                    n = c.index(GROUPS)
                    at_least(dve, proj_ready, n + 1)
                    at_least(dve, sum_made, n)
                    for h in range(2):
                        ins = dve.tensor_tensor(turned[:, 2 * h:2 * h + 2, :],
                                                front[:, 2 * h * S:(2 * h + 2) * S].rearrange("p (w k) -> p w k", w=2),
                                                st.turn[:, :, :], ALU.mult)
                    ins.then_inc(proj_read, 1)
                if t.exists(ITEMS):
                    k = t.index()
                    at_least(dve, s_ready, k + 1)
                    m = top[:, t.phase(4), :]
                    dve.tensor_reduce(m, sv(t), AX.X, ALU.max).then_inc(max_done, 1)
                    at_least(dve, pT_ready, k - 3)
                    dve.wait_ge(max_done, k + 1)
                    dve.tensor_tensor(probs[t.phase(4)][0:S, :, :], sv(t), m.rearrange("p (h a) -> p h a", a=1)
                                      .broadcast_to([S, HG, S]), ALU.subtract).then_inc(shifted, 1)
                u = t.back(7)
                if u.phase(GROUPS) == 0 and u.exists(ITEMS):
                    n, slot = u.index(GROUPS), u.phase(PER) // GROUPS
                    o = outp[slot][0:S, 0:2 * ROW].rearrange("p (w r) -> p w r", w=2)[:, :, 0:HALF * (HD + 1)]\
                        .rearrange("p w (h e) -> p w h e", h=HALF)
                    at_least(dve, pv_done, GROUPS * (n + 1))
                    dve.reciprocal(rsum[:, :].rearrange("p (w h a) -> p w h a", w=2, a=1), o[:, :, :, HD:HD + 1])\
                        .then_inc(rsum_done, 1)
                    at_least(dve, hT_ready, n - 1)
                    dve.wait_ge(rsum_done, n + 1)
                    dve.tensor_tensor(heads[slot][:, :, :].rearrange("p (w h) d -> p w h d", w=2), o[:, :, :, 0:HD],
                                      rsum[:, :].rearrange("p (w h a) -> p w h a", w=2, a=1)
                                      .broadcast_to([S, 2, HALF, HD]), ALU.mult).then_inc(heads_done, 1)
                u = t.back(11)
                if u.phase(GROUPS) == 0 and u.exists(ITEMS):
                    n = u.index(GROUPS)
                    at_least(dve, y_ready, n + 1)
                    at_least(dve, bias_added, n + 1)
                    x = st.xs[:, n, :]
                    dve.tensor_tensor(x, back[0:S, 128:128 + D], x, ALU.add).then_inc(added, 1)
                    dve.wait_ge(added, n + 1)
                    dve.bn_stats(st.stats[:, n, :], x)

            run_steps(dve, step, 2 * GROUPS, ITEMS, 12, PER, 2)

        @block.gpsimd
        def _(pool):
            if tag == "a0":
                load_places(pool, 2)
            pool.wait_ge(setup_done, 1)

            def step(t):
                c = t.back(-GROUPS)
                if t.phase(GROUPS) == 1 and c.exists(ITEMS):
                    n, slot = c.index(GROUPS), c.phase(PER) // GROUPS
                    q = qk[slot]
                    at_least(pool, proj_read, n + 1)
                    at_least(pool, s_ready, (n - 1) * GROUPS)
                    if rotary:
                        tv = turned[:, :, :].rearrange("p (w c) k -> p w c k", c=2)
                        pool.tensor_tensor(q[:, :, :], tv[:, :, 0, :], tv[:, :, 1, :], ALU.add).then_inc(sum_made, 1)
                        pool.wait_ge(sum_made, n + 1)
                        pool.tensor_tensor(q[:, :, :], q[:, :, :], bias_qk[:, :, :], ALU.add).then_inc(biased, 1)
                        pool.wait_ge(biased, n + 1)
                    pool.tensor_tensor(kblk[slot][:, :, :], q[:, 1:2, :].broadcast_to([D, H, S]),
                                       st.headmask[:, :].rearrange("p (h a) -> p h a", a=1).broadcast_to([D, H, S]),
                                       ALU.mult).then_inc(kq_ready, 1)
                    at_least(pool, ln_done, n + 1)
                    x = st.xs[:, n, :]
                    pool.tensor_tensor(x, x, rowbias[:, :], ALU.add).then_inc(bias_added, 1)

            run_steps(pool, step, GROUPS, ITEMS, 0, PER, 2)


class KeyPlan:

    def __init__(self, first, part, chunks, tail, score_bufs, out_banks, start, count):
        self.start, self.count = start, count
        self.items = count * 8
        self.loads = 3 if tail else 2
        self.first, self.part, self.chunks, self.tail = first, part, chunks, tail
        self.score_bufs, self.out_banks = score_bufs, out_banks
        self.main = part * chunks
        self.keys = self.main + tail
        self.cuts = [(i * part, part) for i in range(chunks)] + ([(self.main, tail)] if tail else [])
        self.groups = [self.cuts[i:i + 4] for i in range(0, len(self.cuts), 4)]
        self.front_uses = 3 + len(self.groups)

    def front_use(self, t):
        ph, stride = t.phase(8), 2 if self.front_uses <= 4 else 1
        return ph // stride if ph % stride == 0 and ph // stride < self.front_uses else None


LATE_PLAN = KeyPlan(CTX - 420, 105, 4, 0, 2, 2, 0, NB // 2)
LAST_PLAN = KeyPlan(CTX - 105, 105, 1, 0, 2, 2, NB // 2, NB // 2)
WHOLE_PLAN = KeyPlan(0, 128, 11, 36, 1, 1, 0, NB)


def cross_attention(nc, st, ins):
    H, HD = 8, 64
    with ExitStack() as ctx:
        sp = Space(nc, ctx, "xa")
        sb, ps, sem = sp.sb, sp.ps, sp.sem
        tmp, var, std = sb("tmp", [S, NB]), sb("var", [S, NB]), sb("std", [S, NB])
        nanf = sb("nanf", [S, NB])
        wfold, ofold = sb("wfold", [D, H, D]), sb("ofold", [D, H, D])
        gamma, beta = sb("gamma", [D, 1]), sb("beta", [D, 1])
        flag = sb("flag", [1, 1], I32)
        with ExitStack() as setup_ctx:
            wsp = Space(nc, setup_ctx, "xs")
            wq, wkv, wout = wsp.sb("wq", [D, 4, D]), wsp.sb("wkv", [D, 8, D]), wsp.sb("wout", [D, 4, D])
            wT = wsp.sb("wT", [D, 12, D])
            kept = wsp.sb("kept", [S, NB])
            early = wsp.sb("early", [1, 2])
            bank = [wsp.ps(f"bank{i}") for i in range(7)]
            w_in, pe_done, dve_done, moments, std_ready, chain = [
                wsp.sem(n) for n in ("w_in", "pe_done", "dve_done", "moments",
                                     "std_ready", "chain")]
            block = setup_ctx.enter_context(nc.Block())

            @block.sync
            def _(sync):
                sync.dma_start(wq[:, :, :], ins["L0_xattn_Wq"].rearrange("p (j n) -> p j n", j=4)).then_inc(w_in, 16)
                sync.dma_start(wkv[:, :, :], ins["L0_xattn_Wkv"].rearrange("p (j n) -> p j n", j=8)).then_inc(w_in, 16)
                sync.dma_start(wout[:, :, :], ins["L0_xattn_Wout"].rearrange("(j p) n -> p j n", p=D)).then_inc(w_in, 16)
                sync.dma_start(gamma[:, :], ins["L0_xattn_ln_gamma"].rearrange("(p a) -> p a", a=1)).then_inc(w_in, 16)
                sync.dma_start(beta[:, :], ins["L0_xattn_ln_beta"].rearrange("(p a) -> p a", a=1)).then_inc(w_in, 16)

            @block.scalar
            def _(act):
                for i in range(2):
                    act.wait_ge(moments, i + 1)
                    act.activation(std[:, :], var[:, :], ACT.Sqrt).then_inc(std_ready, 1)

            @block.tensor
            def _(pe):
                pe.wait_ge(w_in, 16 * 5)
                for i in range(12):
                    w = wq[:, i, :] if i < 4 else wkv[:, i - 4, :]
                    ins_ = pe.transpose(bank[i // 4][:, (i % 4) * D:(i % 4 + 1) * D], w, st.ident[:, :])
                ins_.then_inc(pe_done, 1)
                pe.wait_ge(dve_done, 1)
                for h in range(H):
                    rows = slice(HD * (h % 2), HD * (h % 2) + HD)
                    pe.matmul(bank[3 + h % 2][:, (h // 2) * D:(h // 2 + 1) * D], wT[rows, h // 2, :], wT[rows, 4 + h // 2, :],
                              start=True, stop=True)
                for h in range(H):
                    rows = slice(HD * (h % 2), HD * (h % 2) + HD)
                    ins_ = pe.matmul(bank[5 + h % 2][:, (h // 2) * D:(h // 2 + 1) * D], wT[rows, 8 + h // 2, :],
                                     wout[rows, h // 2, :], start=True, stop=True)
                ins_.then_inc(pe_done, 1)

            @block.vector
            def _(dve):
                link = Chain(dve, chain)
                dve.wait_ge(pe_done, 1)
                for i in range(3):
                    c = dve.tensor_copy(wT[:, 4 * i:4 * i + 4, :], bank[i][:, :].rearrange("p (j n) -> p j n", j=4))
                c.then_inc(dve_done, 1)
                layernorm_moments(dve, link, st, tmp, var)
                link(dve.tensor_copy(tmp[:, :], var[:, :]))
                dve.tensor_scalar(var[:, :], var[:, :], EPS, None, ALU.add).then_inc(moments, 1)
                dve.wait_ge(std_ready, 1)
                link(dve.reciprocal(st.rstd[:, :], std[:, :]))
                link(dve.tensor_tensor(tmp[:, :], tmp[:, :], st.rstd[:, :], ALU.mult))
                link(dve.tensor_tensor(tmp[:, :], tmp[:, :], st.rstd[:, :], ALU.mult))
                dve.tensor_scalar(var[:, :], tmp[:, :], EPS, None, ALU.add).then_inc(moments, 1)
                dve.wait_ge(std_ready, 2)
                link(dve.reciprocal(tmp[:, :], std[:, :]))
                link(dve.tensor_tensor(st.rstd[:, :], st.rstd[:, :], tmp[:, :], ALU.mult))
                link(dve.tensor_scalar(kept[:, :], st.reach[:, :], 1.0, None, ALU.min))
                link(dve.reciprocal(tmp[:, :], kept[:, :]))
                link(dve.tensor_tensor(nanf[:, :], kept[:, :], tmp[:, :], ALU.mult))
                for i, plan in enumerate((LATE_PLAN, LAST_PLAN)):
                    link(dve.tensor_scalar(early[:, i:i + 1], st.reach[0:1, plan.start:plan.start + 1],
                                           float(CTX - plan.first), None, ALU.is_gt))
                link(dve.tensor_tensor(early[:, 0:1], early[:, 0:1], early[:, 1:2], ALU.max))
                link(dve.tensor_copy(flag[:, :], early[:, 0:1]))
                dve.wait_ge(pe_done, 2)
                for i in range(2):
                    dve.tensor_copy(wfold[:, i::2, :], bank[3 + i][:, :].rearrange("p (j n) -> p j n", j=4))
                    link(dve.tensor_copy(ofold[:, i::2, :], bank[5 + i][:, :].rearrange("p (j n) -> p j n", j=4)))

        cross_rows(nc, st, ins, "xa", wfold, ofold, gamma, beta, nanf, flag, (LATE_PLAN, WHOLE_PLAN))
        cross_rows(nc, st, ins, "xb", wfold, ofold, gamma, beta, nanf, flag, (LAST_PLAN, None))


def cross_rows(nc, st, ins, tag, wfold, ofold, gamma, beta, nanf, flag, plans):
    H, HD = 8, 64
    SCALE = float(HD) ** -0.5
    UN = 4
    PER = UN * H
    ctx_rows = ins["ctx_1024"]
    mask = ins["mask_BxS2_bk0"]
    with ExitStack() as ctx:
        sp = Space(nc, ctx, tag)
        sb, ps, sem = sp.sb, sp.ps, sp.sem
        xn = sb("xn", [S, D])
        xnT = sb("xnT", [D, S])
        qT = [sb(f"qT{i}", [D, H, S]) for i in range(2)]
        rows_in = [sb(f"rows{i}", [D, 12, D]) for i in range(UN)]
        ctxT = [sb(f"ctxT{i}", [D, CTX]) for i in range(2)]
        mask_rows = [sb(f"mask_rows{i}", [S, CTX], U8) for i in range(UN)]
        maskf = sb("maskf", [S, CTX])
        mask_add = [sb(f"mask_add{i}", [S, CTX]) for i in range(2)]
        probs = [sb(f"probs{i}", [S, CTX]) for i in range(4)]
        probsT = [sb(f"probsT{i}", [D, 12, S]) for i in range(2)]
        top, lowered, rowsum, inv = [sb(n, [S, 4]) for n in ("top", "lowered", "rowsum", "inv")]
        outT = [sb(f"outT{i}", [D, H, S]) for i in range(2)]
        psum = ps("psum", (128, 8 * 512))

        def bank_of(n):
            return psum[:, 512 * n:512 * (n + 1)]

        front, y_bank, pT_bank = bank_of(0), bank_of(1), [bank_of(2), bank_of(3)]

        names = ("rows_loaded0", "rows_loaded1", "rows_loaded2", "rows_loaded3", "ln_done", "front_ready",
                 "front_read", "mask_copied", "mask_made", "s_ready", "max_done", "shifted", "exp_done", "inv_done",
                 "normed", "pT_ready", "pT_read", "pv_done", "o_read", "y_ready", "added")
        sems = {n: sem(n) for n in names}
        gate = sem("gate")
        rows_loaded = [sems[f"rows_loaded{i}"] for i in range(UN)]
        (ln_done, front_ready, front_read, mask_copied, mask_made, s_ready, max_done, shifted, exp_done,
         inv_done, normed, pT_ready, pT_read, pv_done, o_read, y_ready, added) = [sems[n] for n in names[4:]]

        def score_bank(plan, t):
            if plan.score_bufs == 1:
                return psum[:, 4 * 512:7 * 512]
            return bank_of(4 + t.phase(2))

        def out_bank(plan, half):
            return bank_of(6 + half) if plan.out_banks == 2 else bank_of(7)

        block = ctx.enter_context(nc.Block())

        def sync_program(sync, plan):
            def load(place, slot):
                n = sync.value_load(st.order[0:1, bass.ds(plan.start + place, 1)], min_val=0, max_val=NB - 1)
                for lo, size, part in ((0, plan.main, plan.part), (plan.main, plan.tail, plan.tail)):
                    if size:
                        c0 = 0 if lo == 0 else plan.chunks
                        src = ctx_rows[bass.ds(n, 1), plan.first + lo:plan.first + lo + size, :]
                        sync.dma_start(rows_in[slot][0:part, c0:c0 + size // part, :],
                                       src.rearrange("a (p c) d -> (a p) c d", p=part)).then_inc(rows_loaded[slot], 16)
                sync.dma_start(mask_rows[slot][:, 0:plan.keys], mask[bass.ds(n, 1), plan.first:CTX]
                               .broadcast_to([S, plan.keys])).then_inc(rows_loaded[slot], 16)

            for n in range(UN):
                load(n, n)
            with sync.Fori(1, plan.count // UN) as it:
                for slot in range(UN):
                    n = it * UN + slot
                    sync.wait_ge(pv_done, (n - UN + 1) * H)
                    sync.wait_ge(mask_copied, n - UN + 1)
                    load(n, slot)

        def tensor_program(pe, plan):
            uses = plan.front_uses

            def step(t):
                c, ph = t.back(-H), plan.front_use(t)
                if c.exists(plan.items) and ph is not None:
                    n = c.index(H)
                    slot, slot4 = c.phase(2 * H) // H, c.phase(PER) // H
                    if ph == 0:
                        at_least(pe, ln_done, n + 1)
                        at_least(pe, front_read, uses * n)
                        pe.transpose(front[:, 0:S], xn[:, :], st.ident[0:S, 0:S]).then_inc(front_ready, 1)
                    elif ph <= 2:
                        at_least(pe, front_read, uses * n + ph)
                        for j in range(4):
                            i = pe.matmul(front[:, j * S:(j + 1) * S], wfold[:, 4 * (ph - 1) + j, :], xnT[:, :],
                                          start=True, stop=True)
                        i.then_inc(front_ready, 1)
                    else:
                        at_least(pe, front_read, uses * n + ph)
                        at_least(pe, rows_loaded[slot4], (t.back(-H).index(PER) + 1) * 16 * plan.loads)
                        base = plan.groups[ph - 3][0][0]
                        for j, (lo, size) in enumerate(plan.groups[ph - 3]):
                            i = pe.transpose(front[:, lo - base:lo - base + size],
                                             rows_in[slot4][0:size, 4 * (ph - 3) + j, :], st.ident[0:size, 0:size])
                        i.then_inc(front_ready, 1)
                if t.exists(plan.items):
                    k, n, h, slot = t.index(), t.index(H), t.phase(H), t.phase(2 * H) // H
                    at_least(pe, front_read, uses * (n + 1))
                    at_least(pe, shifted, k - plan.score_bufs + 1)
                    for lo in range(0, plan.keys, 512):
                        hi = min(lo + 512, plan.keys)
                        i = pe.matmul(score_bank(plan, t)[0:S, lo:hi], qT[slot][:, h, :], ctxT[slot][:, lo:hi],
                                      start=True, stop=True)
                    i.then_inc(s_ready, 1)
                u = t.back(3)
                if u.exists(plan.items):
                    k = u.index()
                    at_least(pe, normed, k + 1)
                    for g, cuts in enumerate(plan.groups):
                        n_before = k * len(plan.groups) + g
                        at_least(pe, pT_read, n_before - 1)
                        slot = (u.phase(2) * len(plan.groups) + g) % 2
                        for j, (lo, size) in enumerate(cuts):
                            i = pe.transpose(pT_bank[slot][0:size, j * S:(j + 1) * S],
                                             probs[u.phase(4)][:, lo:lo + size], st.ident[0:S, 0:S])
                        i.then_inc(pT_ready, 1)
                u = t.back(4)
                if u.exists(plan.items):
                    k, h, slot4 = u.index(), u.phase(H), u.phase(PER) // H
                    if h % 4 == 0:
                        at_least(pe, o_read, u.index(4) - plan.out_banks + 1)
                    for g, cuts in enumerate(plan.groups):
                        at_least(pe, pT_read, k * len(plan.groups) + g + 1)
                        for j, (lo, size) in enumerate(cuts):
                            c = 4 * g + j
                            i = pe.matmul(out_bank(plan, h // 4)[:, (h % 4) * S:(h % 4 + 1) * S],
                                          rows_in[slot4][0:size, c, :], probsT[u.phase(2)][0:size, c, :],
                                          start=(c == 0), stop=(c == len(plan.cuts) - 1))
                    i.then_inc(pv_done, 1)
                u = t.back(15)
                if u.phase(H) == 0 and u.exists(plan.items):
                    n, slot = u.index(H), u.phase(2 * H) // H
                    at_least(pe, o_read, 2 * (n + 1))
                    at_least(pe, added, n)
                    for h in range(H):
                        i = pe.matmul(y_bank[0:S, 0:D], outT[slot][:, h, :], ofold[:, h, :],
                                      start=(h == 0), stop=(h == H - 1))
                    i.then_inc(y_ready, 1)

            run_steps(pe, step, H, plan.items, 17, PER, 1)

        def scalar_program(act, plan):
            uses = plan.front_uses

            def step(t):
                c, ph = t.back(-H), plan.front_use(t)
                if c.exists(plan.items) and ph is not None:
                    n, slot = c.index(H), c.phase(2 * H) // H
                    at_least(act, front_ready, uses * n + ph + 1)
                    if ph == 0:
                        act.activation(xnT[:, :], front[:, 0:S], ACT.Identity, bias=beta[:, 0:1], scale=gamma[:, 0:1])\
                            .then_inc(front_read, 1)
                    elif ph <= 2:
                        act.activation(qT[slot][:, 4 * (ph - 1):4 * ph, :],
                                       front[:, 0:4 * S].rearrange("p (h q) -> p h q", h=4), ACT.Copy).then_inc(front_read, 1)
                    else:
                        base = plan.groups[ph - 3][0][0]
                        width = sum(size for _, size in plan.groups[ph - 3])
                        act.activation(ctxT[slot][:, base:base + width], front[:, 0:width], ACT.Copy).then_inc(front_read, 1)
                u = t.back(3)
                if u.exists(plan.items):
                    k = u.index()
                    at_least(act, pv_done, k - 1)
                    for g, cuts in enumerate(plan.groups):
                        at_least(act, pT_ready, k * len(plan.groups) + g + 1)
                        slot = (u.phase(2) * len(plan.groups) + g) % 2
                        full = [c for c in cuts if c[1] == plan.part]
                        n_full = len(full)
                        if n_full < len(cuts):
                            act.activation(probsT[u.phase(2)][0:plan.tail, 4 * g + n_full, :],
                                           pT_bank[slot][0:plan.tail, n_full * S:(n_full + 1) * S], ACT.Copy)
                        act.activation(probsT[u.phase(2)][0:plan.part, 4 * g:4 * g + n_full, :],
                                       pT_bank[slot][0:plan.part, 0:n_full * S].rearrange("p (c q) -> p c q", c=n_full),
                                       ACT.Copy).then_inc(pT_read, 1)
                if t.exists(plan.items):
                    k, s4 = t.index(), t.phase(4)
                    at_least(act, shifted, k + 1)
                    p = probs[s4][:, 0:plan.keys]
                    act.activation(p, p, ACT.Exp, bias=lowered[:, s4:s4 + 1], scale=SCALE,
                                   accum_out=rowsum[:, s4:s4 + 1]).then_inc(exp_done, 1)

            run_steps(act, step, H, plan.items, 4, PER, 1)

        def vector_program(dve, plan):
            uses = plan.front_uses

            def step(t):
                c = t.back(-2 * H)
                if t.phase(H) == H // 2 and c.exists(plan.items):
                    n = c.index(H)
                    at_least(dve, front_ready, uses * (n - 1) + 1)
                    p = plan.start + n
                    dve.tensor_scalar(xn[:, :], st.xs[:, p, :], st.mean[:, bass.ds(p, 1)], st.rstd[:, bass.ds(p, 1)],
                                      ALU.subtract, ALU.mult).then_inc(ln_done, 1)
                if t.exists(plan.items):
                    k, n, s4 = t.index(), t.index(H), t.phase(4)
                    at_least(dve, s_ready, k + 1)
                    at_least(dve, mask_made, n + 1)
                    at_least(dve, pT_ready, (k - 3) * len(plan.groups))
                    dve.sem_inc(gate, 1)
                    dve.tensor_tensor_reduce(probs[s4][:, 0:plan.keys], score_bank(plan, t)[0:S, 0:plan.keys],
                                             mask_add[t.phase(2 * H) // H][:, 0:plan.keys], 1.0, -BIG, ALU.add,
                                             ALU.max, top[:, s4:s4 + 1]).then_inc(max_done, 1)
                u = t.back(1)
                if u.exists(plan.items):
                    s4 = u.phase(4)
                    at_least(dve, exp_done, u.index() + 1)
                    dve.reciprocal(inv[:, s4:s4 + 1], rowsum[:, s4:s4 + 1]).then_inc(inv_done, 1)
                if t.exists(plan.items):
                    k, s4 = t.index(), t.phase(4)
                    at_least(dve, max_done, k + 1)
                    dve.tensor_scalar(lowered[:, s4:s4 + 1], top[:, s4:s4 + 1], -SCALE, None, ALU.mult)\
                        .then_inc(shifted, 1)
                if u.exists(plan.items):
                    s4 = u.phase(4)
                    p = probs[s4][:, 0:plan.keys]
                    at_least(dve, inv_done, u.index() + 1)
                    dve.tensor_scalar(p, p, inv[:, s4:s4 + 1], None, ALU.mult).then_inc(normed, 1)
                u = t.back(5)
                if u.phase(4) == 3 and u.exists(plan.items):
                    k, n, slot, half = u.index(), u.index(H), u.phase(2 * H) // H, u.phase(H) // 4
                    at_least(dve, pv_done, k + 1)
                    at_least(dve, y_ready, n - 1)
                    dve.tensor_copy(outT[slot][:, 4 * half:4 * half + 4, :], out_bank(plan, half)[:, 0:4 * S]
                                    .rearrange("p (h q) -> p h q", h=4)).then_inc(o_read, 1)
                u = t.back(16)
                if u.phase(H) == 0 and u.exists(plan.items):
                    n = u.index(H)
                    at_least(dve, y_ready, n + 1)
                    p = plan.start + n
                    x = st.xs[:, p, :]
                    dve.scalar_tensor_tensor(x, y_bank[0:S, 0:D], nanf[:, bass.ds(p, 1)], x, ALU.mult, ALU.add)\
                        .then_inc(added, 1)
                u = t.back(17)
                if u.phase(H) == 0 and u.exists(plan.items):
                    n = u.index(H)
                    p = plan.start + n
                    at_least(dve, added, n + 1)
                    dve.bn_stats(st.stats[:, p, :], st.xs[:, p, :])

            run_steps(dve, step, 2 * H, plan.items, 17, PER, 1)

        def pool_program(pool, plan):
            def step(t):
                c = t.back(-H)
                if t.phase(H) == 0 and c.exists(plan.items):
                    n, slot = c.index(H), c.phase(2 * H) // H
                    slot4 = c.phase(PER) // H
                    rows = mask_rows[slot4]
                    at_least(pool, rows_loaded[slot4], (t.back(-H).index(PER) + 1) * 16 * plan.loads)
                    at_least(pool, mask_made, n)
                    pool.sem_inc(gate, 1)
                    i = pool.tensor_copy(maskf[:, 0:plan.main].rearrange("p (c r) -> p c r", c=plan.chunks),
                                         rows[:, 0:plan.main].rearrange("p (r c) -> p c r", c=plan.chunks))
                    if plan.tail:
                        i = pool.tensor_copy(maskf[:, plan.main:plan.keys], rows[:, plan.main:plan.keys])
                    i.then_inc(mask_copied, 1)
                    at_least(pool, shifted, (n - 1) * H)
                    pool.wait_ge(mask_copied, n + 1)
                    pool.sem_inc(gate, 1)
                    pool.tensor_scalar(mask_add[slot][:, 0:plan.keys], maskf[:, 0:plan.keys], BIG, -BIG,
                                       ALU.mult, ALU.add).then_inc(mask_made, 1)

            run_steps(pool, step, H, plan.items, 0, PER, 1)

        def late_or_whole(eng, program):
            late, whole = plans
            early_kept = eng.value_load(flag[0:1, 0:1], min_val=0, max_val=1)
            with eng.If(early_kept == 0):
                program(eng, late)
            if whole:
                with eng.Else():
                    program(eng, whole)

        @block.sync
        def _(sync):
            late_or_whole(sync, sync_program)

        @block.tensor
        def _(pe):
            late_or_whole(pe, tensor_program)

        @block.scalar
        def _(act):
            late_or_whole(act, scalar_program)

        @block.vector
        def _(dve):
            late_or_whole(dve, vector_program)

        @block.gpsimd
        def _(pool):
            late_or_whole(pool, pool_program)


def experts(nc, st, ins):
    E, F, FQ = 8, 512, 4
    G = 4
    with ExitStack() as ctx:
        sp = Space(nc, ctx, "ex")
        sb, sem = sp.sb, sp.sem
        w1, w2 = sb("w1", [D, E, F]), sb("w2", [D, E, FQ, D])
        b1row, b1 = sb("b1row", [E * FQ, D]), sb("b1", [D, E * FQ])
        b2 = sb("b2", [E, D])
        gates = sb("gates", [S, NB, E])
        xnT = sb("xnT", [D, NB * S])
        w_in = sem("w_in")

        with ExitStack() as route_ctx:
            rsp = Space(nc, route_ctx, "er")
            tmp, var, std = rsp.sb("tmp", [S, NB]), rsp.sb("var", [S, NB]), rsp.sb("std", [S, NB])
            wr, brow, pref = rsp.sb("wr", [D, E]), rsp.sb("brow", [S, E]), rsp.sb("pref", [S, E])
            logits, expo, pick = [rsp.sb(n, [S, NB, E]) for n in ("logits", "expo", "pick")]
            best, total = rsp.sb("best", [S, NB]), rsp.sb("total", [S, NB])
            xn = [rsp.sb(f"xn{i}", [S, D]) for i in range(2)]
            xnTs = [rsp.sb(f"xnTs{i}", [D, S]) for i in range(2)]
            turned = [rsp.ps(f"turned{i}") for i in range(2)]
            lg = [rsp.ps(f"lg{i}") for i in range(2)]
            b1bank = rsp.ps("b1bank")
            (r_in, moments, std_ready, chain, b1_ready, ln_done, xT_ready, xT_read, copied, lg_ready, lg_read, shifted,
             exp_done) = [rsp.sem(n) for n in ("r_in", "moments", "std_ready", "chain", "b1_ready", "ln_done",
                                               "xT_ready", "xT_read", "copied", "lg_ready", "lg_read", "shifted", "exp_done")]
            block = route_ctx.enter_context(nc.Block())

            @block.sync
            def _(sync):
                sync.dma_start(wr[:, :], ins["L0_ffn_Wr"]).then_inc(r_in, 16)
                sync.dma_start(brow[:, :], ins["L0_ffn_br"].rearrange("(a n) -> a n", a=1).broadcast_to([S, E])).then_inc(r_in, 16)
                sync.dma_start(pref[:, :], ins["c_pref"]).then_inc(r_in, 16)
                sync.dma_start(b1row[:, :], ins["L0_ffn_b1"].rearrange("e (j p) -> (e j) p", p=D)).then_inc(r_in, 16)
                sync.dma_start(b2[:, :], ins["L0_ffn_b2"]).then_inc(r_in, 16)
                for h in range(2):
                    half = slice(4 * h, 4 * h + 4)
                    sync.dma_start(w1[:, half, :], ins["L0_ffn_W1"][half].rearrange("e d f -> d e f")).then_inc(w_in, 16)
                    sync.dma_start(w2[:, half, :, :], ins["L0_ffn_W2"][half].rearrange("e (j p) o -> p e j o", p=D))\
                        .then_inc(w_in, 16)

            @block.tensor
            def _(pe):
                pe.wait_ge(r_in, 80)
                pe.transpose(b1bank[:, 0:E * FQ], b1row[:, :], st.ident[0:E * FQ, 0:E * FQ]).then_inc(b1_ready, 1)

                def step(t):
                    if t.exists(NB):
                        n, s = t.index(), t.phase(2)
                        at_least(pe, ln_done, n + 1)
                        at_least(pe, xT_read, n - 1)
                        pe.transpose(turned[s][:, 0:S], xn[s][:, :], st.ident[0:S, 0:S]).then_inc(xT_ready, 1)
                    u = t.back(1)
                    if u.exists(NB):
                        n, s = u.index(), u.phase(2)
                        at_least(pe, xT_read, n + 1)
                        at_least(pe, lg_read, n - 1)
                        pe.matmul(lg[s][0:S, 0:E], xnTs[s][:, :], wr[:, :], start=True, stop=True).then_inc(lg_ready, 1)

                run_steps(pe, step, 0, NB, 2, 2, 1)

            @block.scalar
            def _(act):
                act.wait_ge(moments, 1)
                act.activation(std[:, :], var[:, :], ACT.Sqrt).then_inc(std_ready, 1)

                def step(t):
                    if t.exists(NB):
                        n, s = t.index(), t.phase(2)
                        at_least(act, xT_ready, n + 1)
                        at_least(act, lg_ready, n - 1)
                        at_least(act, copied, n - 1)
                        act.activation(xnTs[s][:, :], turned[s][:, 0:S], ACT.Copy).then_inc(xT_read, 1)

                run_steps(act, step, 0, NB, 0, 2, 1)
                act.wait_ge(shifted, 1)
                act.activation(expo[:, :, :], logits[:, :, :], ACT.Exp).then_inc(exp_done, 1)

            @block.gpsimd
            def _(pool):
                def step(t):
                    if t.exists(NB):
                        n, s = t.index(), t.phase(2)
                        at_least(pool, xT_read, n + 1)
                        start = n * S
                        pool.tensor_copy(xnT[:, bass.ds(start, S)], xnTs[s][:, :]).then_inc(copied, 1)

                run_steps(pool, step, 0, NB, 0, 2, 1)

            @block.vector
            def _(dve):
                link = Chain(dve, chain)
                layernorm_moments(dve, link, st, tmp, var)
                dve.tensor_scalar(var[:, :], var[:, :], EPS, None, ALU.add).then_inc(moments, 1)
                dve.wait_ge(std_ready, 1)
                link(dve.reciprocal(st.rstd[:, :], std[:, :]))
                dve.wait_ge(r_in, 80)
                dve.wait_ge(b1_ready, 1)
                dve.tensor_copy(b1[:, :], b1bank[:, 0:E * FQ])

                def step(t):
                    if t.exists(NB):
                        n, s = t.index(), t.phase(2)
                        at_least(dve, xT_ready, n - 1)
                        dve.tensor_scalar(xn[s][:, :], st.xs[:, n, :], st.mean[:, bass.ds(n, 1)],
                                          st.rstd[:, bass.ds(n, 1)], ALU.subtract, ALU.mult).then_inc(ln_done, 1)
                    u = t.back(2)
                    if u.exists(NB):
                        n = u.index()
                        at_least(dve, lg_ready, n + 1)
                        dve.tensor_tensor(logits[:, n, :], lg[u.phase(2)][0:S, 0:E], brow[:, :], ALU.add).then_inc(lg_read, 1)

                run_steps(dve, step, 0, NB, 3, 2, 1)
                dve.wait_ge(lg_read, NB)

                def over_experts(v):
                    return v[:, :].rearrange("p (n a) -> p n a", a=1).broadcast_to([S, NB, E])

                link(dve.tensor_reduce(best[:, :], logits[:, :, :], AX.X, ALU.max))
                dve.tensor_tensor(logits[:, :, :], logits[:, :, :], over_experts(best), ALU.subtract).then_inc(shifted, 1)
                dve.wait_ge(shifted, 1)
                link(dve.tensor_scalar(pick[:, :, :], logits[:, :, :], 0.0, None, ALU.is_equal))
                link(dve.tensor_tensor(pick[:, :, :], pick[:, :, :],
                                       pref[:, :].rearrange("p (a e) -> p a e", a=1).broadcast_to([S, NB, E]), ALU.mult))
                link(dve.tensor_reduce(best[:, :], pick[:, :, :], AX.X, ALU.max))
                link(dve.tensor_tensor(pick[:, :, :], pick[:, :, :], over_experts(best), ALU.is_equal))
                dve.wait_ge(exp_done, 1)
                link(dve.tensor_reduce(total[:, :], expo[:, :, :], AX.X, ALU.add))
                link(dve.reciprocal(total[:, :], total[:, :]))
                link(dve.tensor_tensor(gates[:, :, :], pick[:, :, :], over_experts(total), ALU.mult))

        hidden = [sb(f"hidden{i}", [D, G * S]) for i in range(4)]
        gateT = sb("gateT", [E, G * S])
        hbank = [sp.ps(f"hbank{i}") for i in range(2)]
        ybank = [sp.ps(f"ybank{i}") for i in range(2)]
        gbank, bias_bank = sp.ps("gbank"), sp.ps("bias_bank")
        h_ready, h_read, y_ready, y_read, g_ready, g_read, bias_ready, bias_read, last_added, stats_done = [
            sem(n) for n in ("h_ready", "h_read", "y_ready", "y_read", "g_ready", "g_read", "bias_ready", "bias_read",
                             "last_added", "stats_done")]
        gates_now = sb("gates_now", [S, G, E])
        gates_set = sem("gates_set")
        PER = E * FQ
        ITEMS = NB // G * PER
        block = ctx.enter_context(nc.Block())

        @block.tensor
        def _(pe):
            pe.wait_ge(w_in, 64)

            def step(t):
                g, ph = t.index(PER), t.phase(PER)
                if t.exists(ITEMS):
                    k, e, f = t.index(), ph // FQ, ph % FQ
                    at_least(pe, h_read, k - 1)
                    start = g * (G * S)
                    pe.matmul(hbank[t.phase(2)][:, 0:G * S], w1[:, e, f * D:(f + 1) * D], xnT[:, bass.ds(start, G * S)],
                              start=True, stop=True).then_inc(h_ready, 1)
                if ph == 4 and t.exists(ITEMS):
                    at_least(pe, gates_set, g + 1)
                    at_least(pe, g_read, g)
                    for b in range(G):
                        i = pe.transpose(gbank[0:E, b * S:(b + 1) * S], gates_now[:, b, :], st.ident[0:S, 0:S])
                    i.then_inc(g_ready, 1)
                if ph == 7 and t.exists(ITEMS):
                    at_least(pe, g_read, g + 1)
                    at_least(pe, bias_read, g)
                    for b in range(G):
                        i = pe.matmul(bias_bank[0:S, b * D:(b + 1) * D], gateT[:, b * S:(b + 1) * S], b2[:, :],
                                      start=True, stop=True)
                    i.then_inc(bias_ready, 1)
                u = t.back(2)
                if u.exists(ITEMS):
                    k, ph = u.index(), u.phase(PER)
                    e, f = ph // FQ, ph % FQ
                    at_least(pe, h_read, k + 1)
                    if f == 0:
                        at_least(pe, y_read, u.index(FQ) - 1)
                    for b in range(G):
                        i = pe.matmul(ybank[e % 2][0:S, b * D:(b + 1) * D], hidden[u.phase(4)][:, b * S:(b + 1) * S],
                                      w2[:, e, f, :], start=(f == 0 and b == 0), stop=(f == FQ - 1),
                                      skip_group_check=True)
                    i.then_inc(y_ready, 1)

            run_steps(pe, step, 0, ITEMS, 3, PER, 1)

        @block.scalar
        def _(act):
            def step(t):
                if t.exists(ITEMS):
                    k, ph = t.index(), t.phase(PER)
                    at_least(act, h_ready, k + 1)
                    at_least(act, y_ready, k - 3)
                    act.activation(hidden[t.phase(4)][:, :], hbank[t.phase(2)][:, 0:G * S], ACT.Gelu,
                                   bias=b1[:, ph:ph + 1]).then_inc(h_read, 1)
                    if ph == 6:
                        g = t.index(PER)
                        at_least(act, g_ready, g + 1)
                        at_least(act, bias_ready, g)
                        act.activation(gateT[:, :], gbank[0:E, 0:G * S], ACT.Copy).then_inc(g_read, 1)

            run_steps(act, step, 0, ITEMS, 0, PER, 1)

        @block.vector
        def _(dve):
            def step(t):
                g, ph = t.index(PER), t.phase(PER)
                if t.exists(ITEMS) and ph == 0:
                    at_least(dve, g_ready, g)
                    first = g * G
                    dve.tensor_copy(gates_now[:, :, :], gates[:, bass.ds(first, G), :]).then_inc(gates_set, 1)
                if t.exists(ITEMS) and ph == 9:
                    at_least(dve, bias_ready, g + 1)
                    at_least(dve, y_read, g * E + 1)
                    first = g * G
                    x = st.xs[:, bass.ds(first, G), :]
                    dve.tensor_tensor(x, bias_bank[0:S, :].rearrange("p (b d) -> p b d", b=G), x, ALU.add)\
                        .then_inc(bias_read, 1)
                    at_least(dve, bias_read, g + 1)
                u = t.back(3)
                if u.phase(FQ) == 3 and u.exists(ITEMS):
                    g, e, k = u.index(PER), u.phase(PER) // FQ, u.index()
                    at_least(dve, y_ready, k + 1)
                    at_least(dve, y_read, g * E + e)
                    for b in range(G):
                        n = g * G + b
                        x = st.xs[:, n, :]
                        i = dve.scalar_tensor_tensor(x, ybank[e % 2][0:S, b * D:(b + 1) * D],
                                                     gates[:, n, e:e + 1], x, ALU.mult, ALU.add)
                    i.then_inc(y_read, 1)
                    if e == E - 1:
                        dve.wait_ge(y_read, (g + 1) * E)
                        for b in range(G):
                            n = g * G + b
                            dve.bn_stats(st.stats[:, n, :], st.xs[:, n, :])

            run_steps(dve, step, 0, ITEMS, 4, PER, 1)


def context_attention(nc, st, ins):
    plan = WHOLE_PLAN
    R = 3
    ITEMS = NB * R
    UN = 4
    PER = UN * R
    G = 4
    with ExitStack() as ctx:
        sp = Space(nc, ctx, "cx")
        sb, sem = sp.sb, sp.sem
        wqv = sb("wqv", [D, 4, D])
        brow = sb("brow", [S, D])
        wsim, bsim = sb("wsim", [D, 3]), sb("bsim", [S, 1])
        eT_all = sb("eT_all", [D, NB * S])
        mx, weight = sb("mx", [S, NB]), sb("weight", [S, NB])
        w_in = sem("w_in")
        with ExitStack() as part_ctx:
            psp = Space(nc, part_ctx, "cp")
            psb, psem = psp.sb, psp.sem
            tmp, var, std = psb("tmp", [S, NB]), psb("var", [S, NB]), psb("std", [S, NB])
            e = psb("e", [S, D])
            eT = [psb(f"eT{i}", [D, S]) for i in range(UN)]
            qT = [psb(f"qT{i}", [D, S]) for i in range(2)]
            rows_in = [psb(f"rows{i}", [D, 12, D]) for i in range(UN)]
            ctxT = [psb(f"ctxT{i}", [D, CTX]) for i in range(2)]
            probs = [psb(f"probs{i}", [S, CTX]) for i in range(2)]
            probsT = [psb(f"probsT{i}", [D, 4, S]) for i in range(2)]
            top3 = [psb(f"top3{i}", [S, R]) for i in range(2)]
            low = [psb(f"low{i}", [S, 1]) for i in range(2)]
            sum3 = [psb(f"sum3{i}", [S, R]) for i in range(UN)]
            inv = psb("inv", [S, 2])
            hT, ehT = psb("hT", [D, S]), psb("ehT", [D, S])
            sbank = psp.ps("sbank", (128, 3 * 512))
            front = [psp.ps(f"front{i}") for i in range(2)]
            pT_bank, h_bank, y_bank = psp.ps("pT_bank"), psp.ps("h_bank"), psp.ps("y_bank")
            rows_loaded = [psem(f"rows_loaded{i}") for i in range(UN)]
            (moments, std_ready, chain, e_ready, f_ready, f_read, eT_copied, bias_added, s_ready, top_done, tops, low_ready,
             exp_done, pT_ready, pT_read, pv_done, hT_read, ehT_made, y_ready, total_done, inv_done, half_added, added) = [
                psem(n) for n in (
                    "moments", "std_ready", "chain", "e_ready", "f_ready", "f_read", "eT_copied", "bias_added", "s_ready",
                    "top_done", "tops", "low_ready", "exp_done", "pT_ready", "pT_read", "pv_done", "hT_read", "ehT_made",
                    "y_ready", "total_done", "inv_done", "half_added", "added")]
            ctx_rows = ins["ctx_1024"]
            block = part_ctx.enter_context(nc.Block())

            def region(t):
                lo = 512 * t.phase(R)
                return lo, min(lo + 512, plan.keys)

            @block.sync
            def _(sync):
                def load(place, slot):
                    n = sync.value_load(st.order[0:1, bass.ds(place, 1)], min_val=0, max_val=NB - 1)
                    for lo, size, part in ((0, plan.main, plan.part), (plan.main, plan.tail, plan.tail)):
                        c0 = 0 if lo == 0 else plan.chunks
                        sync.dma_start(rows_in[slot][0:part, c0:c0 + size // part, :],
                                       ctx_rows[bass.ds(n, 1), lo:lo + size, :].rearrange("a (p c) d -> (a p) c d", p=part))\
                            .then_inc(rows_loaded[slot], 16)

                for j in range(3):
                    sync.dma_start(wsim[:, j:j + 1], ins["L1_xattn_w_sim"][j * D:(j + 1) * D].rearrange("(p a) -> p a", a=1))\
                        .then_inc(w_in, 16)
                sync.dma_start(bsim[:, :], ins["L1_xattn_b_sim"].rearrange("(a n) -> a n", a=1).broadcast_to([S, 1])).then_inc(w_in, 16)
                load(0, 0)
                sync.dma_start(wqv[:, :, :], ins["L1_xattn_W_qv"].rearrange("(j p) o -> p j o", p=D)).then_inc(w_in, 16)
                sync.dma_start(brow[:, :], ins["L1_xattn_b_qv"].rearrange("(a n) -> a n", a=1).broadcast_to([S, D])).then_inc(w_in, 16)
                for n in range(1, UN):
                    load(n, n)
                with sync.Fori(1, NB // UN) as it:
                    for slot in range(UN):
                        n = it * UN + slot
                        sync.wait_ge(pv_done, (n - UN + 1) * R)
                        load(n, slot)

            @block.tensor
            def _(pe):
                pe.wait_ge(w_in, 96)

                def step(t):
                    c, ph = t.back(-R), t.phase(R)
                    if c.exists(ITEMS):
                        n, slot4 = c.index(R), c.phase(PER) // R
                        if ph == 0:
                            at_least(pe, e_ready, n + 1)
                            at_least(pe, f_read, 4 * n - 1)
                            pe.transpose(front[0][:, 0:S], e[:, :], st.ident[0:S, 0:S]).then_inc(f_ready, 1)
                            at_least(pe, rows_loaded[slot4], (c.index(PER) + 1) * 32)
                        at_least(pe, f_read, 4 * n + ph)
                        for j, (lo, size) in enumerate(plan.groups[ph]):
                            i = pe.transpose(front[(ph + 1) % 2][:, 128 * j:128 * j + size],
                                             rows_in[slot4][0:size, 4 * ph + j, :], st.ident[0:size, 0:size])
                        i.then_inc(f_ready, 1)
                    u = t.back(3)
                    if u.exists(ITEMS):
                        k = u.index()
                        at_least(pe, exp_done, k + 1)
                        at_least(pe, pT_read, k)
                        for j, (lo, size) in enumerate(plan.groups[u.phase(R)]):
                            i = pe.transpose(pT_bank[0:size, j * S:(j + 1) * S], probs[u.phase(2 * R) // R][:, lo:lo + size],
                                             st.ident[0:S, 0:S])
                        i.then_inc(pT_ready, 1)
                    if t.exists(ITEMS):
                        k, n = t.index(), t.index(R)
                        lo, hi = region(t)
                        at_least(pe, f_read, 4 * (n + 1))
                        at_least(pe, exp_done, k - 2)
                        slot = t.phase(2 * R) // R
                        pe.matmul(sbank[0:S, lo:hi], qT[slot][:, :], ctxT[slot][:, lo:hi], start=True, stop=True)\
                            .then_inc(s_ready, 1)
                    u = t.back(4)
                    if u.exists(ITEMS):
                        k, r, n = u.index(), u.phase(R), u.index(R)
                        at_least(pe, pT_read, k + 1)
                        if r == 0:
                            at_least(pe, hT_read, n)
                        for j, (lo, size) in enumerate(plan.groups[r]):
                            c = 4 * r + j
                            i = pe.matmul(h_bank[:, 0:S], rows_in[u.phase(PER) // R][0:size, c, :],
                                          probsT[u.phase(2)][0:size, j, :], start=(c == 0), stop=(c == 11))
                        i.then_inc(pv_done, 1)
                    u = t.back(8)
                    if u.phase(R) == 0 and u.exists(ITEMS):
                        n, slot4 = u.index(R), u.phase(PER) // R
                        at_least(pe, added, n)
                        pe.matmul(y_bank[0:S, 400:401], eT[slot4][:, :], wsim[:, 0:1], start=True, stop=True)
                        pe.matmul(y_bank[0:S, 0:D], eT[slot4][:, :], wqv[:, 0, :], start=True, stop=True)
                        at_least(pe, hT_read, n + 1)
                        at_least(pe, ehT_made, n + 1)
                        pe.matmul(y_bank[0:S, D:2 * D], hT[:, :], wqv[:, 1, :], start=True, stop=False)
                        pe.matmul(y_bank[0:S, D:2 * D], ehT[:, :], wqv[:, 2, :], start=False, stop=True).then_inc(y_ready, 1)

                run_steps(pe, step, R, ITEMS, 10, PER, 1)

            @block.scalar
            def _(act):
                act.wait_ge(moments, 1)
                act.activation(std[:, :], var[:, :], ACT.Sqrt).then_inc(std_ready, 1)

                def step(t):
                    u = t.back(2)
                    if u.exists(ITEMS):
                        k, n, r = u.index(), u.index(R), u.phase(R)
                        lo, hi = region(u)
                        slot = u.phase(2 * R) // R
                        at_least(act, low_ready, n + 1)
                        at_least(act, pT_ready, k - 5)
                        if r == 0:
                            at_least(act, added, n - UN + 1)
                        act.activation(probs[slot][:, lo:hi], sbank[0:S, lo:hi], ACT.Exp, bias=low[slot][:, 0:1],
                                       accum_out=sum3[u.phase(PER) // R][:, r:r + 1]).then_inc(exp_done, 1)
                    u = t.back(3)
                    if u.exists(ITEMS):
                        k, r = u.index(), u.phase(R)
                        at_least(act, pT_ready, k + 1)
                        at_least(act, pv_done, k - 1)
                        if r == 2:
                            act.activation(probsT[u.phase(2)][0:plan.tail, 3, :], pT_bank[0:plan.tail, 3 * S:4 * S], ACT.Copy)
                            act.activation(probsT[u.phase(2)][:, 0:3, :], pT_bank[:, 0:3 * S]
                                           .rearrange("p (c q) -> p c q", c=3), ACT.Copy).then_inc(pT_read, 1)
                        else:
                            act.activation(probsT[u.phase(2)][:, :, :], pT_bank[:, 0:4 * S]
                                           .rearrange("p (c q) -> p c q", c=4), ACT.Copy).then_inc(pT_read, 1)
                    u = t.back(6)
                    if u.phase(R) == 0 and u.exists(ITEMS):
                        n = u.index(R)
                        at_least(act, pv_done, R * (n + 1))
                        at_least(act, y_ready, n)
                        act.activation(hT[:, :], h_bank[:, 0:S], ACT.Copy).then_inc(hT_read, 1)

                run_steps(act, step, 0, ITEMS, 8, PER, 1)

            @block.gpsimd
            def _(pool):
                def step(t):
                    c = t.back(-R)
                    if t.phase(R) == 0 and c.exists(ITEMS):
                        n = c.index(R)
                        at_least(pool, e_ready, n + 1)
                        pool.wait_ge(w_in, 96)
                        x = st.xs[:, n, :]
                        pool.tensor_tensor(x, x, brow[:, :], ALU.add).then_inc(bias_added, 1)
                        at_least(pool, f_read, 4 * n + 1)
                        start = n * S
                        pool.tensor_copy(eT_all[:, bass.ds(start, S)], eT[c.phase(PER) // R][:, :]).then_inc(eT_copied, 1)

                run_steps(pool, step, R, ITEMS, 0, PER, 1)

            @block.vector
            def _(dve):
                link = Chain(dve, chain)
                layernorm_moments(dve, link, st, tmp, var)
                dve.tensor_scalar(var[:, :], var[:, :], EPS, None, ALU.add).then_inc(moments, 1)
                dve.wait_ge(std_ready, 1)
                link(dve.reciprocal(st.rstd[:, :], std[:, :]))
                dve.wait_ge(w_in, 96)

                def step(t):
                    c = t.back(-2 * R)
                    if t.phase(R) == 2 and c.exists(ITEMS):
                        n = c.index(R)
                        at_least(dve, f_ready, 4 * (n - 1) + 1)
                        dve.tensor_scalar(e[:, :], st.xs[:, n, :], st.mean[:, bass.ds(n, 1)], st.rstd[:, bass.ds(n, 1)],
                                          ALU.subtract, ALU.mult).then_inc(e_ready, 1)
                    if t.exists(ITEMS):
                        k, n, r = t.index(), t.index(R), t.phase(R)
                        lo, hi = region(t)
                        slot = t.phase(2 * R) // R
                        at_least(dve, s_ready, k + 1)
                        dve.tensor_reduce(top3[slot][:, r:r + 1], sbank[0:S, lo:hi], AX.X, ALU.max).then_inc(top_done, 1)
                        if r == 2:
                            dve.wait_ge(top_done, k + 1)
                            dve.tensor_reduce(mx[:, bass.ds(n, 1)], top3[slot][:, :], AX.X, ALU.max).then_inc(tops, 1)
                            at_least(dve, exp_done, R * (n - 1))
                            dve.wait_ge(tops, n + 1)
                            dve.tensor_scalar(low[slot][:, 0:1], mx[:, bass.ds(n, 1)], -1.0, None, ALU.mult)\
                                .then_inc(low_ready, 1)
                    c, ph = t.back(-R), t.phase(R)
                    if c.exists(ITEMS):
                        n, slot = c.index(R), c.phase(2 * R) // R
                        if ph == 0:
                            at_least(dve, f_ready, 4 * n + 1)
                            at_least(dve, y_ready, n - UN + 1)
                            at_least(dve, eT_copied, n - UN + 1)
                            dve.tensor_scalar(qT[slot][:, :], front[0][:, 0:S], wsim[:, 2:3], wsim[:, 1:2], ALU.mult, ALU.add)
                            dve.tensor_copy(eT[c.phase(PER) // R][:, :], front[0][:, 0:S]).then_inc(f_read, 1)
                        base = plan.groups[ph][0][0]
                        for lo, hi in ((base, min(base + 512, plan.keys)),):
                            at_least(dve, f_ready, 4 * n + ph + 2)
                            dve.tensor_copy(ctxT[slot][:, lo:hi], front[(ph + 1) % 2][:, 0:hi - lo]).then_inc(f_read, 1)
                    u = t.back(7)
                    if u.phase(R) == 0 and u.exists(ITEMS):
                        n, slot4 = u.index(R), u.phase(PER) // R
                        at_least(dve, hT_read, n + 1)
                        at_least(dve, y_ready, n)
                        dve.tensor_tensor(ehT[:, :], hT[:, :], eT[slot4][:, :], ALU.mult).then_inc(ehT_made, 1)
                        dve.tensor_reduce(inv[:, 0:1], sum3[slot4][:, :], AX.X, ALU.add).then_inc(total_done, 1)
                        dve.wait_ge(total_done, n + 1)
                        at_least(dve, half_added, n)
                        dve.reciprocal(inv[:, 1:2], inv[:, 0:1]).then_inc(inv_done, 1)
                    u = t.back(9)
                    if u.phase(R) == 0 and u.exists(ITEMS):
                        n = u.index(R)
                        x = st.xs[:, n, :]
                        at_least(dve, y_ready, n + 1)
                        at_least(dve, bias_added, n + 1)
                        at_least(dve, inv_done, n + 1)
                        dve.scalar_tensor_tensor(x, y_bank[0:S, D:2 * D], inv[:, 1:2], x, ALU.mult, ALU.add)\
                            .then_inc(half_added, 1)
                        dve.scalar_tensor_tensor(weight[:, bass.ds(n, 1)], y_bank[0:S, 400:401], bsim[:, 0:1],
                                                 mx[:, bass.ds(n, 1)], ALU.add, ALU.add)
                        dve.wait_ge(half_added, n + 1)
                        dve.tensor_tensor(x, y_bank[0:S, 0:D], x, ALU.add).then_inc(added, 1)

                run_steps(dve, step, 2 * R, ITEMS, 10, PER, 1)

        tokens = sb("tokens", [NB, S])
        lowest, total = sb("lowest", [NB, 1]), sb("total", [NB, 2])
        spread = sb("spread", [NB, NB * S])
        ones = sb("ones", [NB, D])
        weighed = [sb(f"weighed{i}", [D, G, S]) for i in range(2)]
        mean_e = [sb(f"mean_e{i}", [D, G]) for i in range(2)]
        ecT = [sb(f"ecT{i}", [D, G, S]) for i in range(2)]
        wbank = sp.ps("wbank")
        bbank = [sp.ps(f"bbank{i}") for i in range(2)]
        obank = [sp.ps(f"obank{i}") for i in range(2)]
        (t_ready, low_done, e_done, spread_done, chain2, b_ready, b_read, m_done, ec_done, o_ready, o_read) = [
            sem(n) for n in ("t_ready", "low_done", "e_done", "spread_done", "chain2", "b_ready", "b_read", "m_done",
                             "ec_done", "o_ready", "o_read")]
        block = ctx.enter_context(nc.Block())
        GROUPS = NB // G

        @block.tensor
        def _(pe):
            pe.transpose(wbank[0:NB, 0:S], weight[:, :], st.ident[0:S, 0:S]).then_inc(t_ready, 1)
            pe.wait_ge(spread_done, 1)

            def step(t):
                if t.exists(GROUPS):
                    g = t.index()
                    at_least(pe, b_read, g - 1)
                    start = g * (G * S)
                    pe.matmul(bbank[t.phase(2)][:, 0:G * S], ones[:, :], spread[:, bass.ds(start, G * S)],
                              start=True, stop=True).then_inc(b_ready, 1)
                u = t.back(1)
                if u.exists(GROUPS):
                    g = u.index()
                    at_least(pe, ec_done, g + 1)
                    at_least(pe, o_read, g - 1)
                    for b in range(G):
                        i = pe.matmul(obank[u.phase(2)][0:S, b * D:(b + 1) * D], ecT[u.phase(2)][:, b, :], wqv[:, 3, :],
                                      start=True, stop=True)
                    i.then_inc(o_ready, 1)

            run_steps(pe, step, 0, GROUPS, 2, 2, 1)

        @block.scalar
        def _(act):
            act.wait_ge(low_done, 1)
            act.activation(tokens[:, :], wbank[0:NB, 0:S], ACT.Exp, bias=lowest[:, 0:1], accum_out=total[:, 0:1])\
                .then_inc(e_done, 1)

        @block.vector
        def _(dve):
            link = Chain(dve, chain2)
            dve.memset(ones[:, :], 1.0)
            dve.wait_ge(t_ready, 1)
            link(dve.tensor_reduce(lowest[:, :], wbank[0:NB, 0:S], AX.X, ALU.max))
            dve.tensor_scalar(lowest[:, :], lowest[:, :], -1.0, None, ALU.mult).then_inc(low_done, 1)
            dve.wait_ge(e_done, 1)
            link(dve.reciprocal(total[:, 1:2], total[:, 0:1]))
            link(dve.tensor_scalar(tokens[:, :], tokens[:, :], total[:, 1:2], None, ALU.mult))
            dve.tensor_tensor(spread[:, :].rearrange("p (n s) -> p n s", n=NB),
                              tokens[:, :].rearrange("p (a s) -> p a s", a=1).broadcast_to([NB, NB, S]),
                              st.ident[0:NB, 0:NB].rearrange("p (n a) -> p n a", a=1).broadcast_to([NB, NB, S]),
                              ALU.mult).then_inc(spread_done, 1)

            def step(t):
                if t.exists(GROUPS):
                    g, s = t.index(), t.phase(2)
                    start = g * (G * S)
                    eT_g = eT_all[:, bass.ds(start, G * S)].rearrange("p (b q) -> p b q", b=G)
                    at_least(dve, b_ready, g + 1)
                    dve.tensor_tensor(weighed[s][:, :, :], bbank[s][:, 0:G * S].rearrange("p (b q) -> p b q", b=G), eT_g,
                                      ALU.mult).then_inc(b_read, 1)
                    dve.wait_ge(b_read, g + 1)
                    dve.tensor_reduce(mean_e[s][:, :], weighed[s][:, :, :], AX.X, ALU.add).then_inc(m_done, 1)
                    at_least(dve, o_ready, g - 1)
                    dve.wait_ge(m_done, g + 1)
                    dve.tensor_tensor(ecT[s][:, :, :], eT_g, mean_e[s][:, :].rearrange("p (b a) -> p b a", a=1)
                                      .broadcast_to([D, G, S]), ALU.mult).then_inc(ec_done, 1)
                u = t.back(1)
                if u.exists(GROUPS):
                    g = u.index()
                    first = g * G
                    x = st.xs[:, bass.ds(first, G), :]
                    at_least(dve, o_ready, g + 1)
                    dve.tensor_tensor(x, obank[u.phase(2)][0:S, :].rearrange("p (b d) -> p b d", b=G), x, ALU.add)\
                        .then_inc(o_read, 1)
                    dve.wait_ge(o_read, g + 1)
                    for b in range(G):
                        n = g * G + b
                        dve.bn_stats(st.stats[:, n, :], st.xs[:, n, :])

            run_steps(dve, step, 0, GROUPS, 2, 2, 1)


def feed_forward(nc, st, ins):
    I = 352
    QMAX = 127.0
    CUTS = [(0, 128), (128, 128), (256, 96)]
    J, G = len(CUTS), 4
    GROUPS = NB // G
    W = G * S
    with ExitStack() as ctx:
        sp = Space(nc, ctx, "ff")
        sb, sem = sp.sb, sp.sem
        e_all = sb("e_all", [S, NB, D])
        hT = sb("hT", [D, J, NB * S])
        upT, downT = sb("upT", [D, 2, I], BF16), sb("downT", [D, J, D], BF16)
        w_scale = sb("w_scale", [D, 2 * J])
        h_scale = sb("h_scale", [D, 2 * J])
        down_row = sb("down_row", [S, D])
        sig = sb("sig", [D, 2])
        inv_x, inv_h, round_up = sb("inv_x", [D, 1]), sb("inv_h", [D, 1]), sb("round_up", [D, 1])
        sx = sb("sx", [D, 2])
        hm = sb("hm", [D, GROUPS * J])
        ones = sb("ones", [D, D])
        one_row = sb("one_row", [1, D])

        def scales_from(dve, link, bank, which, scale, inverse):
            link(dve.tensor_scalar(scale, bank[:, 0:1], sig[:, which:which + 1], 1.0 / QMAX, ALU.mult, ALU.mult))
            link(dve.reciprocal(inverse, scale))

        with ExitStack() as part_ctx:
            psp = Space(nc, part_ctx, "fp")
            tmp, var, std = psp.sb("tmp", [S, NB]), psp.sb("var", [S, NB]), psp.sb("std", [S, NB])
            wraw = psp.sb("wraw", [D, 2 * J, D])
            draw = psp.sb("draw", [D, I])
            wq, dq = psp.sb("wq", [D, 2 * J, D], BF16), psp.sb("dq", [D, I], BF16)
            w_inv, d_scale, d_inv, diag = (psp.sb("w_inv", [D, 2 * J]), psp.sb("d_scale", [D, 1]), psp.sb("d_inv", [D, 1]),
                                           psp.sb("diag", [D, D]))
            clip = psp.sb("clip", [D, 2])
            em, emax, etop = psp.sb("em", [S, GROUPS]), psp.sb("emax", [S, 1]), psp.sb("etop", [1, 1])
            tbank = [psp.ps(f"tbank{i}", (128, 1024), BF16) for i in range(2)]
            row_bank, m_bank, top_bank = psp.ps("row_bank"), psp.ps("m_bank"), psp.ps("top_bank")
            w_in, moments, std_ready, chain, clip_done, wq_done, diag_done, t_ready, m_ready, m_read, top_ready, e_done = [
                psp.sem(n) for n in ("w_in", "moments", "std_ready", "chain", "clip_done", "wq_done", "diag_done",
                                     "t_ready", "m_ready", "m_read", "top_ready", "e_done")]
            block = part_ctx.enter_context(nc.Block())

            @block.sync
            def _(sync):
                for w, name in enumerate(("w_gate", "w_up")):
                    src = ins["L1_ffn_" + name]
                    sync.dma_start(wraw[:, J * w:J * w + 2, :], src[0:256, :].rearrange("(j p) n -> p j n", p=D)).then_inc(w_in, 16)
                    sync.dma_start(wraw[0:96, J * w + 2, :], src[256:I, :]).then_inc(w_in, 16)
                sync.dma_start(draw[:, :], ins["L1_ffn_w_down"]).then_inc(w_in, 16)
                for i, name in enumerate(("clip_x", "clip_down")):
                    sync.dma_start(clip[:, i:i + 1], ins["L1_ffn_" + name].rearrange("(a n) -> a n", a=1).broadcast_to([D, 1]))\
                        .then_inc(w_in, 16)

            @block.scalar
            def _(act):
                act.wait_ge(moments, 1)
                act.activation(std[:, :], var[:, :], ACT.Sqrt).then_inc(std_ready, 1)
                act.wait_ge(w_in, 16 * 7)
                act.activation(sig[:, :], clip[:, :], ACT.Exp, scale=-1.0).then_inc(clip_done, 1)

            @block.tensor
            def _(pe):
                pe.wait_ge(wq_done, 1)
                for w in range(2):
                    for j, (lo, size) in enumerate(CUTS):
                        i = pe.transpose(tbank[w][:, lo:lo + size], wq[0:size, J * w + j, :], st.ident_b[0:size, 0:size])
                i.then_inc(t_ready, 1)
                pe.wait_ge(t_ready, 1)
                for j, (lo, size) in enumerate(CUTS):
                    i = pe.transpose(tbank[1][0:size, 512 + j * D:512 + (j + 1) * D], dq[:, lo:lo + size], st.ident_b[:, :])
                i.then_inc(t_ready, 1)
                pe.wait_ge(diag_done, 1)
                pe.matmul(row_bank[0:S, 0:D], ones[:, 0:S], diag[:, :], start=True, stop=True).then_inc(t_ready, 1)
                pe.wait_ge(e_done, GROUPS + 1)
                pe.transpose(m_bank[0:1, 0:S], emax[:, :], st.ident[0:S, 0:S]).then_inc(m_ready, 1)
                pe.wait_ge(m_read, 1)
                pe.matmul(top_bank[:, 0:1], one_row[:, :], etop[:, :], start=True, stop=True).then_inc(top_ready, 1)

            @block.vector
            def _(dve):
                link = Chain(dve, chain)
                dve.memset(ones[:, :], 1.0)
                dve.memset(one_row[:, :], 1.0)
                dve.memset(hm[:, :], 0.0)
                dve.memset(round_up[:, :], ROUND)
                link(dve.memset(wraw[96:D, 2, :], 1.0))
                link(dve.memset(wraw[96:D, 5, :], 1.0))
                layernorm_moments(dve, link, st, tmp, var)
                dve.tensor_scalar(var[:, :], var[:, :], EPS, None, ALU.add).then_inc(moments, 1)
                dve.wait_ge(std_ready, 1)
                link(dve.reciprocal(st.rstd[:, :], std[:, :]))
                for g in range(GROUPS):
                    for n in range(G * g, G * g + G):
                        i = dve.tensor_scalar(e_all[:, n, :], st.xs[:, n, :], st.mean[:, n:n + 1], st.rstd[:, n:n + 1],
                                              ALU.subtract, ALU.mult)
                    link(i)
                    dve.tensor_reduce(em[:, g:g + 1], e_all[:, G * g:G * g + G, :], AX.XY, ALU.max,
                                      apply_absolute_value=True).then_inc(e_done, 1)
                dve.wait_ge(e_done, GROUPS)
                dve.tensor_reduce(emax[:, :], em[:, :], AX.X, ALU.max).then_inc(e_done, 1)
                dve.wait_ge(w_in, 16 * 7)
                dve.tensor_reduce(w_scale[:, :], wraw[:, :, :], AX.X, ALU.max, apply_absolute_value=True)
                link(dve.tensor_reduce(d_scale[:, :], draw[:, :], AX.X, ALU.max, apply_absolute_value=True))
                dve.tensor_scalar(w_scale[:, :], w_scale[:, :], 1.0 / QMAX, None, ALU.mult)
                link(dve.tensor_scalar(d_scale[:, :], d_scale[:, :], 1.0 / QMAX, None, ALU.mult))
                dve.reciprocal(w_inv[:, :], w_scale[:, :])
                link(dve.reciprocal(d_inv[:, :], d_scale[:, :]))
                for j in range(2 * J):
                    i = dve.tensor_scalar(wraw[:, j, :], wraw[:, j, :], w_inv[:, j:j + 1], ROUND, ALU.mult, ALU.add)
                link(dve.tensor_scalar(draw[:, :], draw[:, :], d_inv[:, 0:1], ROUND, ALU.mult, ALU.add))
                for v, _ in ((wraw[:, :, :], 0), (draw[:, :], 0)):
                    i = dve.tensor_scalar(v, v, ROUND + QMAX, ROUND - QMAX - 1.0, ALU.min, ALU.max)
                link(i)
                dve.tensor_scalar(wq[:, :, :], wraw[:, :, :], ROUND, None, ALU.subtract)
                dve.tensor_scalar(dq[:, :], draw[:, :], ROUND, None, ALU.subtract).then_inc(wq_done, 1)
                dve.tensor_scalar(diag[:, :], st.ident[:, :], d_scale[:, 0:1], None, ALU.mult).then_inc(diag_done, 1)
                dve.wait_ge(clip_done, 1)
                link(dve.tensor_scalar(sig[:, :], sig[:, :], 1.0, None, ALU.add))
                link(dve.reciprocal(sig[:, :], sig[:, :]))
                dve.wait_ge(t_ready, 3)
                dve.tensor_copy(upT[:, 0, :], tbank[0][:, 0:I])
                dve.tensor_copy(upT[:, 1, :], tbank[1][:, 0:I])
                for j, (lo, size) in enumerate(CUTS):
                    dve.tensor_copy(downT[0:size, j, :], tbank[1][0:size, 512 + j * D:512 + (j + 1) * D])
                link(dve.tensor_copy(down_row[:, :], row_bank[0:S, 0:D]))
                dve.wait_ge(m_ready, 1)
                dve.tensor_reduce(etop[:, :], m_bank[0:1, 0:S], AX.X, ALU.max).then_inc(m_read, 1)
                dve.wait_ge(top_ready, 1)
                scales_from(dve, link, top_bank, 0, sx[:, 0:1], inv_x[:, :])
                link(dve.tensor_scalar(h_scale[:, :], w_scale[:, :], sx[:, 0:1], None, ALU.mult))

        with ExitStack() as part_ctx:
            psp = Space(nc, part_ctx, "fu")
            whole = psp.sb("whole", [S, G * D])
            qx = psp.sb("qx", [S, G * D], BF16)
            qxT = [psp.sb(f"qxT{i}", [D, W], BF16) for i in range(2)]
            silu = [psp.sb(f"silu{i}", [D, W]) for i in range(2)]
            tbank = psp.ps("tbank", (128, 1024), BF16)
            gbank = [psp.ps(f"gbank{i}") for i in range(2)]
            ubank = [psp.ps(f"ubank{i}") for i in range(2)]
            (rounded, clipped, qx_ready, t_ready, t_read, g_ready, u_ready, g_read, h_made, h_top) = [
                psp.sem(n) for n in ("rounded", "clipped", "qx_ready", "t_ready", "t_read", "g_ready", "u_ready",
                                     "g_read", "h_made", "h_top")]
            gate = psp.sem("gate")
            block = part_ctx.enter_context(nc.Block())
            ITEMS, PER = GROUPS * J, 2 * J

            @block.scalar
            def _(act):
                def step(t):
                    c = t.back(-2 * J)
                    if t.phase(J) == 1 and c.exists(ITEMS):
                        g = c.index(J)
                        first = g * G
                        at_least(act, qx_ready, g)
                        act.activation(whole[:, :], e_all[:, bass.ds(first, G), :].rearrange("p b d -> p (b d)"),
                                       ACT.Identity, bias=round_up[0:S, 0:1], scale=inv_x[0:S, 0:1]).then_inc(rounded, 1)
                    if t.exists(ITEMS):
                        k, j = t.index(), t.phase(J)
                        size = CUTS[j][1]
                        at_least(act, g_ready, k + 1)
                        at_least(act, h_made, k - 1)
                        act.activation(silu[t.phase(2)][0:size, :], gbank[t.phase(2)][0:size, 0:W], ACT.Silu,
                                       scale=h_scale[0:size, j:j + 1]).then_inc(g_read, 1)
                    c = t.back(-J)
                    if t.phase(J) == 1 and c.exists(ITEMS):
                        g = c.index(J)
                        at_least(act, t_ready, g + 1)
                        at_least(act, u_ready, (g - 1) * J)
                        act.activation(qxT[c.phase(PER) // J][:, :], tbank[:, 0:W], ACT.Copy).then_inc(t_read, 1)

                run_steps(act, step, 2 * J, ITEMS, 0, PER, 1)

            @block.gpsimd
            def _(pool):
                def step(t):
                    c = t.back(-2 * J)
                    if t.phase(J) == 2 and c.exists(ITEMS):
                        g = c.index(J)
                        at_least(pool, clipped, g + 1)
                        at_least(pool, t_ready, g)
                        pool.sem_inc(gate, 1)
                        pool.tensor_scalar(qx[:, :], whole[:, :], -ROUND, None, ALU.add).then_inc(qx_ready, 1)

                run_steps(pool, step, 2 * J, ITEMS, 0, PER, 1)

            @block.tensor
            def _(pe):
                def step(t):
                    c = t.back(-J)
                    if t.phase(J) == 0 and c.exists(ITEMS):
                        g = c.index(J)
                        at_least(pe, qx_ready, g + 1)
                        at_least(pe, t_read, g)
                        for b in range(G):
                            i = pe.transpose(tbank[:, b * S:(b + 1) * S], qx[:, b * D:(b + 1) * D], st.ident_b[0:S, 0:S])
                        i.then_inc(t_ready, 1)
                    if t.exists(ITEMS):
                        k, g, j = t.index(), t.index(J), t.phase(J)
                        lo, size = CUTS[j]
                        at_least(pe, t_read, g + 1)
                        at_least(pe, h_made, k - 1)
                        at_least(pe, g_read, k - 1)
                        rhs = qxT[t.phase(PER) // J][:, :]
                        pe.matmul(gbank[t.phase(2)][0:size, 0:W], upT[:, 0, lo:lo + size], rhs, start=True, stop=True)\
                            .then_inc(g_ready, 1)
                        pe.matmul(ubank[t.phase(2)][0:size, 0:W], upT[:, 1, lo:lo + size], rhs, start=True, stop=True)\
                            .then_inc(u_ready, 1)

                run_steps(pe, step, J, ITEMS, 0, PER, 1)

            @block.vector
            def _(dve):
                def step(t):
                    c = t.back(-2 * J)
                    if t.phase(J) == 1 and c.exists(ITEMS):
                        g = c.index(J)
                        at_least(dve, rounded, g + 1)
                        dve.tensor_scalar(whole[:, :], whole[:, :], ROUND + QMAX, ROUND - QMAX - 1.0, ALU.min, ALU.max)\
                            .then_inc(clipped, 1)
                    if t.exists(ITEMS):
                        k, g, j = t.index(), t.index(J), t.phase(J)
                        size = CUTS[j][1]
                        at_least(dve, g_read, k + 1)
                        at_least(dve, u_ready, k + 1)
                        start = g * W
                        out = hT[0:size, j, bass.ds(start, W)]
                        dve.scalar_tensor_tensor(out, ubank[t.phase(2)][0:size, 0:W], h_scale[0:size, J + j:J + j + 1],
                                                 silu[t.phase(2)][0:size, :], ALU.mult, ALU.mult).then_inc(h_made, 1)
                        dve.wait_ge(h_made, k + 1)
                        dve.tensor_reduce(hm[0:size, bass.ds(k, 1)], out, AX.X, ALU.max, apply_absolute_value=True)\
                            .then_inc(h_top, 1)

                run_steps(dve, step, 2 * J, ITEMS, 0, PER, 1)

        with ExitStack() as part_ctx:
            psp = Space(nc, part_ctx, "fd")
            hmax, htop = psp.sb("hmax", [D, 1]), psp.sb("htop", [1, 1])
            whole = [psp.sb(f"whole{i}", [D, W]) for i in range(2)]
            qh = [psp.sb(f"qh{i}", [D, J, W], BF16) for i in range(2)]
            scaled = psp.sb("scaled", [S, G * D])
            m_bank, top_bank = psp.ps("m_bank"), psp.ps("top_bank")
            ybank = [psp.ps(f"ybank{i}") for i in range(2)]
            (chain, m_ready, m_read, hmax_done, top_ready, scales, rounded, clipped, qh_ready, y_ready, y_read, stored) = [
                psp.sem(n) for n in ("chain", "m_ready", "m_read", "hmax_done", "top_ready", "scales", "rounded", "clipped",
                                     "qh_ready", "y_ready", "y_read", "stored")]
            added = psp.sem("added")
            gate = psp.sem("gate")
            block = part_ctx.enter_context(nc.Block())
            ITEMS, PER = GROUPS * J, 2 * J

            @block.tensor
            def _(pe):
                pe.wait_ge(hmax_done, 1)
                pe.transpose(m_bank[0:1, 0:D], hmax[:, :], st.ident[:, :]).then_inc(m_ready, 1)
                pe.wait_ge(m_read, 1)
                pe.matmul(top_bank[:, 0:1], one_row[:, :], htop[:, :], start=True, stop=True).then_inc(top_ready, 1)

                def step(t):
                    u = t.back(3)
                    if u.phase(J) == 2 and u.exists(ITEMS):
                        g, s = u.index(J), u.phase(PER) // J
                        at_least(pe, qh_ready, J * (g + 1))
                        at_least(pe, y_read, g - 1)
                        for b in range(G):
                            for j, (lo, size) in enumerate(CUTS):
                                i = pe.matmul(ybank[s][0:S, b * D:(b + 1) * D], qh[s][0:size, j, b * S:(b + 1) * S],
                                              downT[0:size, j, :], start=(j == 0), stop=(j == J - 1))
                        i.then_inc(y_ready, 1)

                run_steps(pe, step, 0, ITEMS, 4, PER, 1)

            @block.scalar
            def _(act):
                act.wait_ge(scales, 1)

                def step(t):
                    if t.exists(ITEMS):
                        k, g, j = t.index(), t.index(J), t.phase(J)
                        size = CUTS[j][1]
                        start = g * W
                        at_least(act, qh_ready, k - 1)
                        act.activation(whole[t.phase(2)][0:size, :], hT[0:size, j, bass.ds(start, W)], ACT.Identity,
                                       bias=round_up[0:size, 0:1], scale=inv_h[0:size, 0:1]).then_inc(rounded, 1)

                run_steps(act, step, 0, ITEMS, 0, PER, 1)

            @block.gpsimd
            def _(pool):
                def step(t):
                    u = t.back(1)
                    if u.exists(ITEMS):
                        k, g, j, s = u.index(), u.index(J), u.phase(J), u.phase(PER) // J
                        size = CUTS[j][1]
                        at_least(pool, clipped, k + 1)
                        at_least(pool, y_ready, g - 1)
                        pool.sem_inc(gate, 1)
                        pool.tensor_scalar(qh[s][0:size, j, :], whole[u.phase(2)][0:size, :], -ROUND, None, ALU.add)\
                            .then_inc(qh_ready, 1)

                run_steps(pool, step, 0, ITEMS, 2, PER, 1)

            @block.vector
            def _(dve):
                link = Chain(dve, chain)
                dve.tensor_reduce(hmax[:, :], hm[:, :], AX.X, ALU.max).then_inc(hmax_done, 1)
                dve.wait_ge(m_ready, 1)
                dve.tensor_reduce(htop[:, :], m_bank[0:1, 0:D], AX.X, ALU.max).then_inc(m_read, 1)
                dve.wait_ge(top_ready, 1)
                scales_from(dve, link, top_bank, 1, sx[:, 1:2], inv_h[:, :])
                dve.tensor_scalar(down_row[:, :], down_row[:, :], sx[0:S, 1:2], None, ALU.mult).then_inc(scales, 1)
                dve.wait_ge(scales, 1)

                def step(t):
                    if t.exists(ITEMS):
                        k, j = t.index(), t.phase(J)
                        size = CUTS[j][1]
                        at_least(dve, rounded, k + 1)
                        v = whole[t.phase(2)][0:size, :]
                        dve.tensor_scalar(v, v, ROUND + QMAX, ROUND - QMAX - 1.0, ALU.min, ALU.max).then_inc(clipped, 1)
                    u = t.back(4)
                    if u.phase(J) == 2 and u.exists(ITEMS):
                        g, s = u.index(J), u.phase(PER) // J
                        at_least(dve, y_ready, g + 1)
                        at_least(dve, added, g)
                        dve.tensor_tensor(scaled[:, :].rearrange("p (b d) -> p b d", b=G),
                                          ybank[s][0:S, :].rearrange("p (b d) -> p b d", b=G),
                                          down_row[:, :].rearrange("p (a d) -> p a d", a=1).broadcast_to([S, G, D]),
                                          ALU.mult).then_inc(y_read, 1)
                        dve.wait_ge(y_read, g + 1)
                        first = g * G
                        x = st.xs[:, bass.ds(first, G), :]
                        dve.tensor_tensor(x, scaled[:, :].rearrange("p (b d) -> p b d", b=G), x, ALU.add).then_inc(added, 1)

                run_steps(dve, step, 0, ITEMS, 5, PER, 1)

            @block.sync
            def _(sync):
                with sync.Fori(0, GROUPS) as g:
                    first = g * G
                    sync.wait_ge(added, g + 1)
                    for b in range(G):
                        p = first + b
                        n = sync.value_load(st.order[0:1, bass.ds(p, 1)], min_val=0, max_val=NB - 1)
                        sync.dma_start(st.out[bass.ds(n, 1)].rearrange("b s d -> s b d"), st.xs[:, bass.ds(p, 1), :])\
                            .then_inc(stored, 16)
                sync.wait_ge(stored, 16 * NB)


class Stream:
    pass


def rank_sequences(nc, st, ins, causal32):
    with ExitStack() as ctx:
        sp = Space(nc, ctx, "rk")
        sb, sem = sp.sb, sp.sem
        mask8, mask32, far = sb("mask8", [NB, CTX], U8), sb("mask32", [NB, CTX]), sb("far", [NB, CTX])
        table = sb("table", [NB, NB + 2])
        reach, key, rank = sb("reach", [NB, 1]), sb("key", [NB, 1]), sb("rank", [NB, 1])
        diag, above, place, ones = [sb(n, [NB, NB]) for n in ("diag", "above", "place", "ones")]
        number = sb("number", [1, NB])
        bank = sp.ps("bank")
        mask_in, chain, keys_spread, row_ready, place_made, order_ready = [
            sem(n) for n in ("mask_in", "chain", "keys_spread", "row_ready", "place_made", "order_ready")]
        block = ctx.enter_context(nc.Block())

        @block.sync
        def _(sync):
            sync.dma_start(mask8[:, :], ins["mask_BxS2_bk0"]).then_inc(mask_in, 16)

        @block.scalar
        def _(act):
            for dst, name in ((far, "c_far"), (table, "c_table"), (st.ident, "c_ident"), (st.rotT, "c_rotT"),
                              (st.turn, "c_turn"), (st.headmask, "c_headmask"), (causal32, "c_causal")):
                act.dma_start(dst[:], ins[name]).then_inc(st.consts_in, 16)

        @block.tensor
        def _(pe):
            pe.wait_ge(keys_spread, 1)
            pe.matmul(bank[0:NB, 0:NB], ones[:, :], diag[:, :], start=True, stop=True).then_inc(row_ready, 1)
            pe.wait_ge(place_made, 1)
            pe.matmul(bank[0:1, 128:128 + NB], table[:, 0:1], place[:, :], start=True, stop=True)
            pe.matmul(bank[0:S, 256:256 + NB], reach[:, :].broadcast_to([NB, S]), place[:, :], start=True, stop=True)\
                .then_inc(order_ready, 1)

        @block.vector
        def _(dve):
            link = Chain(dve, chain)
            dve.memset(ones[:, :], 1.0)
            dve.wait_ge(mask_in, 16)
            link(dve.tensor_copy(mask32[:, :], mask8[:, :]))
            dve.wait_ge(st.consts_in, 16 * st.n_consts)
            link(dve.tensor_tensor(mask32[:, :], mask32[:, :], far[:, :], ALU.mult))
            link(dve.tensor_reduce(reach[:, :], mask32[:, :], AX.X, ALU.max))
            link(dve.tensor_scalar(key[:, :], reach[:, :], float(NB), None, ALU.mult))
            link(dve.tensor_tensor(key[:, :], key[:, :], table[:, 1:2], ALU.add))
            dve.tensor_scalar(diag[:, :], st.ident[0:NB, 0:NB], key[:, 0:1], None, ALU.mult).then_inc(keys_spread, 1)
            dve.tensor_copy(st.ident_b[:, :], st.ident[:, :])
            dve.tensor_copy(st.causal[:, :, :], causal32[:, :].rearrange("p (a k) -> p a k", a=1)
                            .broadcast_to([S, 4, S]))
            dve.wait_ge(row_ready, 1)
            link(dve.tensor_scalar(above[:, :], bank[0:NB, 0:NB], key[:, 0:1], None, ALU.is_gt))
            link(dve.tensor_reduce(rank[:, :], above[:, :], AX.X, ALU.add))
            dve.tensor_scalar(place[:, :], table[:, 2:NB + 2], rank[:, 0:1], None, ALU.is_equal).then_inc(place_made, 1)
            dve.wait_ge(order_ready, 1)
            dve.tensor_copy(st.reach[:, :], bank[0:S, 256:256 + NB])
            link(dve.tensor_copy(number[:, :], bank[0:1, 128:128 + NB]))
            link(dve.tensor_copy(st.order[:, :], number[:, :]))


def decoder(nc, ins, out, upto=6):
    with ExitStack() as ctx:
        sp = Space(nc, ctx, "all")
        st = Stream()
        st.xs = sp.sb("xs", [S, NB, D])
        st.stats = sp.sb("stats", [S, NB, 6])
        st.mean = sp.sb("mean", [S, NB])
        st.rstd = sp.sb("rstd", [S, NB])
        st.ident = sp.sb("ident", [D, D])
        st.rotT = sp.sb("rotT", [D, D])
        st.turn = sp.sb("turn", [D, 2, S])
        st.headmask = sp.sb("headmask", [D, D // 8])
        st.ident_b = sp.sb("ident_b", [D, D], BF16)
        st.causal = sp.sb("causal", [S, 4, S], BF16)
        st.consts_in = sp.sem("consts_in")
        st.x_in = [sp.sem(f"x_in{i}") for i in range(3)]
        st.out = out
        causal32 = sp.sb("causal32", [S, S])
        st.order = sp.sb("order", [1, NB], I32)
        st.reach = sp.sb("reach", [S, NB])
        st.n_consts = 7

        st.x = ins["x"]
        rank_sequences(nc, st, ins, causal32)

        if upto >= 1:
            attention(nc, st, "a0", True, {n: ins["L0_attn_" + n] for n in ("wq", "bq", "wk", "bk", "wv", "bv", "wo", "bo")})
        if upto >= 2:
            cross_attention(nc, st, ins)
        if upto >= 3:
            experts(nc, st, ins)
        if upto >= 4:
            attention(nc, st, "a1", False, {n: ins["L1_attn_" + n] for n in ("W_qkv", "b_qkv", "W_proj", "b_proj")})
        if upto >= 5:
            context_attention(nc, st, ins)
        if upto >= 6:
            feed_forward(nc, st, ins)
        if upto == 6:
            return
        stored = sp.sem("stored")
        with nc.Block() as block:
            @block.sync
            def _(sync):
                with sync.Fori(0, NB) as p:
                    n = sync.value_load(st.order[0:1, bass.ds(p, 1)], min_val=0, max_val=NB - 1)
                    sync.dma_start(out[bass.ds(n, 1)].rearrange("b s d -> s b d"), st.xs[:, bass.ds(p, 1), :])\
                        .then_inc(stored, 16)
                sync.wait_ge(stored, 16 * NB)


UPTO = 6


def _constants():
    hd = 8
    rot = np.zeros((D, D), np.float32)
    for o in range(D):
        d = o % hd
        if d < hd // 2:
            rot[o, o + hd // 2] = -1.0
        else:
            rot[o, o - hd // 2] = 1.0
    freq = (1.0 / np.float32(10000.0) ** (np.arange(0, hd, 2, dtype=np.float32) / np.float32(hd))).astype(np.float32)
    angle = np.arange(S, dtype=np.float32)[:, None] * freq[None, :]
    cos = np.repeat(np.cos(angle), 2, axis=-1).astype(np.float32)
    sin = np.repeat(np.sin(angle), 2, axis=-1).astype(np.float32)
    turn = np.stack([np.tile(cos.T, (D // hd, 1)), np.tile(sin.T, (D // hd, 1))], axis=1)
    headmask = (np.arange(D)[:, None] // hd == np.arange(D // hd)[None, :]).astype(np.float32)
    causal = np.where(np.arange(S)[None, :] <= np.arange(S)[:, None], 0.0, -BIG)
    number = np.arange(NB, dtype=np.float32)[:, None]
    return {
        "c_far": np.tile(CTX - np.arange(CTX, dtype=np.float32), (NB, 1)),
        "c_table": np.concatenate([number, NB - 1 - number, np.tile(number.T, (NB, 1))], axis=1),
        "c_ident": np.eye(D, dtype=np.float32),
        "c_rotT": np.ascontiguousarray(rot.T),
        "c_turn": np.ascontiguousarray(turn, dtype=np.float32),
        "c_headmask": headmask,
        "c_pref": np.tile(np.arange(8, 0, -1, dtype=np.float32), (S, 1)),
        "c_causal": causal.astype(np.float32),
    }


def kernel(**inputs):
    import concourse.bacc as bacc
    from concourse.bass_utils import run_bass_kernel_spmd

    nc = bacc.Bacc("TRN2", target_bir_lowering=False, num_devices=1)
    arrays, aps = {}, {}
    for name, value in {**inputs, **_constants()}.items():
        a = np.ascontiguousarray(value)
        arrays[f"in_{name}"] = a
        aps[name] = nc.dram_tensor(f"in_{name}", a.shape, mybir.dt.from_np(a.dtype), kind="ExternalInput").ap()
    out = nc.dram_tensor("out_0", (NB, S, D), F32, kind="ExternalOutput").ap()
    decoder(nc, aps, out, UPTO)
    r = run_bass_kernel_spmd(nc, [arrays], core_ids=[0])
    return r.results[0]["out_0"]
```

```python
from contextlib import ExitStack

import numpy as np

import concourse.bass as bass
from concourse import mybir

ALU = mybir.AluOpType
ACT = mybir.ActivationFunctionType
AX = mybir.AxisListType
F32 = mybir.dt.float32
BF16 = mybir.dt.bfloat16
I32 = mybir.dt.int32
U8 = mybir.dt.uint8

NB, S, D = 32, 100, 128
CTX = 1444
EPS = 1e-5
BIG = 3.0e38
ROUND = 1.5 * 2.0 ** 23


class Tick:

    def __init__(self, it, off, per):
        self.it, self.off, self.per = it, off, per

    def back(self, lag):
        return Tick(self.it, self.off - lag, self.per)

    def index(self, of=1):
        return self.it * (self.per // of) + self.off // of

    def exists(self, count):
        if not isinstance(self.it, int):
            return True
        return 0 <= self.it * self.per + self.off < count

    def phase(self, n):
        return self.off % n


def at_least(eng, sem, value):
    if isinstance(value, int) and value <= 0:
        return
    eng.wait_ge(sem, value)


def run_steps(eng, step, lead, items, drain, per, peel):
    for off in range(-lead, peel * per):
        step(Tick(0, off, per))
    last = items // per - 1
    with eng.Fori(peel, last) as it:
        for off in range(per):
            step(Tick(it, off, per))
    for off in range(per + drain):
        step(Tick(last, off, per))


class Space:

    def __init__(self, nc, ctx, tag):
        self.nc, self.ctx, self.tag = nc, ctx, tag
        self.sems = []
        ctx.callback(self.clear)

    def clear(self):
        if self.sems:
            self.nc.clear_and_free_semaphores(self.sems)
            self.nc.all_engine_barrier()

    def sb(self, name, shape, dt=F32):
        return self.ctx.enter_context(self.nc.sbuf_tensor(f"{self.tag}_{name}", shape, dt))

    def ps(self, name, shape=(128, 512), dt=F32):
        return self.ctx.enter_context(self.nc.psum_tensor(f"{self.tag}_{name}", list(shape), dt))

    def sem(self, name):
        self.sems.append(self.nc.alloc_semaphore(f"{self.tag}_{name}"))
        return self.sems[-1]


class Chain:

    def __init__(self, eng, sem):
        self.eng, self.sem, self.count = eng, sem, 0

    def __call__(self, ins):
        self.count += 1
        ins.then_inc(self.sem, 1)
        self.eng.wait_ge(self.sem, self.count)


def layernorm_moments(dve, link, st, tmp, var):
    link(dve.tensor_tensor(st.mean[:, :], st.stats[:, :, 1], st.stats[:, :, 4], ALU.add))
    link(dve.tensor_scalar(st.mean[:, :], st.mean[:, :], 0.5, None, ALU.mult))
    link(dve.tensor_tensor(tmp[:, :], st.stats[:, :, 1], st.mean[:, :], ALU.subtract))
    link(dve.tensor_tensor(tmp[:, :], tmp[:, :], tmp[:, :], ALU.mult))
    link(dve.tensor_tensor(var[:, :], st.stats[:, :, 2], st.stats[:, :, 5], ALU.add))
    link(dve.scalar_tensor_tensor(var[:, :], var[:, :], 1.0 / D, tmp[:, :], ALU.mult, ALU.add))


def attention(nc, st, tag, rotary, wts):
    H, HD, HG = 16, 8, 4
    GROUPS = H // HG
    ITEMS = NB * GROUPS
    SCALE = float(HD) ** -0.5
    PER = 2 * GROUPS
    PLACES = ((0, 10), (10, 20), (20, NB))
    with ExitStack() as ctx:
        sp = Space(nc, ctx, tag)
        sb, ps, sem = sp.sb, sp.ps, sp.sem
        tmp, var, std = sb("tmp", [S, NB]), sb("var", [S, NB]), sb("std", [S, NB])
        nproj = 4 if rotary else 2
        wproj = sb("wproj", [D, nproj, D])
        wv, wo = sb("wv", [D, D]), sb("wo", [D, D])
        wraw = sb("wraw", [D, 4, D])
        bcol = sb("bcol", [D, 8])
        brow = sb("brow", [S, D])
        bias_qk = sb("bias_qk", [D, 2, S])
        rowbias = sb("rowbias", [S, D])
        xn = sb("xn", [S, D])
        xnT = [sb(f"xnT{i}", [D, S]) for i in range(2)]
        turned = sb("turned", [D, 4, S])
        qk = [sb(f"qk{i}", [D, 2, S]) for i in range(2)]
        kblk = [sb(f"kblk{i}", [D, H, S]) for i in range(2)]
        ROW, HALF = S, H // 2
        vone = [sb(f"vone{i}", [D, H, ROW]) for i in range(2)]
        probs = [sb(f"probs{i}", [S, HG, S]) for i in range(4)]
        probsT = [sb(f"probsT{i}", [D, HG, S]) for i in range(2)]
        top = sb("top", [S, 4, HG])
        rsum = sb("rsum", [S, H])
        heads = [sb(f"heads{i}", [S, H, HD]) for i in range(2)]
        headsT = sb("headsT", [D, S])
        scores = [ps(f"scores{i}") for i in range(2)]
        pT = [ps(f"pT{i}") for i in range(2)]
        outp = [ps(f"outp{i}") for i in range(2)]
        front, back = ps("front"), ps("back")

        (weights_in, moments, std_ready, rstd_ready, chain, setup_pe, setup_read, setup_done, ones_set,
         ln_done, xT_ready, xnT_ready, proj_ready, proj_read, v_ready, v_read, sum_made, biased, kq_ready,
         s_ready, max_done, shifted, exp_done, pT_ready, pT_read, pv_done,
         rsum_done, heads_done, hT_ready, hT_read, y_ready, added, bias_added) = [sem(n) for n in (
            "weights_in", "moments", "std_ready", "rstd_ready", "chain", "setup_pe", "setup_read", "setup_done",
            "ones_set", "ln_done", "xT_ready", "xnT_ready", "proj_ready", "proj_read", "v_ready", "v_read",
            "sum_made", "biased", "kq_ready",
            "s_ready", "max_done", "shifted", "exp_done", "pT_ready", "pT_read", "pv_done",
            "rsum_done", "heads_done", "hT_ready", "hT_read", "y_ready", "added", "bias_added")]

        def v_places(v, half, lo, hi):
            flat = v[:, :, :].rearrange("p h e -> p (h e)")[:, half * HALF * ROW:(half + 1) * HALF * ROW]
            step = ROW + HD + 1
            return bass.AP(flat.tensor, flat.offset + lo, [list(flat.ap[0]), [step, HALF], [1, hi - lo]])

        def sv(t):
            return scores[t.phase(2)][0:S, 0:HG * S].rearrange("p (h k) -> p h k", h=HG)

        n_weights = 8 if rotary else 7
        block = ctx.enter_context(nc.Block())

        def load_places(eng, part):
            first, past = PLACES[part]
            with eng.Fori(first // 2, past // 2) as it:
                for b in range(2):
                    p = it * 2 + b
                    n = eng.value_load(st.order[0:1, bass.ds(p, 1)], min_val=0, max_val=NB - 1)
                    eng.dma_start(st.xs[:, bass.ds(p, 1), :], st.x[bass.ds(n, 1)].rearrange("b s d -> s b d"))\
                        .then_inc(st.x_in[part], 16)

        @block.sync
        def _(sync):
            if rotary:
                for i, name in enumerate(("wq", "wk", "wv", "wo")):
                    sync.dma_start(wraw[:, i, :], wts[name]).then_inc(weights_in, 16)
                for i, name in enumerate(("bq", "bk", "bv")):
                    sync.dma_start(bcol[:, i:i + 1], wts[name].rearrange("(p a) -> p a", a=1)).then_inc(weights_in, 16)
                sync.dma_start(brow[:, :], wts["bo"].rearrange("(a n) -> a n", a=1).broadcast_to([S, D]))\
                    .then_inc(weights_in, 16)
            else:
                sync.dma_start(wproj[:, :, :], wts["W_qkv"][:, 0:2 * D].rearrange("p (w n) -> p w n", w=2))\
                    .then_inc(weights_in, 16)
                sync.dma_start(wv[:, :], wts["W_qkv"][:, 2 * D:3 * D]).then_inc(weights_in, 16)
                sync.dma_start(wo[:, :], wts["W_proj"]).then_inc(weights_in, 16)
                for i in range(3):
                    sync.dma_start(bcol[:, i:i + 1], wts["b_qkv"][i * D:(i + 1) * D].rearrange("(p a) -> p a", a=1))\
                        .then_inc(weights_in, 16)
                sync.dma_start(brow[:, :], wts["b_proj"].rearrange("(a n) -> a n", a=1).broadcast_to([S, D]))\
                    .then_inc(weights_in, 16)
            if tag == "a0":
                load_places(sync, 0)

        @block.tensor
        def _(pe):
            pe.wait_ge(weights_in, 16 * n_weights)
            pe.wait_ge(st.consts_in, 16 * st.n_consts)
            if rotary:
                for i in range(4):
                    pe.transpose(scores[0][:, i * D:(i + 1) * D], wraw[:, i, :], st.ident[:, :])
                for i in range(2):
                    pe.matmul(scores[1][:, i * D:(i + 1) * D], wraw[:, i, :], st.rotT[:, :], start=True, stop=True)
                pe.matmul(pT[0][:, 0:2], st.rotT[:, :], bcol[:, 0:2], start=True, stop=True).then_inc(setup_pe, 1)
                pe.wait_ge(setup_read, 1)
            pe.matmul(pT[1][0:S, 0:D], bcol[:, 2:3].broadcast_to([D, S]), wo[:, :], start=True, stop=True)\
                .then_inc(setup_pe, 1)

            def step(t):
                c = t.back(-GROUPS)
                if t.phase(GROUPS) == 0 and c.exists(ITEMS):
                    n = c.index(GROUPS)
                    at_least(pe, ln_done, n + 1)
                    at_least(pe, v_read, n)
                    pe.transpose(front[:, 0:S], xn[:, :], st.ident[0:S, 0:S]).then_inc(xT_ready, 1)
                if t.phase(GROUPS) == 1 and c.exists(ITEMS):
                    n = c.index(GROUPS)
                    at_least(pe, xnT_ready, n + 1)
                    for j in range(nproj):
                        ins = pe.matmul(front[:, j * S:(j + 1) * S], wproj[:, j, :], xnT[c.phase(PER) // GROUPS][:, :],
                                        start=True, stop=True)
                    ins.then_inc(proj_ready, 1)
                if t.exists(ITEMS):
                    k, n, g = t.index(), t.index(GROUPS), t.phase(GROUPS)
                    slot = t.phase(PER) // GROUPS
                    at_least(pe, kq_ready, n + 1)
                    at_least(pe, shifted, k - 1)
                    if not rotary:
                        pe.matmul(scores[t.phase(2)][0:S, 0:HG * S], st.ident_b[0:S, 0:S],
                                  st.causal[:, :, :], start=True, stop=False)
                    pe.matmul(scores[t.phase(2)][0:S, 0:HG * S], qk[slot][:, 0, :],
                              kblk[slot][:, HG * g:HG * g + HG, :], start=rotary, stop=True).then_inc(s_ready, 1)
                u = t.back(2)
                if u.exists(ITEMS):
                    k = u.index()
                    at_least(pe, exp_done, k + 1)
                    at_least(pe, pT_read, k - 1)
                    for h in range(HG):
                        ins = pe.transpose(pT[u.phase(2)][0:S, h * S:(h + 1) * S], probs[u.phase(4)][:, h, :],
                                           st.ident[0:S, 0:S])
                    ins.then_inc(pT_ready, 1)
                u = t.back(3)
                if u.exists(ITEMS):
                    k, n, g = u.index(), u.index(GROUPS), u.phase(GROUPS)
                    slot = u.phase(PER) // GROUPS
                    at_least(pe, pT_read, k + 1)
                    at_least(pe, v_read, n + 1)
                    if g == 0:
                        at_least(pe, heads_done, n - 1)
                    half = g // 2
                    for h in range(HG):
                        hh = HG * g + h
                        ins = pe.matmul(outp[slot][0:S, half * ROW:(half + 1) * ROW], probsT[u.phase(2)][:, h, :],
                                        vone[slot][:, hh, :], start=(hh % HALF == 0), stop=(hh % HALF == HALF - 1))
                    ins.then_inc(pv_done, 1)
                if t.phase(GROUPS) == 2 and c.exists(ITEMS):
                    n = c.index(GROUPS)
                    at_least(pe, proj_read, n + 1)
                    pe.matmul(front[0:S, 0:D], xnT[c.phase(PER) // GROUPS][:, :], wv[:, :], start=True, stop=True)\
                        .then_inc(v_ready, 1)
                u = t.back(8)
                if u.phase(GROUPS) == 0 and u.exists(ITEMS):
                    n = u.index(GROUPS)
                    at_least(pe, heads_done, n + 1)
                    at_least(pe, added, n)
                    pe.transpose(back[:, 0:S], heads[u.phase(PER) // GROUPS][:, :, :].rearrange("p h d -> p (h d)"),
                                 st.ident[0:S, 0:S]).then_inc(hT_ready, 1)
                u = t.back(10)
                if u.phase(GROUPS) == 0 and u.exists(ITEMS):
                    n = u.index(GROUPS)
                    at_least(pe, hT_read, n + 1)
                    pe.matmul(back[0:S, 128:128 + D], headsT[:, :], wo[:, :], start=True, stop=True)\
                        .then_inc(y_ready, 1)

            run_steps(pe, step, GROUPS, ITEMS, 12, PER, 2)

        @block.scalar
        def _(act):
            if tag == "a0":
                load_places(act, 1)
            act.wait_ge(moments, 1)
            act.wait_ge(ones_set, 1)
            act.activation(std[:, :], var[:, :], ACT.Sqrt).then_inc(std_ready, 1)

            def step(t):
                c = t.back(-GROUPS)
                if t.phase(GROUPS) == 0 and c.exists(ITEMS):
                    n = c.index(GROUPS)
                    at_least(act, xT_ready, n + 1)
                    at_least(act, v_ready, n - 1)
                    act.activation(xnT[c.phase(PER) // GROUPS][:, :], front[:, 0:S], ACT.Copy).then_inc(xnT_ready, 1)
                if not rotary and t.phase(GROUPS) == 1 and c.exists(ITEMS):
                    n, slot = c.index(GROUPS), c.phase(PER) // GROUPS
                    at_least(act, proj_ready, n + 1)
                    at_least(act, s_ready, (n - 1) * GROUPS)
                    for j in range(2):
                        ins = act.activation(qk[slot][:, j, :], front[:, j * S:(j + 1) * S], ACT.Identity,
                                             bias=bcol[:, j:j + 1])
                    ins.then_inc(proj_read, 1)
                if t.phase(GROUPS) == 3 and c.exists(ITEMS):
                    n, slot = c.index(GROUPS), c.phase(PER) // GROUPS
                    at_least(act, v_ready, n + 1)
                    at_least(act, pv_done, (n - 1) * GROUPS)
                    for half in range(2):
                        ins = act.activation(v_places(vone[slot], half, 0, HD)[0:S], front[0:S, half * 64:half * 64 + 64]
                                             .rearrange("p (h d) -> p h d", h=HALF), ACT.Copy)
                    ins.then_inc(v_read, 1)
                u = t.back(2)
                if u.exists(ITEMS):
                    k = u.index()
                    at_least(act, pT_ready, k + 1)
                    at_least(act, pv_done, k - 1)
                    act.activation(probsT[u.phase(2)][0:S, :, :], pT[u.phase(2)][0:S, 0:HG * S]
                                   .rearrange("p (h k) -> p h k", h=HG), ACT.Copy).then_inc(pT_read, 1)
                if t.exists(ITEMS):
                    k = t.index()
                    at_least(act, shifted, k + 1)
                    p = probs[t.phase(4)][0:S, :, :]
                    act.activation(p, p, ACT.Exp, scale=SCALE).then_inc(exp_done, 1)
                u = t.back(9)
                if u.phase(GROUPS) == 0 and u.exists(ITEMS):
                    n = u.index(GROUPS)
                    at_least(act, hT_ready, n + 1)
                    at_least(act, y_ready, n)
                    act.activation(headsT[:, :], back[:, 0:S], ACT.Copy).then_inc(hT_read, 1)

            run_steps(act, step, GROUPS, ITEMS, 12, PER, 2)

        @block.vector
        def _(dve):
            link = Chain(dve, chain)
            for p in probsT:
                dve.memset(p[96:D, :, :], 0.0)
            for v in vone:
                link(dve.memset(v[:, :, :], 0.0))
                for half in range(2):
                    ins = dve.memset(v_places(v, half, HD, HD + 1)[0:S], 1.0)
            ins.then_inc(ones_set, 1)
            if tag == "a0":
                for part in (2, 0, 1):
                    first, past = PLACES[part]
                    dve.wait_ge(st.x_in[part], 16 * (past - first))
                    for n in range(first, past):
                        ins = dve.bn_stats(st.stats[:, n, :], st.xs[:, n, :])
                link(ins)
            layernorm_moments(dve, link, st, tmp, var)
            dve.tensor_scalar(var[:, :], var[:, :], EPS, None, ALU.add).then_inc(moments, 1)
            dve.wait_ge(std_ready, 1)
            dve.reciprocal(st.rstd[:, :], std[:, :]).then_inc(rstd_ready, 1)
            dve.wait_ge(rstd_ready, 1)
            if rotary:
                dve.wait_ge(setup_pe, 1)
                dve.tensor_copy(bcol[:, 3:5], pT[0][:, 0:2])
                for i in range(2):
                    dve.tensor_copy(wproj[:, 2 * i, :], scores[0][:, i * D:(i + 1) * D])
                    dve.tensor_copy(wproj[:, 2 * i + 1, :], scores[1][:, i * D:(i + 1) * D])
                dve.tensor_copy(wv[:, :], scores[0][:, 2 * D:3 * D])
                link(dve.tensor_copy(wo[:, :], scores[0][:, 3 * D:4 * D]))
                for i in range(2):
                    link(dve.tensor_scalar(bias_qk[:, i, :], st.turn[:, 0, :], bcol[:, i:i + 1], None, ALU.mult))
                    link(dve.scalar_tensor_tensor(bias_qk[:, i, :], st.turn[:, 1, :], bcol[:, 3 + i:4 + i],
                                                  bias_qk[:, i, :], ALU.mult, ALU.add))
                dve.tensor_copy(std[:, 0:1], std[:, 0:1]).then_inc(setup_read, 1)
            dve.wait_ge(setup_pe, 2 if rotary else 1)
            dve.wait_ge(weights_in, 16 * n_weights)
            dve.tensor_tensor(rowbias[:, :], pT[1][0:S, 0:D], brow[:, :], ALU.add).then_inc(setup_done, 1)

            def step(t):
                c = t.back(-2 * GROUPS)
                if t.phase(GROUPS) == 3 and c.exists(ITEMS):
                    n = c.index(GROUPS)
                    at_least(dve, xT_ready, n)
                    dve.tensor_scalar(xn[:, :], st.xs[:, n, :], st.mean[:, bass.ds(n, 1)], st.rstd[:, bass.ds(n, 1)],
                                      ALU.subtract, ALU.mult).then_inc(ln_done, 1)
                c = t.back(-GROUPS)
                if rotary and t.phase(GROUPS) == 1 and c.exists(ITEMS):
                    n = c.index(GROUPS)
                    at_least(dve, proj_ready, n + 1)
                    at_least(dve, sum_made, n)
                    for h in range(2):
                        ins = dve.tensor_tensor(turned[:, 2 * h:2 * h + 2, :],
                                                front[:, 2 * h * S:(2 * h + 2) * S].rearrange("p (w k) -> p w k", w=2),
                                                st.turn[:, :, :], ALU.mult)
                    ins.then_inc(proj_read, 1)
                if t.exists(ITEMS):
                    k = t.index()
                    at_least(dve, s_ready, k + 1)
                    m = top[:, t.phase(4), :]
                    dve.tensor_reduce(m, sv(t), AX.X, ALU.max).then_inc(max_done, 1)
                    at_least(dve, pT_ready, k - 3)
                    dve.wait_ge(max_done, k + 1)
                    dve.tensor_tensor(probs[t.phase(4)][0:S, :, :], sv(t), m.rearrange("p (h a) -> p h a", a=1)
                                      .broadcast_to([S, HG, S]), ALU.subtract).then_inc(shifted, 1)
                u = t.back(7)
                if u.phase(GROUPS) == 0 and u.exists(ITEMS):
                    n, slot = u.index(GROUPS), u.phase(PER) // GROUPS
                    o = outp[slot][0:S, 0:2 * ROW].rearrange("p (w r) -> p w r", w=2)[:, :, 0:HALF * (HD + 1)]\
                        .rearrange("p w (h e) -> p w h e", h=HALF)
                    at_least(dve, pv_done, GROUPS * (n + 1))
                    dve.reciprocal(rsum[:, :].rearrange("p (w h a) -> p w h a", w=2, a=1), o[:, :, :, HD:HD + 1])\
                        .then_inc(rsum_done, 1)
                    at_least(dve, hT_ready, n - 1)
                    dve.wait_ge(rsum_done, n + 1)
                    dve.tensor_tensor(heads[slot][:, :, :].rearrange("p (w h) d -> p w h d", w=2), o[:, :, :, 0:HD],
                                      rsum[:, :].rearrange("p (w h a) -> p w h a", w=2, a=1)
                                      .broadcast_to([S, 2, HALF, HD]), ALU.mult).then_inc(heads_done, 1)
                u = t.back(11)
                if u.phase(GROUPS) == 0 and u.exists(ITEMS):
                    n = u.index(GROUPS)
                    at_least(dve, y_ready, n + 1)
                    at_least(dve, bias_added, n + 1)
                    x = st.xs[:, n, :]
                    dve.tensor_tensor(x, back[0:S, 128:128 + D], x, ALU.add).then_inc(added, 1)
                    dve.wait_ge(added, n + 1)
                    dve.bn_stats(st.stats[:, n, :], x)

            run_steps(dve, step, 2 * GROUPS, ITEMS, 12, PER, 2)

        @block.gpsimd
        def _(pool):
            if tag == "a0":
                load_places(pool, 2)
            pool.wait_ge(setup_done, 1)

            def step(t):
                c = t.back(-GROUPS)
                if t.phase(GROUPS) == 1 and c.exists(ITEMS):
                    n, slot = c.index(GROUPS), c.phase(PER) // GROUPS
                    q = qk[slot]
                    at_least(pool, proj_read, n + 1)
                    at_least(pool, s_ready, (n - 1) * GROUPS)
                    if rotary:
                        tv = turned[:, :, :].rearrange("p (w c) k -> p w c k", c=2)
                        pool.tensor_tensor(q[:, :, :], tv[:, :, 0, :], tv[:, :, 1, :], ALU.add).then_inc(sum_made, 1)
                        pool.wait_ge(sum_made, n + 1)
                        pool.tensor_tensor(q[:, :, :], q[:, :, :], bias_qk[:, :, :], ALU.add).then_inc(biased, 1)
                        pool.wait_ge(biased, n + 1)
                    pool.tensor_tensor(kblk[slot][:, :, :], q[:, 1:2, :].broadcast_to([D, H, S]),
                                       st.headmask[:, :].rearrange("p (h a) -> p h a", a=1).broadcast_to([D, H, S]),
                                       ALU.mult).then_inc(kq_ready, 1)
                    at_least(pool, ln_done, n + 1)
                    x = st.xs[:, n, :]
                    pool.tensor_tensor(x, x, rowbias[:, :], ALU.add).then_inc(bias_added, 1)

            run_steps(pool, step, GROUPS, ITEMS, 0, PER, 2)


class KeyPlan:

    def __init__(self, first, part, chunks, tail, score_bufs, out_banks, start, count):
        self.start, self.count = start, count
        self.items = count * 8
        self.pool_divides = chunks == 1
        self.loads = 3 if tail else 2
        self.first, self.part, self.chunks, self.tail = first, part, chunks, tail
        self.score_bufs, self.out_banks = score_bufs, out_banks
        self.main = part * chunks
        self.keys = self.main + tail
        self.cuts = [(i * part, part) for i in range(chunks)] + ([(self.main, tail)] if tail else [])
        self.groups = [self.cuts[i:i + 4] for i in range(0, len(self.cuts), 4)]
        self.front_uses = 3 + len(self.groups)

    def front_use(self, t):
        ph, stride = t.phase(8), 2 if self.front_uses <= 4 else 1
        return ph // stride if ph % stride == 0 and ph // stride < self.front_uses else None


LATE_PLAN = KeyPlan(CTX - 420, 105, 4, 0, 2, 2, 0, NB // 2)
LAST_PLAN = KeyPlan(CTX - 105, 105, 1, 0, 2, 2, NB // 2, NB // 2)
WHOLE_PLAN = KeyPlan(0, 128, 11, 36, 1, 1, 0, NB)


def cross_attention(nc, st, ins):
    H, HD = 8, 64
    with ExitStack() as ctx:
        sp = Space(nc, ctx, "xa")
        sb = sp.sb
        tmp, var, std = sb("tmp", [S, NB]), sb("var", [S, NB]), sb("std", [S, NB])
        nanf = sb("nanf", [S, NB])
        wfold, ofold = sb("wfold", [D, H, D]), sb("ofold", [D, H, D])
        gamma, beta = sb("gamma", [D, 1]), sb("beta", [D, 1])
        flag = sb("flag", [1, 1], I32)
        with ExitStack() as setup_ctx:
            wsp = Space(nc, setup_ctx, "xs")
            wq, wkv, wout = wsp.sb("wq", [D, 4, D]), wsp.sb("wkv", [D, 8, D]), wsp.sb("wout", [D, 4, D])
            wT = wsp.sb("wT", [D, 12, D])
            kept = wsp.sb("kept", [S, NB])
            early = wsp.sb("early", [1, 2])
            bank = [wsp.ps(f"bank{i}") for i in range(7)]
            w_in, pe_done, dve_done, moments, std_ready, chain = [
                wsp.sem(n) for n in ("w_in", "pe_done", "dve_done", "moments",
                                     "std_ready", "chain")]
            block = setup_ctx.enter_context(nc.Block())

            @block.sync
            def _(sync):
                sync.dma_start(wq[:, :, :], ins["L0_xattn_Wq"].rearrange("p (j n) -> p j n", j=4)).then_inc(w_in, 16)
                sync.dma_start(wkv[:, :, :], ins["L0_xattn_Wkv"].rearrange("p (j n) -> p j n", j=8)).then_inc(w_in, 16)
                sync.dma_start(wout[:, :, :], ins["L0_xattn_Wout"].rearrange("(j p) n -> p j n", p=D)).then_inc(w_in, 16)
                sync.dma_start(gamma[:, :], ins["L0_xattn_ln_gamma"].rearrange("(p a) -> p a", a=1)).then_inc(w_in, 16)
                sync.dma_start(beta[:, :], ins["L0_xattn_ln_beta"].rearrange("(p a) -> p a", a=1)).then_inc(w_in, 16)

            @block.scalar
            def _(act):
                for i in range(2):
                    act.wait_ge(moments, i + 1)
                    act.activation(std[:, :], var[:, :], ACT.Sqrt).then_inc(std_ready, 1)

            @block.tensor
            def _(pe):
                pe.wait_ge(w_in, 16 * 5)
                for i in range(12):
                    w = wq[:, i, :] if i < 4 else wkv[:, i - 4, :]
                    ins_ = pe.transpose(bank[i // 4][:, (i % 4) * D:(i % 4 + 1) * D], w, st.ident[:, :])
                ins_.then_inc(pe_done, 1)
                pe.wait_ge(dve_done, 1)
                for h in range(H):
                    rows = slice(HD * (h % 2), HD * (h % 2) + HD)
                    pe.matmul(bank[3 + h % 2][:, (h // 2) * D:(h // 2 + 1) * D], wT[rows, h // 2, :], wT[rows, 4 + h // 2, :],
                              start=True, stop=True)
                for h in range(H):
                    rows = slice(HD * (h % 2), HD * (h % 2) + HD)
                    ins_ = pe.matmul(bank[5 + h % 2][:, (h // 2) * D:(h // 2 + 1) * D], wT[rows, 8 + h // 2, :],
                                     wout[rows, h // 2, :], start=True, stop=True)
                ins_.then_inc(pe_done, 1)

            @block.vector
            def _(dve):
                link = Chain(dve, chain)
                dve.wait_ge(pe_done, 1)
                for i in range(3):
                    c = dve.tensor_copy(wT[:, 4 * i:4 * i + 4, :], bank[i][:, :].rearrange("p (j n) -> p j n", j=4))
                c.then_inc(dve_done, 1)
                layernorm_moments(dve, link, st, tmp, var)
                link(dve.tensor_copy(tmp[:, :], var[:, :]))
                dve.tensor_scalar(var[:, :], var[:, :], EPS, None, ALU.add).then_inc(moments, 1)
                dve.wait_ge(std_ready, 1)
                link(dve.reciprocal(st.rstd[:, :], std[:, :]))
                link(dve.tensor_tensor(tmp[:, :], tmp[:, :], st.rstd[:, :], ALU.mult))
                link(dve.tensor_tensor(tmp[:, :], tmp[:, :], st.rstd[:, :], ALU.mult))
                dve.tensor_scalar(var[:, :], tmp[:, :], EPS, None, ALU.add).then_inc(moments, 1)
                dve.wait_ge(std_ready, 2)
                link(dve.reciprocal(tmp[:, :], std[:, :]))
                link(dve.tensor_tensor(st.rstd[:, :], st.rstd[:, :], tmp[:, :], ALU.mult))
                link(dve.tensor_scalar(kept[:, :], st.reach[:, :], 1.0, None, ALU.min))
                link(dve.reciprocal(tmp[:, :], kept[:, :]))
                link(dve.tensor_tensor(nanf[:, :], kept[:, :], tmp[:, :], ALU.mult))
                for i, plan in enumerate((LATE_PLAN, LAST_PLAN)):
                    link(dve.tensor_scalar(early[:, i:i + 1], st.reach[0:1, plan.start:plan.start + 1],
                                           float(CTX - plan.first), None, ALU.is_gt))
                link(dve.tensor_tensor(early[:, 0:1], early[:, 0:1], early[:, 1:2], ALU.max))
                link(dve.tensor_copy(flag[:, :], early[:, 0:1]))
                dve.wait_ge(pe_done, 2)
                for i in range(2):
                    dve.tensor_copy(wfold[:, i::2, :], bank[3 + i][:, :].rearrange("p (j n) -> p j n", j=4))
                    link(dve.tensor_copy(ofold[:, i::2, :], bank[5 + i][:, :].rearrange("p (j n) -> p j n", j=4)))

        cross_rows(nc, st, ins, "xa", wfold, ofold, gamma, beta, nanf, flag, (LATE_PLAN, WHOLE_PLAN))
        cross_rows(nc, st, ins, "xb", wfold, ofold, gamma, beta, nanf, flag, (LAST_PLAN, None))


def cross_rows(nc, st, ins, tag, wfold, ofold, gamma, beta, nanf, flag, plans):
    H, HD = 8, 64
    SCALE = float(HD) ** -0.5
    UN = 4
    PER = UN * H
    ctx_rows = ins["ctx_1024"]
    mask = ins["mask_BxS2_bk0"]
    with ExitStack() as ctx:
        sp = Space(nc, ctx, tag)
        sb, ps, sem = sp.sb, sp.ps, sp.sem
        xn = sb("xn", [S, D])
        xnT = sb("xnT", [D, S])
        qT = [sb(f"qT{i}", [D, H, S]) for i in range(2)]
        rows_in = [sb(f"rows{i}", [D, 12, D]) for i in range(UN)]
        ctxT = [sb(f"ctxT{i}", [D, CTX]) for i in range(2)]
        mask_rows = [sb(f"mask_rows{i}", [S, CTX], U8) for i in range(UN)]
        maskf = sb("maskf", [S, CTX])
        mask_add = [sb(f"mask_add{i}", [S, CTX]) for i in range(2)]
        probs = [sb(f"probs{i}", [S, CTX]) for i in range(4)]
        probsT = [sb(f"probsT{i}", [D, 12, S]) for i in range(2)]
        top, lowered, rowsum, inv = [sb(n, [S, 4]) for n in ("top", "lowered", "rowsum", "inv")]
        outT = [sb(f"outT{i}", [D, H, S]) for i in range(2)]
        psum = ps("psum", (128, 8 * 512))

        def bank_of(n):
            return psum[:, 512 * n:512 * (n + 1)]

        front, y_bank, pT_bank = bank_of(0), bank_of(1), [bank_of(2), bank_of(3)]

        names = ("rows_loaded0", "rows_loaded1", "rows_loaded2", "rows_loaded3", "ln_done", "front_ready",
                 "front_read", "mask_copied", "mask_made", "s_ready", "max_done", "shifted", "exp_done", "inv_done",
                 "normed", "pT_ready", "pT_read", "pv_done", "o_read", "y_ready", "added")
        sems = {n: sem(n) for n in names}
        gate = sem("gate")
        rows_loaded = [sems[f"rows_loaded{i}"] for i in range(UN)]
        (ln_done, front_ready, front_read, mask_copied, mask_made, s_ready, max_done, shifted, exp_done,
         inv_done, normed, pT_ready, pT_read, pv_done, o_read, y_ready, added) = [sems[n] for n in names[4:]]

        def score_bank(plan, t):
            if plan.score_bufs == 1:
                return psum[:, 4 * 512:7 * 512]
            return bank_of(4 + t.phase(2))

        def out_bank(plan, half):
            return bank_of(6 + half) if plan.out_banks == 2 else bank_of(7)

        block = ctx.enter_context(nc.Block())

        def sync_program(sync, plan):
            def load(place, slot):
                n = sync.value_load(st.order[0:1, bass.ds(plan.start + place, 1)], min_val=0, max_val=NB - 1)
                for lo, size, part in ((0, plan.main, plan.part), (plan.main, plan.tail, plan.tail)):
                    if size:
                        c0 = 0 if lo == 0 else plan.chunks
                        src = ctx_rows[bass.ds(n, 1), plan.first + lo:plan.first + lo + size, :]
                        sync.dma_start(rows_in[slot][0:part, c0:c0 + size // part, :],
                                       src.rearrange("a (p c) d -> (a p) c d", p=part)).then_inc(rows_loaded[slot], 16)
                sync.dma_start(mask_rows[slot][:, 0:plan.keys], mask[bass.ds(n, 1), plan.first:CTX]
                               .broadcast_to([S, plan.keys])).then_inc(rows_loaded[slot], 16)

            for n in range(UN):
                load(n, n)
            with sync.Fori(1, plan.count // UN) as it:
                for slot in range(UN):
                    n = it * UN + slot
                    sync.wait_ge(pv_done, (n - UN + 1) * H)
                    sync.wait_ge(mask_copied, n - UN + 1)
                    load(n, slot)

        def tensor_program(pe, plan):
            uses = plan.front_uses

            def step(t):
                c, ph = t.back(-H), plan.front_use(t)
                if c.exists(plan.items) and ph is not None:
                    n = c.index(H)
                    slot, slot4 = c.phase(2 * H) // H, c.phase(PER) // H
                    if ph == 0:
                        at_least(pe, ln_done, n + 1)
                        at_least(pe, front_read, uses * n)
                        pe.transpose(front[:, 0:S], xn[:, :], st.ident[0:S, 0:S]).then_inc(front_ready, 1)
                    elif ph <= 2:
                        at_least(pe, front_read, uses * n + ph)
                        for j in range(4):
                            i = pe.matmul(front[:, j * S:(j + 1) * S], wfold[:, 4 * (ph - 1) + j, :], xnT[:, :],
                                          start=True, stop=True)
                        i.then_inc(front_ready, 1)
                    else:
                        at_least(pe, front_read, uses * n + ph)
                        at_least(pe, rows_loaded[slot4], (t.back(-H).index(PER) + 1) * 16 * plan.loads)
                        base = plan.groups[ph - 3][0][0]
                        for j, (lo, size) in enumerate(plan.groups[ph - 3]):
                            i = pe.transpose(front[:, lo - base:lo - base + size],
                                             rows_in[slot4][0:size, 4 * (ph - 3) + j, :], st.ident[0:size, 0:size])
                        i.then_inc(front_ready, 1)
                if t.exists(plan.items):
                    k, n, h, slot = t.index(), t.index(H), t.phase(H), t.phase(2 * H) // H
                    at_least(pe, front_read, uses * (n + 1))
                    at_least(pe, shifted, k - plan.score_bufs + 1)
                    for lo in range(0, plan.keys, 512):
                        hi = min(lo + 512, plan.keys)
                        i = pe.matmul(score_bank(plan, t)[0:S, lo:hi], qT[slot][:, h, :], ctxT[slot][:, lo:hi],
                                      start=True, stop=True)
                    i.then_inc(s_ready, 1)
                u = t.back(3)
                if u.exists(plan.items):
                    k = u.index()
                    at_least(pe, normed, k + 1)
                    for g, cuts in enumerate(plan.groups):
                        n_before = k * len(plan.groups) + g
                        at_least(pe, pT_read, n_before - 1)
                        slot = (u.phase(2) * len(plan.groups) + g) % 2
                        for j, (lo, size) in enumerate(cuts):
                            i = pe.transpose(pT_bank[slot][0:size, j * S:(j + 1) * S],
                                             probs[u.phase(4)][:, lo:lo + size], st.ident[0:S, 0:S])
                        i.then_inc(pT_ready, 1)
                u = t.back(4)
                if u.exists(plan.items):
                    k, h, slot4 = u.index(), u.phase(H), u.phase(PER) // H
                    if h % 4 == 0:
                        at_least(pe, o_read, u.index(4) - plan.out_banks + 1)
                    for g, cuts in enumerate(plan.groups):
                        at_least(pe, pT_read, k * len(plan.groups) + g + 1)
                        for j, (lo, size) in enumerate(cuts):
                            c = 4 * g + j
                            i = pe.matmul(out_bank(plan, h // 4)[:, (h % 4) * S:(h % 4 + 1) * S],
                                          rows_in[slot4][0:size, c, :], probsT[u.phase(2)][0:size, c, :],
                                          start=(c == 0), stop=(c == len(plan.cuts) - 1))
                    i.then_inc(pv_done, 1)
                u = t.back(15)
                if u.phase(H) == 0 and u.exists(plan.items):
                    n, slot = u.index(H), u.phase(2 * H) // H
                    at_least(pe, o_read, 2 * (n + 1))
                    at_least(pe, added, n)
                    for h in range(H):
                        i = pe.matmul(y_bank[0:S, 0:D], outT[slot][:, h, :], ofold[:, h, :],
                                      start=(h == 0), stop=(h == H - 1))
                    i.then_inc(y_ready, 1)

            run_steps(pe, step, H, plan.items, 17, PER, 1)

        def scalar_program(act, plan):
            uses = plan.front_uses

            def step(t):
                c, ph = t.back(-H), plan.front_use(t)
                if c.exists(plan.items) and ph is not None:
                    n, slot = c.index(H), c.phase(2 * H) // H
                    at_least(act, front_ready, uses * n + ph + 1)
                    if ph == 0:
                        act.activation(xnT[:, :], front[:, 0:S], ACT.Identity, bias=beta[:, 0:1], scale=gamma[:, 0:1])\
                            .then_inc(front_read, 1)
                    elif ph <= 2:
                        act.activation(qT[slot][:, 4 * (ph - 1):4 * ph, :],
                                       front[:, 0:4 * S].rearrange("p (h q) -> p h q", h=4), ACT.Copy).then_inc(front_read, 1)
                    else:
                        base = plan.groups[ph - 3][0][0]
                        width = sum(size for _, size in plan.groups[ph - 3])
                        act.activation(ctxT[slot][:, base:base + width], front[:, 0:width], ACT.Copy).then_inc(front_read, 1)
                u = t.back(3)
                if u.exists(plan.items):
                    k = u.index()
                    at_least(act, pv_done, k - 1)
                    for g, cuts in enumerate(plan.groups):
                        at_least(act, pT_ready, k * len(plan.groups) + g + 1)
                        slot = (u.phase(2) * len(plan.groups) + g) % 2
                        full = [c for c in cuts if c[1] == plan.part]
                        n_full = len(full)
                        if n_full < len(cuts):
                            act.activation(probsT[u.phase(2)][0:plan.tail, 4 * g + n_full, :],
                                           pT_bank[slot][0:plan.tail, n_full * S:(n_full + 1) * S], ACT.Copy)
                        act.activation(probsT[u.phase(2)][0:plan.part, 4 * g:4 * g + n_full, :],
                                       pT_bank[slot][0:plan.part, 0:n_full * S].rearrange("p (c q) -> p c q", c=n_full),
                                       ACT.Copy).then_inc(pT_read, 1)
                if t.exists(plan.items):
                    k, s4 = t.index(), t.phase(4)
                    at_least(act, shifted, k + 1)
                    p = probs[s4][:, 0:plan.keys]
                    act.activation(p, p, ACT.Exp, bias=lowered[:, s4:s4 + 1], scale=SCALE,
                                   accum_out=rowsum[:, s4:s4 + 1]).then_inc(exp_done, 1)

            run_steps(act, step, H, plan.items, 4, PER, 1)

        def vector_program(dve, plan):
            uses = plan.front_uses

            def step(t):
                c = t.back(-2 * H)
                if t.phase(H) == H // 2 and c.exists(plan.items):
                    n = c.index(H)
                    at_least(dve, front_ready, uses * (n - 1) + 1)
                    p = plan.start + n
                    dve.tensor_scalar(xn[:, :], st.xs[:, p, :], st.mean[:, bass.ds(p, 1)], st.rstd[:, bass.ds(p, 1)],
                                      ALU.subtract, ALU.mult).then_inc(ln_done, 1)
                if t.exists(plan.items):
                    k, n, s4 = t.index(), t.index(H), t.phase(4)
                    at_least(dve, s_ready, k + 1)
                    at_least(dve, mask_made, n + 1)
                    at_least(dve, pT_ready, (k - 3) * len(plan.groups))
                    dve.sem_inc(gate, 1)
                    dve.tensor_tensor_reduce(probs[s4][:, 0:plan.keys], score_bank(plan, t)[0:S, 0:plan.keys],
                                             mask_add[t.phase(2 * H) // H][:, 0:plan.keys], 1.0, -BIG, ALU.add,
                                             ALU.max, top[:, s4:s4 + 1]).then_inc(max_done, 1)
                u = t.back(1)
                if u.exists(plan.items):
                    s4 = u.phase(4)
                    at_least(dve, exp_done, u.index() + 1)
                    dve.reciprocal(inv[:, s4:s4 + 1], rowsum[:, s4:s4 + 1]).then_inc(inv_done, 1)
                if t.exists(plan.items):
                    k, s4 = t.index(), t.phase(4)
                    at_least(dve, max_done, k + 1)
                    dve.tensor_scalar(lowered[:, s4:s4 + 1], top[:, s4:s4 + 1], -SCALE, None, ALU.mult)\
                        .then_inc(shifted, 1)
                if not plan.pool_divides and u.exists(plan.items):
                    s4 = u.phase(4)
                    p = probs[s4][:, 0:plan.keys]
                    at_least(dve, inv_done, u.index() + 1)
                    dve.tensor_scalar(p, p, inv[:, s4:s4 + 1], None, ALU.mult).then_inc(normed, 1)
                u = t.back(5)
                if u.phase(4) == 3 and u.exists(plan.items):
                    k, n, slot, half = u.index(), u.index(H), u.phase(2 * H) // H, u.phase(H) // 4
                    at_least(dve, pv_done, k + 1)
                    at_least(dve, y_ready, n - 1)
                    dve.tensor_copy(outT[slot][:, 4 * half:4 * half + 4, :], out_bank(plan, half)[:, 0:4 * S]
                                    .rearrange("p (h q) -> p h q", h=4)).then_inc(o_read, 1)
                u = t.back(16)
                if u.phase(H) == 0 and u.exists(plan.items):
                    n = u.index(H)
                    at_least(dve, y_ready, n + 1)
                    p = plan.start + n
                    x = st.xs[:, p, :]
                    dve.scalar_tensor_tensor(x, y_bank[0:S, 0:D], nanf[:, bass.ds(p, 1)], x, ALU.mult, ALU.add)\
                        .then_inc(added, 1)
                u = t.back(17)
                if u.phase(H) == 0 and u.exists(plan.items):
                    n = u.index(H)
                    p = plan.start + n
                    at_least(dve, added, n + 1)
                    dve.bn_stats(st.stats[:, p, :], st.xs[:, p, :])

            run_steps(dve, step, 2 * H, plan.items, 17, PER, 1)

        def pool_program(pool, plan):
            def step(t):
                c = t.back(-H)
                if t.phase(H) == 0 and c.exists(plan.items):
                    n, slot = c.index(H), c.phase(2 * H) // H
                    slot4 = c.phase(PER) // H
                    rows = mask_rows[slot4]
                    at_least(pool, rows_loaded[slot4], (t.back(-H).index(PER) + 1) * 16 * plan.loads)
                    at_least(pool, mask_made, n)
                    pool.sem_inc(gate, 1)
                    i = pool.tensor_copy(maskf[:, 0:plan.main].rearrange("p (c r) -> p c r", c=plan.chunks),
                                         rows[:, 0:plan.main].rearrange("p (r c) -> p c r", c=plan.chunks))
                    if plan.tail:
                        i = pool.tensor_copy(maskf[:, plan.main:plan.keys], rows[:, plan.main:plan.keys])
                    i.then_inc(mask_copied, 1)
                    at_least(pool, shifted, (n - 1) * H)
                    pool.wait_ge(mask_copied, n + 1)
                    pool.sem_inc(gate, 1)
                    pool.tensor_scalar(mask_add[slot][:, 0:plan.keys], maskf[:, 0:plan.keys], BIG, -BIG,
                                       ALU.mult, ALU.add).then_inc(mask_made, 1)
                u = t.back(1)
                if plan.pool_divides and u.exists(plan.items):
                    s4 = u.phase(4)
                    p = probs[s4][:, 0:plan.keys]
                    at_least(pool, inv_done, u.index() + 1)
                    pool.sem_inc(gate, 1)
                    pool.tensor_scalar(p, p, inv[:, s4:s4 + 1], None, ALU.mult).then_inc(normed, 1)

            run_steps(pool, step, H, plan.items, 2, PER, 1)

        def late_or_whole(eng, program):
            late, whole = plans
            early_kept = eng.value_load(flag[0:1, 0:1], min_val=0, max_val=1)
            with eng.If(early_kept == 0):
                program(eng, late)
            if whole:
                with eng.Else():
                    program(eng, whole)

        @block.sync
        def _(sync):
            late_or_whole(sync, sync_program)

        @block.tensor
        def _(pe):
            late_or_whole(pe, tensor_program)

        @block.scalar
        def _(act):
            late_or_whole(act, scalar_program)

        @block.vector
        def _(dve):
            late_or_whole(dve, vector_program)

        @block.gpsimd
        def _(pool):
            late_or_whole(pool, pool_program)


def experts(nc, st, ins):
    E, F, FQ = 8, 512, 4
    TILE = D
    MOST = NB * S // TILE
    TILES = (NB * S + E * (TILE - 1)) // TILE
    G = 4
    with ExitStack() as ctx:
        sp = Space(nc, ctx, "ex")
        sb, sem = sp.sb, sp.sem
        w1, w2 = sb("w1", [D, E * F]), sb("w2", [D, E, FQ, D])
        b1row, b2row = sb("b1row", [TILE, E * F]), sb("b2row", [TILE, E * D])
        gate = sb("gate", [S, NB])
        tile_expert = sb("tile_expert", [1, TILES], I32)
        w_in, scattered = sem("w_in"), sem("scattered")
        routed = nc.dram_tensor("routed", (TILES * TILE, D + 1), F32, kind="Internal").ap()
        answers = nc.dram_tensor("answers", (NB * S + TILES * TILE, D), F32, kind="Internal").ap()

        with ExitStack() as route_ctx:
            rsp = Space(nc, route_ctx, "er")
            tmp, var, std = rsp.sb("tmp", [S, NB]), rsp.sb("var", [S, NB]), rsp.sb("std", [S, NB])
            wr, brow, pref = rsp.sb("wr", [D, E]), rsp.sb("brow", [S, E]), rsp.sb("pref", [S, E])
            logits, expo, pick = [rsp.sb(n, [S, NB, E]) for n in ("logits", "expo", "pick")]
            sums = [rsp.sb(f"sums{i}", [S, NB, E]) for i in range(2)]
            before = rsp.sb("before", [S, S])
            ones = rsp.sb("ones", [S, S])
            numbers = rsp.sb("numbers", [S, TILES + MOST])
            fills = rsp.sb("fills", [S, E, MOST])
            last, used, base = [rsp.sb(n, [S, E]) for n in ("last", "used", "base")]
            ends = [rsp.sb(f"ends{i}", [S, E]) for i in range(2)]
            past = rsp.sb("past", [1, TILES, E])
            owner = rsp.sb("owner", [1, TILES])
            rowf, row = rsp.sb("rowf", [S, NB]), rsp.sb("row", [S, NB], I32)
            spare_rows = rsp.sb("spare_rows", [TILE, TILES, D + 1])
            spare = rsp.sb("spare", [TILE, TILES])
            best, total = rsp.sb("best", [S, NB]), rsp.sb("total", [S, NB])
            xn = rsp.sb("xn", [S, NB, D + 1])
            token = rsp.sb("token", [S, NB])
            xn_now = [rsp.sb(f"xn_now{i}", [S, D]) for i in range(4)]
            xnTs = [rsp.sb(f"xnTs{i}", [D, S]) for i in range(2)]
            turned = [rsp.ps(f"turned{i}") for i in range(2)]
            lg = [rsp.ps(f"lg{i}") for i in range(2)]
            counts = rsp.ps("counts")
            (r_in, moments, std_ready, chain, ln_done, xT_ready, xT_read, lg_ready, lg_read, shifted, exp_done,
             zero_set, zeroed, picked, counted, rows_ready) = [rsp.sem(n) for n in (
                 "r_in", "moments", "std_ready", "chain", "ln_done", "xT_ready", "xT_read", "lg_ready", "lg_read",
                 "shifted", "exp_done", "zero_set", "zeroed", "picked", "counted", "rows_ready")]
            kept, gate_sem = rsp.sem("kept"), rsp.sem("gate_sem")
            block = route_ctx.enter_context(nc.Block())

            @block.sync
            def _(sync):
                sync.dma_start(wr[:, :], ins["L0_ffn_Wr"]).then_inc(r_in, 16)
                sync.dma_start(brow[:, :], ins["L0_ffn_br"].rearrange("(a n) -> a n", a=1).broadcast_to([S, E])).then_inc(r_in, 16)
                sync.dma_start(pref[:, :], ins["c_pref"]).then_inc(r_in, 16)
                sync.dma_start(before[:, :], ins["c_before"]).then_inc(r_in, 16)
                sync.dma_start(numbers[:, :], ins["c_numbers"]).then_inc(r_in, 16)
                sync.dma_start(token[:, :], ins["c_token"]).then_inc(r_in, 16)
                sync.dma_start(spare[:, :], ins["c_spare"]).then_inc(r_in, 16)
                sync.wait_ge(zero_set, 1)
                sync.dma_start(routed.rearrange("(p r) d -> p (r d)", p=TILE),
                               spare_rows[:, :, :].rearrange("p r d -> p (r d)")).then_inc(zeroed, 16)
                for h in range(2):
                    half = slice(4 * h, 4 * h + 4)
                    sync.dma_start(w1[:, :].rearrange("p (e f) -> p e f", e=E)[:, half, :],
                                   ins["L0_ffn_W1"][half].rearrange("e d f -> d e f")).then_inc(w_in, 16)
                    sync.dma_start(w2[:, half, :, :], ins["L0_ffn_W2"][half].rearrange("e (j p) o -> p e j o", p=D))\
                        .then_inc(w_in, 16)
                for dst, name in ((b1row, "L0_ffn_b1"), (b2row, "L0_ffn_b2")):
                    sync.dma_start(dst[:, :], ins[name].rearrange("(a e) f -> a (e f)", a=1)
                                   .broadcast_to([TILE, dst.shape[1]])).then_inc(w_in, 16)

            @block.tensor
            def _(pe):
                pe.wait_ge(r_in, 112)

                def step(t):
                    if t.exists(NB):
                        n, s = t.index(), t.phase(2)
                        at_least(pe, ln_done, n + 1)
                        at_least(pe, xT_read, n - 1)
                        pe.transpose(turned[s][:, 0:S], xn_now[t.phase(4)][:, :], st.ident[0:S, 0:S]).then_inc(xT_ready, 1)
                    u = t.back(1)
                    if u.exists(NB):
                        n, s = u.index(), u.phase(2)
                        at_least(pe, xT_read, n + 1)
                        at_least(pe, lg_read, n - 1)
                        pe.matmul(lg[s][0:S, 0:E], xnTs[s][:, :], wr[:, :], start=True, stop=True).then_inc(lg_ready, 1)

                run_steps(pe, step, 0, NB, 2, 4, 1)
                pe.wait_ge(picked, 1)
                flat = pick[:, :, :].rearrange("p n e -> p (n e)")
                pe.matmul(counts[0:S, 0:NB * E], before[:, :], flat, start=True, stop=True)
                pe.matmul(counts[0:S, NB * E:2 * NB * E], ones[:, :], flat, start=True, stop=True).then_inc(counted, 1)

            @block.scalar
            def _(act):
                act.wait_ge(moments, 1)
                act.activation(std[:, :], var[:, :], ACT.Sqrt).then_inc(std_ready, 1)

                def step(t):
                    if t.exists(NB):
                        n, s = t.index(), t.phase(2)
                        at_least(act, xT_ready, n + 1)
                        at_least(act, lg_ready, n - 1)
                        act.activation(xnTs[s][:, :], turned[s][:, 0:S], ACT.Copy).then_inc(xT_read, 1)

                run_steps(act, step, 0, NB, 0, 4, 1)
                act.wait_ge(shifted, 1)
                act.activation(expo[:, :, :], logits[:, :, :], ACT.Exp).then_inc(exp_done, 1)

            @block.gpsimd
            def _(pool):
                def step(t):
                    if t.exists(NB):
                        n = t.index()
                        at_least(pool, ln_done, n + 1)
                        pool.sem_inc(gate_sem, 1)
                        pool.tensor_copy(xn[:, n, 0:D], xn_now[t.phase(4)][:, :]).then_inc(kept, 1)

                run_steps(pool, step, 0, NB, 0, 4, 1)
                pool.wait_ge(kept, NB)
                pool.wait_ge(zeroed, 16)
                pool.wait_ge(rows_ready, 1)
                for n in range(NB):
                    pool.indirect_dma_start(routed, bass.IndirectOffsetOnAxis(ap=row[:, n:n + 1], axis=0),
                                            xn[:, n, :], None).then_inc(scattered, 16)

            @block.vector
            def _(dve):
                link = Chain(dve, chain)
                dve.memset(ones[:, :], 1.0)
                link(dve.memset(spare_rows[:, :, :], 0.0))
                layernorm_moments(dve, link, st, tmp, var)
                dve.tensor_scalar(var[:, :], var[:, :], EPS, None, ALU.add).then_inc(moments, 1)
                dve.wait_ge(std_ready, 1)
                link(dve.reciprocal(st.rstd[:, :], std[:, :]))
                dve.wait_ge(r_in, 112)
                dve.tensor_copy(spare_rows[:, :, D], spare[:, :]).then_inc(zero_set, 1)
                dve.tensor_copy(xn[:, :, D], token[:, :])

                def step(t):
                    if t.exists(NB):
                        n = t.index()
                        at_least(dve, xT_ready, n - 3)
                        at_least(dve, kept, n - 3)
                        dve.tensor_scalar(xn_now[t.phase(4)][:, :], st.xs[:, n, :], st.mean[:, bass.ds(n, 1)],
                                          st.rstd[:, bass.ds(n, 1)], ALU.subtract, ALU.mult).then_inc(ln_done, 1)
                    u = t.back(3)
                    if u.exists(NB):
                        n = u.index()
                        at_least(dve, lg_ready, n + 1)
                        dve.tensor_tensor(logits[:, n, :], lg[u.phase(2)][0:S, 0:E], brow[:, :], ALU.add).then_inc(lg_read, 1)

                run_steps(dve, step, 0, NB, 4, 4, 1)
                dve.wait_ge(lg_read, NB)

                def over_experts(v):
                    return v[:, :].rearrange("p (n a) -> p n a", a=1).broadcast_to([S, NB, E])

                link(dve.tensor_reduce(best[:, :], logits[:, :, :], AX.X, ALU.max))
                dve.tensor_tensor(logits[:, :, :], logits[:, :, :], over_experts(best), ALU.subtract).then_inc(shifted, 1)
                dve.wait_ge(shifted, 1)
                link(dve.tensor_scalar(pick[:, :, :], logits[:, :, :], 0.0, None, ALU.is_equal))
                link(dve.tensor_tensor(pick[:, :, :], pick[:, :, :],
                                       pref[:, :].rearrange("p (a e) -> p a e", a=1).broadcast_to([S, NB, E]), ALU.mult))
                link(dve.tensor_reduce(best[:, :], pick[:, :, :], AX.X, ALU.max))
                dve.tensor_tensor(pick[:, :, :], pick[:, :, :], over_experts(best), ALU.is_equal).then_inc(picked, 1)
                dve.wait_ge(exp_done, 1)
                link(dve.tensor_reduce(total[:, :], expo[:, :, :], AX.X, ALU.add))
                link(dve.reciprocal(gate[:, :], total[:, :]))

                dve.wait_ge(counted, 1)
                tot = counts[0:S, NB * E:2 * NB * E].rearrange("p (n e) -> p n e", n=NB)
                link(dve.tensor_copy(sums[0][:, :, :], tot))
                now = 0
                for k in (1, 2, 4, 8, 16):
                    a, b = sums[now], sums[1 - now]
                    dve.tensor_copy(b[:, 0:k, :], a[:, 0:k, :])
                    link(dve.tensor_tensor(b[:, k:NB, :], a[:, k:NB, :], a[:, 0:NB - k, :], ALU.add))
                    now = 1 - now
                upto = sums[now]
                link(dve.tensor_copy(last[:, :], upto[:, NB - 1, :]))
                link(dve.tensor_tensor(fills[:, :, :], last[:, :].rearrange("p (e a) -> p e a", a=1).broadcast_to([S, E, MOST]),
                                       numbers[:, TILES:TILES + MOST].rearrange("p (a i) -> p a i", a=1)
                                       .broadcast_to([S, E, MOST]), ALU.is_gt))
                link(dve.tensor_reduce(used[:, :], fills[:, :, :], AX.X, ALU.add))
                link(dve.tensor_copy(ends[0][:, :], used[:, :]))
                at = 0
                for k in (1, 2, 4):
                    a, b = ends[at], ends[1 - at]
                    dve.tensor_copy(b[:, 0:k], a[:, 0:k])
                    link(dve.tensor_tensor(b[:, k:E], a[:, k:E], a[:, 0:E - k], ALU.add))
                    at = 1 - at
                end = ends[at]
                link(dve.tensor_tensor(base[:, :], end[:, :], used[:, :], ALU.subtract))
                link(dve.tensor_scalar(base[:, :], base[:, :], float(TILE), None, ALU.mult))
                other = sums[1 - now]
                link(dve.tensor_tensor(other[:, :, :], upto[:, :, :], tot, ALU.subtract))
                link(dve.tensor_tensor(other[:, :, :], other[:, :, :],
                                       counts[0:S, 0:NB * E].rearrange("p (n e) -> p n e", n=NB), ALU.add))
                link(dve.tensor_tensor(other[:, :, :], other[:, :, :], base[:, :].rearrange("p (a e) -> p a e", a=1)
                                       .broadcast_to([S, NB, E]), ALU.add))
                link(dve.tensor_tensor(other[:, :, :], other[:, :, :], pick[:, :, :], ALU.mult))
                link(dve.tensor_reduce(rowf[:, :], other[:, :, :], AX.X, ALU.add))
                dve.tensor_copy(row[:, :], rowf[:, :]).then_inc(rows_ready, 1)
                link(dve.tensor_tensor(past[:, :, :], numbers[0:1, 0:TILES].rearrange("p (j a) -> p j a", a=1)
                                       .broadcast_to([1, TILES, E]), end[0:1, :].rearrange("p (a e) -> p a e", a=1)
                                       .broadcast_to([1, TILES, E]), ALU.is_ge))
                link(dve.tensor_reduce(owner[:, :], past[:, :, :], AX.X, ALU.add))
                link(dve.tensor_scalar(owner[:, :], owner[:, :], float(E - 1), None, ALU.min))
                link(dve.tensor_copy(tile_expert[:, :], owner[:, :]))

        xin = [sb(f"xin{i}", [TILE, G, D + 1]) for i in range(2)]
        home = sb("home", [TILE, TILES], I32)
        yout = [sb(f"yout{i}", [TILE, G, D]) for i in range(2)]
        xT = [sb(f"xT{i}", [D, TILE]) for i in range(2)]
        hidden = [sb(f"hidden{i}", [TILE, F]) for i in range(2)]
        hiddenT = [sb(f"hiddenT{i}", [D, FQ, TILE]) for i in range(2)]
        back = sb("back", [S, NB, D])
        tbank, hbank, hTbank, ybank = [[sp.ps(f"{n}{i}") for i in range(2)] for n in ("tbank", "hbank", "hTbank", "ybank")]
        (x_loaded0, x_loaded1, stored0, stored1, t_ready, t_read, h_ready, h_read, gelu_done, hT_ready, hT_read, y_ready, y_done,
         added) = [sem(n) for n in ("x_loaded0", "x_loaded1", "stored0", "stored1", "t_ready", "t_read", "h_ready", "h_read",
                                    "gelu_done", "hT_ready", "hT_read", "y_ready", "y_done", "added")]
        home_ready = sem("home_ready")
        x_loaded, stored = [x_loaded0, x_loaded1], [stored0, stored1]
        returned = [sem(f"returned{q}") for q in range(4)]
        PER = 2 * G
        block = ctx.enter_context(nc.Block())

        def expert_of(eng, t):
            return eng.value_load(tile_expert[0:1, bass.ds(t.index(), 1)], min_val=0, max_val=E - 1)

        @block.sync
        def _(sync):
            def load(g, slot):
                sync.dma_start(xin[slot][:, :, :], routed[bass.ds(g * (G * TILE), G * TILE)]
                               .rearrange("(j p) d -> p j d", p=TILE)).then_inc(x_loaded[slot], 16)

            sync.wait_ge(scattered, 16 * NB)
            for g in range(2):
                load(g, g)

            with sync.Fori(0, TILES // PER - 1) as it:
                for slot in range(2):
                    g = it * 2 + slot
                    sync.wait_ge(home_ready, g + 1)
                    load(g + 2, slot)
            for done in stored:
                sync.wait_ge(done, 16 * TILES // 2)
            for q in range(4):
                n = q * NB // 4
                sync.dma_start(back[:, n:n + NB // 4, :], answers[n * S:(n + NB // 4) * S].rearrange("(n s) d -> s n d", s=S))\
                    .then_inc(returned[q], 16)

        @block.tensor
        def _(pe):
            pe.wait_ge(w_in, 96)

            def step(t):
                if t.exists(TILES):
                    k, s = t.index(), t.phase(2)
                    at_least(pe, x_loaded[t.phase(PER) // G], (t.index(PER) + 1) * 16)
                    at_least(pe, t_read, k - 1)
                    pe.transpose(tbank[s][:, 0:TILE], xin[t.phase(PER) // G][:, t.phase(G), 0:D], st.ident[:, :])\
                        .then_inc(t_ready, 1)
                u = t.back(1)
                if u.exists(TILES):
                    k, s = u.index(), u.phase(2)
                    e = expert_of(pe, u)
                    at_least(pe, t_read, k + 1)
                    at_least(pe, h_read, k - 1)
                    pe.matmul(hbank[s][:, :], xT[s][:, :], w1[:, bass.ds(e * F, F)], start=True, stop=True)\
                        .then_inc(h_ready, 1)
                u = t.back(3)
                if u.exists(TILES):
                    k, s = u.index(), u.phase(2)
                    at_least(pe, gelu_done, k + 1)
                    at_least(pe, hT_read, k - 1)
                    for f in range(FQ):
                        i = pe.transpose(hTbank[s][:, f * TILE:(f + 1) * TILE], hidden[s][:, f * D:(f + 1) * D], st.ident[:, :])
                    i.then_inc(hT_ready, 1)
                u = t.back(4)
                if u.exists(TILES):
                    k, s = u.index(), u.phase(2)
                    e = expert_of(pe, u)
                    at_least(pe, hT_read, k + 1)
                    at_least(pe, y_done, k - 1)
                    for f in range(FQ):
                        i = pe.matmul(ybank[s][:, 0:D], hiddenT[s][:, f, :], w2[:, bass.ds(e, 1), f, :]
                                      .rearrange("p a o -> p (a o)"), start=(f == 0), stop=(f == FQ - 1))
                    i.then_inc(y_ready, 1)

            run_steps(pe, step, 0, TILES, 5, PER, 1)

        @block.scalar
        def _(act):
            def step(t):
                u = t.back(3)
                if u.exists(TILES):
                    k, s = u.index(), u.phase(2)
                    at_least(act, hT_ready, k + 1)
                    at_least(act, y_ready, k - 1)
                    act.activation(hiddenT[s][:, :, :], hTbank[s][:, :].rearrange("p (f q) -> p f q", f=FQ), ACT.Copy)\
                        .then_inc(hT_read, 1)
                u = t.back(1)
                if u.exists(TILES):
                    k, s = u.index(), u.phase(2)
                    at_least(act, h_read, k + 1)
                    act.activation(hidden[s][:, :], hidden[s][:, :], ACT.Gelu).then_inc(gelu_done, 1)

            run_steps(act, step, 0, TILES, 4, PER, 1)

        @block.vector
        def _(dve):
            dve.wait_ge(w_in, 96)

            def step(t):
                if t.exists(TILES):
                    k, s = t.index(), t.phase(2)
                    at_least(dve, t_ready, k + 1)
                    at_least(dve, h_ready, k - 1)
                    dve.tensor_copy(xT[s][:, :], tbank[s][:, 0:TILE]).then_inc(t_read, 1)
                    if t.phase(G) == G - 1:
                        dve.tensor_copy(home[:, bass.ds(t.back(G - 1).index(), G)], xin[t.phase(PER) // G][:, :, D])\
                            .then_inc(home_ready, 1)
                u = t.back(1)
                if u.exists(TILES):
                    k, s = u.index(), u.phase(2)
                    e = expert_of(dve, u)
                    at_least(dve, h_ready, k + 1)
                    at_least(dve, hT_ready, k - 1)
                    dve.tensor_tensor(hidden[s][:, :], hbank[s][:, :], b1row[:, bass.ds(e * F, F)], ALU.add)\
                        .then_inc(h_read, 1)
                u = t.back(5)
                if u.exists(TILES):
                    k, s = u.index(), u.phase(2)
                    e = expert_of(dve, u)
                    at_least(dve, y_ready, k + 1)
                    if u.phase(G) == 0:
                        at_least(dve, stored[u.phase(PER) // G], u.index(PER) * 16 * G)
                    dve.tensor_tensor(yout[u.phase(PER) // G][:, u.phase(G), :], ybank[s][:, 0:D],
                                      b2row[:, bass.ds(e * D, D)], ALU.add).then_inc(y_done, 1)

            run_steps(dve, step, 0, TILES, 6, PER, 1)
            for q in range(4):
                dve.wait_ge(returned[q], 16)
                for n in range(q * NB // 4, (q + 1) * NB // 4):
                    i = dve.scalar_tensor_tensor(st.xs[:, n, :], back[:, n, :], gate[:, n:n + 1], st.xs[:, n, :],
                                                 ALU.mult, ALU.add)
                i.then_inc(added, 1)
                dve.wait_ge(added, q + 1)
                for n in range(q * NB // 4, (q + 1) * NB // 4):
                    dve.bn_stats(st.stats[:, n, :], st.xs[:, n, :])

        @block.gpsimd
        def _(pool):
            for k in range(TILES):
                slot = k // G % 2
                if k % G == 0:
                    pool.wait_ge(home_ready, k // G + 1)
                pool.wait_ge(y_done, k + 1)
                pool.indirect_dma_start(answers, bass.IndirectOffsetOnAxis(ap=home[:, k:k + 1], axis=0),
                                        yout[slot][:, k % G, :], None).then_inc(stored[slot], 16)


def context_attention(nc, st, ins):
    plan = WHOLE_PLAN
    R = 3
    ITEMS = NB * R
    UN = 4
    PER = UN * R
    G = 4
    with ExitStack() as ctx:
        sp = Space(nc, ctx, "cx")
        sb, sem = sp.sb, sp.sem
        wqv = sb("wqv", [D, 4, D])
        brow = sb("brow", [S, D])
        wsim, bsim = sb("wsim", [D, 3]), sb("bsim", [S, 1])
        eT_all = sb("eT_all", [D, NB * S])
        mx, weight = sb("mx", [S, NB]), sb("weight", [S, NB])
        w_in = sem("w_in")
        with ExitStack() as part_ctx:
            psp = Space(nc, part_ctx, "cp")
            psb, psem = psp.sb, psp.sem
            tmp, var, std = psb("tmp", [S, NB]), psb("var", [S, NB]), psb("std", [S, NB])
            e = psb("e", [S, D])
            eT = [psb(f"eT{i}", [D, S]) for i in range(UN)]
            qT = [psb(f"qT{i}", [D, S]) for i in range(2)]
            rows_in = [psb(f"rows{i}", [D, 12, D]) for i in range(UN)]
            ctxT = [psb(f"ctxT{i}", [D, CTX]) for i in range(2)]
            probs = [psb(f"probs{i}", [S, CTX]) for i in range(2)]
            probsT = [psb(f"probsT{i}", [D, 4, S]) for i in range(2)]
            top3 = [psb(f"top3{i}", [S, R]) for i in range(2)]
            low = [psb(f"low{i}", [S, 1]) for i in range(2)]
            sum3 = [psb(f"sum3{i}", [S, R]) for i in range(UN)]
            inv = psb("inv", [S, 2])
            hT, ehT = psb("hT", [D, S]), psb("ehT", [D, S])
            sbank = psp.ps("sbank", (128, 3 * 512))
            front = [psp.ps(f"front{i}") for i in range(2)]
            pT_bank, h_bank, y_bank = psp.ps("pT_bank"), psp.ps("h_bank"), psp.ps("y_bank")
            rows_loaded = [psem(f"rows_loaded{i}") for i in range(UN)]
            (moments, std_ready, chain, e_ready, f_ready, f_read, eT_copied, bias_added, s_ready, top_done, tops, low_ready,
             exp_done, pT_ready, pT_read, pv_done, hT_read, ehT_made, y_ready, total_done, inv_done, half_added, added) = [
                psem(n) for n in (
                    "moments", "std_ready", "chain", "e_ready", "f_ready", "f_read", "eT_copied", "bias_added", "s_ready",
                    "top_done", "tops", "low_ready", "exp_done", "pT_ready", "pT_read", "pv_done", "hT_read", "ehT_made",
                    "y_ready", "total_done", "inv_done", "half_added", "added")]
            ctx_rows = ins["ctx_1024"]
            block = part_ctx.enter_context(nc.Block())

            def region(t):
                lo = 512 * t.phase(R)
                return lo, min(lo + 512, plan.keys)

            @block.sync
            def _(sync):
                def load(place, slot):
                    n = sync.value_load(st.order[0:1, bass.ds(place, 1)], min_val=0, max_val=NB - 1)
                    for lo, size, part in ((0, plan.main, plan.part), (plan.main, plan.tail, plan.tail)):
                        c0 = 0 if lo == 0 else plan.chunks
                        sync.dma_start(rows_in[slot][0:part, c0:c0 + size // part, :],
                                       ctx_rows[bass.ds(n, 1), lo:lo + size, :].rearrange("a (p c) d -> (a p) c d", p=part))\
                            .then_inc(rows_loaded[slot], 16)

                for j in range(3):
                    sync.dma_start(wsim[:, j:j + 1], ins["L1_xattn_w_sim"][j * D:(j + 1) * D].rearrange("(p a) -> p a", a=1))\
                        .then_inc(w_in, 16)
                sync.dma_start(bsim[:, :], ins["L1_xattn_b_sim"].rearrange("(a n) -> a n", a=1).broadcast_to([S, 1])).then_inc(w_in, 16)
                load(0, 0)
                sync.dma_start(wqv[:, :, :], ins["L1_xattn_W_qv"].rearrange("(j p) o -> p j o", p=D)).then_inc(w_in, 16)
                sync.dma_start(brow[:, :], ins["L1_xattn_b_qv"].rearrange("(a n) -> a n", a=1).broadcast_to([S, D])).then_inc(w_in, 16)
                for n in range(1, UN):
                    load(n, n)
                with sync.Fori(1, NB // UN) as it:
                    for slot in range(UN):
                        n = it * UN + slot
                        sync.wait_ge(pv_done, (n - UN + 1) * R)
                        load(n, slot)

            @block.tensor
            def _(pe):
                pe.wait_ge(w_in, 96)

                def step(t):
                    c, ph = t.back(-R), t.phase(R)
                    if c.exists(ITEMS):
                        n, slot4 = c.index(R), c.phase(PER) // R
                        if ph == 0:
                            at_least(pe, e_ready, n + 1)
                            at_least(pe, f_read, 4 * n - 1)
                            pe.transpose(front[0][:, 0:S], e[:, :], st.ident[0:S, 0:S]).then_inc(f_ready, 1)
                            at_least(pe, rows_loaded[slot4], (c.index(PER) + 1) * 32)
                        at_least(pe, f_read, 4 * n + ph)
                        for j, (lo, size) in enumerate(plan.groups[ph]):
                            i = pe.transpose(front[(ph + 1) % 2][:, 128 * j:128 * j + size],
                                             rows_in[slot4][0:size, 4 * ph + j, :], st.ident[0:size, 0:size])
                        i.then_inc(f_ready, 1)
                    if t.exists(ITEMS):
                        k, n = t.index(), t.index(R)
                        lo, hi = region(t)
                        at_least(pe, f_read, 4 * (n + 1))
                        at_least(pe, exp_done, k - 2)
                        slot = t.phase(2 * R) // R
                        pe.matmul(sbank[0:S, lo:hi], qT[slot][:, :], ctxT[slot][:, lo:hi], start=True, stop=True)\
                            .then_inc(s_ready, 1)
                    u = t.back(3)
                    if u.exists(ITEMS):
                        k = u.index()
                        at_least(pe, exp_done, k + 1)
                        at_least(pe, pT_read, k)
                        for j, (lo, size) in enumerate(plan.groups[u.phase(R)]):
                            i = pe.transpose(pT_bank[0:size, j * S:(j + 1) * S], probs[u.phase(2 * R) // R][:, lo:lo + size],
                                             st.ident[0:S, 0:S])
                        i.then_inc(pT_ready, 1)
                    u = t.back(4)
                    if u.exists(ITEMS):
                        k, r, n = u.index(), u.phase(R), u.index(R)
                        at_least(pe, pT_read, k + 1)
                        if r == 0:
                            at_least(pe, hT_read, n)
                        for j, (lo, size) in enumerate(plan.groups[r]):
                            c = 4 * r + j
                            i = pe.matmul(h_bank[:, 0:S], rows_in[u.phase(PER) // R][0:size, c, :],
                                          probsT[u.phase(2)][0:size, j, :], start=(c == 0), stop=(c == 11))
                        i.then_inc(pv_done, 1)
                    u = t.back(8)
                    if u.phase(R) == 0 and u.exists(ITEMS):
                        n, slot4 = u.index(R), u.phase(PER) // R
                        at_least(pe, added, n)
                        pe.matmul(y_bank[0:S, 400:401], eT[slot4][:, :], wsim[:, 0:1], start=True, stop=True)
                        pe.matmul(y_bank[0:S, 0:D], eT[slot4][:, :], wqv[:, 0, :], start=True, stop=True)
                        at_least(pe, hT_read, n + 1)
                        at_least(pe, ehT_made, n + 1)
                        pe.matmul(y_bank[0:S, D:2 * D], hT[:, :], wqv[:, 1, :], start=True, stop=False)
                        pe.matmul(y_bank[0:S, D:2 * D], ehT[:, :], wqv[:, 2, :], start=False, stop=True).then_inc(y_ready, 1)

                run_steps(pe, step, R, ITEMS, 10, PER, 1)

            @block.scalar
            def _(act):
                act.wait_ge(moments, 1)
                act.activation(std[:, :], var[:, :], ACT.Sqrt).then_inc(std_ready, 1)

                def step(t):
                    u = t.back(2)
                    if u.exists(ITEMS):
                        k, n, r = u.index(), u.index(R), u.phase(R)
                        lo, hi = region(u)
                        slot = u.phase(2 * R) // R
                        at_least(act, low_ready, n + 1)
                        at_least(act, pT_ready, k - 5)
                        if r == 0:
                            at_least(act, added, n - UN + 1)
                        act.activation(probs[slot][:, lo:hi], sbank[0:S, lo:hi], ACT.Exp, bias=low[slot][:, 0:1],
                                       accum_out=sum3[u.phase(PER) // R][:, r:r + 1]).then_inc(exp_done, 1)
                    u = t.back(3)
                    if u.exists(ITEMS):
                        k, r = u.index(), u.phase(R)
                        at_least(act, pT_ready, k + 1)
                        at_least(act, pv_done, k - 1)
                        if r == 2:
                            act.activation(probsT[u.phase(2)][0:plan.tail, 3, :], pT_bank[0:plan.tail, 3 * S:4 * S], ACT.Copy)
                            act.activation(probsT[u.phase(2)][:, 0:3, :], pT_bank[:, 0:3 * S]
                                           .rearrange("p (c q) -> p c q", c=3), ACT.Copy).then_inc(pT_read, 1)
                        else:
                            act.activation(probsT[u.phase(2)][:, :, :], pT_bank[:, 0:4 * S]
                                           .rearrange("p (c q) -> p c q", c=4), ACT.Copy).then_inc(pT_read, 1)
                    u = t.back(6)
                    if u.phase(R) == 0 and u.exists(ITEMS):
                        n = u.index(R)
                        at_least(act, pv_done, R * (n + 1))
                        at_least(act, y_ready, n)
                        act.activation(hT[:, :], h_bank[:, 0:S], ACT.Copy).then_inc(hT_read, 1)

                run_steps(act, step, 0, ITEMS, 8, PER, 1)

            @block.gpsimd
            def _(pool):
                def step(t):
                    c = t.back(-R)
                    if t.phase(R) == 0 and c.exists(ITEMS):
                        n = c.index(R)
                        at_least(pool, e_ready, n + 1)
                        pool.wait_ge(w_in, 96)
                        x = st.xs[:, n, :]
                        pool.tensor_tensor(x, x, brow[:, :], ALU.add).then_inc(bias_added, 1)
                        at_least(pool, f_read, 4 * n + 1)
                        start = n * S
                        pool.tensor_copy(eT_all[:, bass.ds(start, S)], eT[c.phase(PER) // R][:, :]).then_inc(eT_copied, 1)

                run_steps(pool, step, R, ITEMS, 0, PER, 1)

            @block.vector
            def _(dve):
                link = Chain(dve, chain)
                layernorm_moments(dve, link, st, tmp, var)
                dve.tensor_scalar(var[:, :], var[:, :], EPS, None, ALU.add).then_inc(moments, 1)
                dve.wait_ge(std_ready, 1)
                link(dve.reciprocal(st.rstd[:, :], std[:, :]))
                dve.wait_ge(w_in, 96)

                def step(t):
                    c = t.back(-2 * R)
                    if t.phase(R) == 2 and c.exists(ITEMS):
                        n = c.index(R)
                        at_least(dve, f_ready, 4 * (n - 1) + 1)
                        dve.tensor_scalar(e[:, :], st.xs[:, n, :], st.mean[:, bass.ds(n, 1)], st.rstd[:, bass.ds(n, 1)],
                                          ALU.subtract, ALU.mult).then_inc(e_ready, 1)
                    c, ph = t.back(-R), t.phase(R)
                    if c.exists(ITEMS):
                        n, slot = c.index(R), c.phase(2 * R) // R
                        if ph == 0:
                            at_least(dve, f_ready, 4 * n + 1)
                            at_least(dve, y_ready, n - UN + 1)
                            at_least(dve, eT_copied, n - UN + 1)
                            dve.tensor_scalar(qT[slot][:, :], front[0][:, 0:S], wsim[:, 2:3], wsim[:, 1:2], ALU.mult, ALU.add)
                            dve.tensor_copy(eT[c.phase(PER) // R][:, :], front[0][:, 0:S]).then_inc(f_read, 1)
                        base = plan.groups[ph][0][0]
                        past = min(base + 512, plan.keys)
                        at_least(dve, f_ready, 4 * n + ph + 2)
                        dve.tensor_copy(ctxT[slot][:, base:past], front[(ph + 1) % 2][:, 0:past - base]).then_inc(f_read, 1)
                    if t.exists(ITEMS):
                        k, n, r = t.index(), t.index(R), t.phase(R)
                        lo, hi = region(t)
                        slot = t.phase(2 * R) // R
                        at_least(dve, s_ready, k + 1)
                        dve.tensor_reduce(top3[slot][:, r:r + 1], sbank[0:S, lo:hi], AX.X, ALU.max).then_inc(top_done, 1)
                        if r == 2:
                            dve.wait_ge(top_done, k + 1)
                            dve.tensor_reduce(mx[:, bass.ds(n, 1)], top3[slot][:, :], AX.X, ALU.max).then_inc(tops, 1)
                            at_least(dve, exp_done, R * (n - 1))
                            dve.wait_ge(tops, n + 1)
                            dve.tensor_scalar(low[slot][:, 0:1], mx[:, bass.ds(n, 1)], -1.0, None, ALU.mult)\
                                .then_inc(low_ready, 1)
                    u = t.back(7)
                    if u.phase(R) == 0 and u.exists(ITEMS):
                        n, slot4 = u.index(R), u.phase(PER) // R
                        at_least(dve, hT_read, n + 1)
                        at_least(dve, y_ready, n)
                        dve.tensor_tensor(ehT[:, :], hT[:, :], eT[slot4][:, :], ALU.mult).then_inc(ehT_made, 1)
                        dve.tensor_reduce(inv[:, 0:1], sum3[slot4][:, :], AX.X, ALU.add).then_inc(total_done, 1)
                        dve.wait_ge(total_done, n + 1)
                        at_least(dve, half_added, n)
                        dve.reciprocal(inv[:, 1:2], inv[:, 0:1]).then_inc(inv_done, 1)
                    u = t.back(9)
                    if u.phase(R) == 0 and u.exists(ITEMS):
                        n = u.index(R)
                        x = st.xs[:, n, :]
                        at_least(dve, y_ready, n + 1)
                        at_least(dve, bias_added, n + 1)
                        at_least(dve, inv_done, n + 1)
                        dve.scalar_tensor_tensor(x, y_bank[0:S, D:2 * D], inv[:, 1:2], x, ALU.mult, ALU.add)\
                            .then_inc(half_added, 1)
                        dve.scalar_tensor_tensor(weight[:, bass.ds(n, 1)], y_bank[0:S, 400:401], bsim[:, 0:1],
                                                 mx[:, bass.ds(n, 1)], ALU.add, ALU.add)
                        dve.wait_ge(half_added, n + 1)
                        dve.tensor_tensor(x, y_bank[0:S, 0:D], x, ALU.add).then_inc(added, 1)

                run_steps(dve, step, 2 * R, ITEMS, 10, PER, 1)

        tokens = sb("tokens", [NB, S])
        lowest, total = sb("lowest", [NB, 1]), sb("total", [NB, 2])
        spread = sb("spread", [NB, NB * S])
        ones = sb("ones", [NB, D])
        weighed = [sb(f"weighed{i}", [D, G, S]) for i in range(2)]
        mean_e = [sb(f"mean_e{i}", [D, G]) for i in range(2)]
        ecT = [sb(f"ecT{i}", [D, G, S]) for i in range(2)]
        wbank = sp.ps("wbank")
        bbank = [sp.ps(f"bbank{i}") for i in range(2)]
        obank = [sp.ps(f"obank{i}") for i in range(2)]
        (t_ready, low_done, e_done, spread_done, chain2, b_ready, b_read, m_done, ec_done, o_ready, o_read) = [
            sem(n) for n in ("t_ready", "low_done", "e_done", "spread_done", "chain2", "b_ready", "b_read", "m_done",
                             "ec_done", "o_ready", "o_read")]
        block = ctx.enter_context(nc.Block())
        GROUPS = NB // G

        @block.tensor
        def _(pe):
            pe.transpose(wbank[0:NB, 0:S], weight[:, :], st.ident[0:S, 0:S]).then_inc(t_ready, 1)
            pe.wait_ge(spread_done, 1)

            def step(t):
                if t.exists(GROUPS):
                    g = t.index()
                    at_least(pe, b_read, g - 1)
                    start = g * (G * S)
                    pe.matmul(bbank[t.phase(2)][:, 0:G * S], ones[:, :], spread[:, bass.ds(start, G * S)],
                              start=True, stop=True).then_inc(b_ready, 1)
                u = t.back(1)
                if u.exists(GROUPS):
                    g = u.index()
                    at_least(pe, ec_done, g + 1)
                    at_least(pe, o_read, g - 1)
                    for b in range(G):
                        i = pe.matmul(obank[u.phase(2)][0:S, b * D:(b + 1) * D], ecT[u.phase(2)][:, b, :], wqv[:, 3, :],
                                      start=True, stop=True)
                    i.then_inc(o_ready, 1)

            run_steps(pe, step, 0, GROUPS, 2, 2, 1)

        @block.scalar
        def _(act):
            act.wait_ge(low_done, 1)
            act.activation(tokens[:, :], wbank[0:NB, 0:S], ACT.Exp, bias=lowest[:, 0:1], accum_out=total[:, 0:1])\
                .then_inc(e_done, 1)

        @block.vector
        def _(dve):
            link = Chain(dve, chain2)
            dve.memset(ones[:, :], 1.0)
            dve.wait_ge(t_ready, 1)
            link(dve.tensor_reduce(lowest[:, :], wbank[0:NB, 0:S], AX.X, ALU.max))
            dve.tensor_scalar(lowest[:, :], lowest[:, :], -1.0, None, ALU.mult).then_inc(low_done, 1)
            dve.wait_ge(e_done, 1)
            link(dve.reciprocal(total[:, 1:2], total[:, 0:1]))
            link(dve.tensor_scalar(tokens[:, :], tokens[:, :], total[:, 1:2], None, ALU.mult))
            dve.tensor_tensor(spread[:, :].rearrange("p (n s) -> p n s", n=NB),
                              tokens[:, :].rearrange("p (a s) -> p a s", a=1).broadcast_to([NB, NB, S]),
                              st.ident[0:NB, 0:NB].rearrange("p (n a) -> p n a", a=1).broadcast_to([NB, NB, S]),
                              ALU.mult).then_inc(spread_done, 1)

            def step(t):
                if t.exists(GROUPS):
                    g, s = t.index(), t.phase(2)
                    start = g * (G * S)
                    eT_g = eT_all[:, bass.ds(start, G * S)].rearrange("p (b q) -> p b q", b=G)
                    at_least(dve, b_ready, g + 1)
                    dve.tensor_tensor(weighed[s][:, :, :], bbank[s][:, 0:G * S].rearrange("p (b q) -> p b q", b=G), eT_g,
                                      ALU.mult).then_inc(b_read, 1)
                    dve.wait_ge(b_read, g + 1)
                    dve.tensor_reduce(mean_e[s][:, :], weighed[s][:, :, :], AX.X, ALU.add).then_inc(m_done, 1)
                    at_least(dve, o_ready, g - 1)
                    dve.wait_ge(m_done, g + 1)
                    dve.tensor_tensor(ecT[s][:, :, :], eT_g, mean_e[s][:, :].rearrange("p (b a) -> p b a", a=1)
                                      .broadcast_to([D, G, S]), ALU.mult).then_inc(ec_done, 1)
                u = t.back(1)
                if u.exists(GROUPS):
                    g = u.index()
                    first = g * G
                    x = st.xs[:, bass.ds(first, G), :]
                    at_least(dve, o_ready, g + 1)
                    dve.tensor_tensor(x, obank[u.phase(2)][0:S, :].rearrange("p (b d) -> p b d", b=G), x, ALU.add)\
                        .then_inc(o_read, 1)
                    dve.wait_ge(o_read, g + 1)
                    for b in range(G):
                        n = g * G + b
                        dve.bn_stats(st.stats[:, n, :], st.xs[:, n, :])

            run_steps(dve, step, 0, GROUPS, 2, 2, 1)


def feed_forward(nc, st, ins):
    I = 352
    QMAX = 127.0
    CUTS = [(0, 128), (128, 128), (256, 96)]
    J, G = len(CUTS), 4
    GROUPS = NB // G
    W = G * S
    with ExitStack() as ctx:
        sp = Space(nc, ctx, "ff")
        sb = sp.sb
        e_all = sb("e_all", [S, NB, D])
        hT = sb("hT", [D, J, NB * S])
        upT, downT = sb("upT", [D, 2, I], BF16), sb("downT", [D, J, D], BF16)
        w_scale = sb("w_scale", [D, 2 * J])
        h_scale = sb("h_scale", [D, 2 * J])
        down_row = sb("down_row", [S, D])
        sig = sb("sig", [D, 2])
        inv_x, inv_h, round_up = sb("inv_x", [D, 1]), sb("inv_h", [D, 1]), sb("round_up", [D, 1])
        sx = sb("sx", [D, 2])
        hm = sb("hm", [D, GROUPS * J])
        ones = sb("ones", [D, D])
        one_row = sb("one_row", [1, D])

        def scales_from(dve, link, bank, which, scale, inverse):
            link(dve.tensor_scalar(scale, bank[:, 0:1], sig[:, which:which + 1], 1.0 / QMAX, ALU.mult, ALU.mult))
            link(dve.reciprocal(inverse, scale))

        with ExitStack() as part_ctx:
            psp = Space(nc, part_ctx, "fp")
            tmp, var, std = psp.sb("tmp", [S, NB]), psp.sb("var", [S, NB]), psp.sb("std", [S, NB])
            wraw = psp.sb("wraw", [D, 2 * J, D])
            draw = psp.sb("draw", [D, I])
            wq, dq = psp.sb("wq", [D, 2 * J, D], BF16), psp.sb("dq", [D, I], BF16)
            w_inv, d_scale, d_inv, diag = (psp.sb("w_inv", [D, 2 * J]), psp.sb("d_scale", [D, 1]), psp.sb("d_inv", [D, 1]),
                                           psp.sb("diag", [D, D]))
            clip = psp.sb("clip", [D, 2])
            em, emax, etop = psp.sb("em", [S, GROUPS]), psp.sb("emax", [S, 1]), psp.sb("etop", [1, 1])
            tbank = [psp.ps(f"tbank{i}", (128, 1024), BF16) for i in range(2)]
            row_bank, m_bank, top_bank = psp.ps("row_bank"), psp.ps("m_bank"), psp.ps("top_bank")
            w_in, moments, std_ready, chain, clip_done, wq_done, diag_done, t_ready, m_ready, m_read, top_ready, e_done = [
                psp.sem(n) for n in ("w_in", "moments", "std_ready", "chain", "clip_done", "wq_done", "diag_done",
                                     "t_ready", "m_ready", "m_read", "top_ready", "e_done")]
            block = part_ctx.enter_context(nc.Block())

            @block.sync
            def _(sync):
                for w, name in enumerate(("w_gate", "w_up")):
                    src = ins["L1_ffn_" + name]
                    sync.dma_start(wraw[:, J * w:J * w + 2, :], src[0:256, :].rearrange("(j p) n -> p j n", p=D)).then_inc(w_in, 16)
                    sync.dma_start(wraw[0:96, J * w + 2, :], src[256:I, :]).then_inc(w_in, 16)
                sync.dma_start(draw[:, :], ins["L1_ffn_w_down"]).then_inc(w_in, 16)
                for i, name in enumerate(("clip_x", "clip_down")):
                    sync.dma_start(clip[:, i:i + 1], ins["L1_ffn_" + name].rearrange("(a n) -> a n", a=1).broadcast_to([D, 1]))\
                        .then_inc(w_in, 16)

            @block.scalar
            def _(act):
                act.wait_ge(moments, 1)
                act.activation(std[:, :], var[:, :], ACT.Sqrt).then_inc(std_ready, 1)
                act.wait_ge(w_in, 16 * 7)
                act.activation(sig[:, :], clip[:, :], ACT.Exp, scale=-1.0).then_inc(clip_done, 1)

            @block.tensor
            def _(pe):
                pe.wait_ge(wq_done, 1)
                for w in range(2):
                    for j, (lo, size) in enumerate(CUTS):
                        i = pe.transpose(tbank[w][:, lo:lo + size], wq[0:size, J * w + j, :], st.ident_b[0:size, 0:size])
                i.then_inc(t_ready, 1)
                pe.wait_ge(t_ready, 1)
                for j, (lo, size) in enumerate(CUTS):
                    i = pe.transpose(tbank[1][0:size, 512 + j * D:512 + (j + 1) * D], dq[:, lo:lo + size], st.ident_b[:, :])
                i.then_inc(t_ready, 1)
                pe.wait_ge(diag_done, 1)
                pe.matmul(row_bank[0:S, 0:D], ones[:, 0:S], diag[:, :], start=True, stop=True).then_inc(t_ready, 1)
                pe.wait_ge(e_done, GROUPS + 1)
                pe.transpose(m_bank[0:1, 0:S], emax[:, :], st.ident[0:S, 0:S]).then_inc(m_ready, 1)
                pe.wait_ge(m_read, 1)
                pe.matmul(top_bank[:, 0:1], one_row[:, :], etop[:, :], start=True, stop=True).then_inc(top_ready, 1)

            @block.vector
            def _(dve):
                link = Chain(dve, chain)
                dve.memset(ones[:, :], 1.0)
                dve.memset(one_row[:, :], 1.0)
                dve.memset(hm[:, :], 0.0)
                dve.memset(round_up[:, :], ROUND)
                link(dve.memset(wraw[96:D, 2, :], 1.0))
                link(dve.memset(wraw[96:D, 5, :], 1.0))
                layernorm_moments(dve, link, st, tmp, var)
                dve.tensor_scalar(var[:, :], var[:, :], EPS, None, ALU.add).then_inc(moments, 1)
                dve.wait_ge(std_ready, 1)
                link(dve.reciprocal(st.rstd[:, :], std[:, :]))
                for g in range(GROUPS):
                    for n in range(G * g, G * g + G):
                        i = dve.tensor_scalar(e_all[:, n, :], st.xs[:, n, :], st.mean[:, n:n + 1], st.rstd[:, n:n + 1],
                                              ALU.subtract, ALU.mult)
                    link(i)
                    dve.tensor_reduce(em[:, g:g + 1], e_all[:, G * g:G * g + G, :], AX.XY, ALU.max,
                                      apply_absolute_value=True).then_inc(e_done, 1)
                dve.wait_ge(e_done, GROUPS)
                dve.tensor_reduce(emax[:, :], em[:, :], AX.X, ALU.max).then_inc(e_done, 1)
                dve.wait_ge(w_in, 16 * 7)
                dve.tensor_reduce(w_scale[:, :], wraw[:, :, :], AX.X, ALU.max, apply_absolute_value=True)
                link(dve.tensor_reduce(d_scale[:, :], draw[:, :], AX.X, ALU.max, apply_absolute_value=True))
                dve.tensor_scalar(w_scale[:, :], w_scale[:, :], 1.0 / QMAX, None, ALU.mult)
                link(dve.tensor_scalar(d_scale[:, :], d_scale[:, :], 1.0 / QMAX, None, ALU.mult))
                dve.reciprocal(w_inv[:, :], w_scale[:, :])
                link(dve.reciprocal(d_inv[:, :], d_scale[:, :]))
                for j in range(2 * J):
                    i = dve.tensor_scalar(wraw[:, j, :], wraw[:, j, :], w_inv[:, j:j + 1], ROUND, ALU.mult, ALU.add)
                link(dve.tensor_scalar(draw[:, :], draw[:, :], d_inv[:, 0:1], ROUND, ALU.mult, ALU.add))
                for v, _ in ((wraw[:, :, :], 0), (draw[:, :], 0)):
                    i = dve.tensor_scalar(v, v, ROUND + QMAX, ROUND - QMAX - 1.0, ALU.min, ALU.max)
                link(i)
                dve.tensor_scalar(wq[:, :, :], wraw[:, :, :], ROUND, None, ALU.subtract)
                dve.tensor_scalar(dq[:, :], draw[:, :], ROUND, None, ALU.subtract).then_inc(wq_done, 1)
                dve.tensor_scalar(diag[:, :], st.ident[:, :], d_scale[:, 0:1], None, ALU.mult).then_inc(diag_done, 1)
                dve.wait_ge(clip_done, 1)
                link(dve.tensor_scalar(sig[:, :], sig[:, :], 1.0, None, ALU.add))
                link(dve.reciprocal(sig[:, :], sig[:, :]))
                dve.wait_ge(t_ready, 3)
                dve.tensor_copy(upT[:, 0, :], tbank[0][:, 0:I])
                dve.tensor_copy(upT[:, 1, :], tbank[1][:, 0:I])
                for j, (lo, size) in enumerate(CUTS):
                    dve.tensor_copy(downT[0:size, j, :], tbank[1][0:size, 512 + j * D:512 + (j + 1) * D])
                link(dve.tensor_copy(down_row[:, :], row_bank[0:S, 0:D]))
                dve.wait_ge(m_ready, 1)
                dve.tensor_reduce(etop[:, :], m_bank[0:1, 0:S], AX.X, ALU.max).then_inc(m_read, 1)
                dve.wait_ge(top_ready, 1)
                scales_from(dve, link, top_bank, 0, sx[:, 0:1], inv_x[:, :])
                link(dve.tensor_scalar(h_scale[:, :], w_scale[:, :], sx[:, 0:1], None, ALU.mult))

        with ExitStack() as part_ctx:
            psp = Space(nc, part_ctx, "fu")
            whole = psp.sb("whole", [S, G * D])
            qx = psp.sb("qx", [S, G * D], BF16)
            qxT = [psp.sb(f"qxT{i}", [D, W], BF16) for i in range(2)]
            silu = [psp.sb(f"silu{i}", [D, W]) for i in range(2)]
            tbank = psp.ps("tbank", (128, 1024), BF16)
            gbank = [psp.ps(f"gbank{i}") for i in range(2)]
            ubank = [psp.ps(f"ubank{i}") for i in range(2)]
            (rounded, clipped, qx_ready, t_ready, t_read, g_ready, u_ready, g_read, h_made, h_top) = [
                psp.sem(n) for n in ("rounded", "clipped", "qx_ready", "t_ready", "t_read", "g_ready", "u_ready",
                                     "g_read", "h_made", "h_top")]
            gate = psp.sem("gate")
            block = part_ctx.enter_context(nc.Block())
            ITEMS, PER = GROUPS * J, 2 * J

            @block.scalar
            def _(act):
                def step(t):
                    c = t.back(-2 * J)
                    if t.phase(J) == 0 and c.exists(ITEMS):
                        g = c.index(J)
                        first = g * G
                        at_least(act, qx_ready, g)
                        act.activation(whole[:, :], e_all[:, bass.ds(first, G), :].rearrange("p b d -> p (b d)"),
                                       ACT.Identity, bias=round_up[0:S, 0:1], scale=inv_x[0:S, 0:1]).then_inc(rounded, 1)
                    if t.exists(ITEMS):
                        k, j = t.index(), t.phase(J)
                        size = CUTS[j][1]
                        at_least(act, g_ready, k + 1)
                        at_least(act, h_made, k - 1)
                        act.activation(silu[t.phase(2)][0:size, :], gbank[t.phase(2)][0:size, 0:W], ACT.Silu,
                                       scale=h_scale[0:size, j:j + 1]).then_inc(g_read, 1)
                    c = t.back(-J)
                    if t.phase(J) == 1 and c.exists(ITEMS):
                        g = c.index(J)
                        at_least(act, t_ready, g + 1)
                        at_least(act, u_ready, (g - 1) * J)
                        act.activation(qxT[c.phase(PER) // J][:, :], tbank[:, 0:W], ACT.Copy).then_inc(t_read, 1)

                run_steps(act, step, 2 * J, ITEMS, 0, PER, 1)

            @block.gpsimd
            def _(pool):
                def step(t):
                    c = t.back(-2 * J)
                    if t.phase(J) == 1 and c.exists(ITEMS):
                        g = c.index(J)
                        at_least(pool, clipped, g + 1)
                        at_least(pool, t_ready, g)
                        pool.sem_inc(gate, 1)
                        pool.tensor_scalar(qx[:, :], whole[:, :], -ROUND, None, ALU.add).then_inc(qx_ready, 1)

                run_steps(pool, step, 2 * J, ITEMS, 0, PER, 1)

            @block.tensor
            def _(pe):
                def step(t):
                    c = t.back(-J)
                    if t.phase(J) == 0 and c.exists(ITEMS):
                        g = c.index(J)
                        at_least(pe, qx_ready, g + 1)
                        at_least(pe, t_read, g)
                        for b in range(G):
                            i = pe.transpose(tbank[:, b * S:(b + 1) * S], qx[:, b * D:(b + 1) * D], st.ident_b[0:S, 0:S])
                        i.then_inc(t_ready, 1)
                    if t.exists(ITEMS):
                        k, g, j = t.index(), t.index(J), t.phase(J)
                        lo, size = CUTS[j]
                        at_least(pe, t_read, g + 1)
                        at_least(pe, h_made, k - 1)
                        at_least(pe, g_read, k - 1)
                        rhs = qxT[t.phase(PER) // J][:, :]
                        pe.matmul(gbank[t.phase(2)][0:size, 0:W], upT[:, 0, lo:lo + size], rhs, start=True, stop=True)\
                            .then_inc(g_ready, 1)
                        pe.matmul(ubank[t.phase(2)][0:size, 0:W], upT[:, 1, lo:lo + size], rhs, start=True, stop=True)\
                            .then_inc(u_ready, 1)

                run_steps(pe, step, J, ITEMS, 0, PER, 1)

            @block.vector
            def _(dve):
                def step(t):
                    c = t.back(-2 * J)
                    if t.phase(J) == 0 and c.exists(ITEMS):
                        g = c.index(J)
                        at_least(dve, rounded, g + 1)
                        dve.tensor_scalar(whole[:, :], whole[:, :], ROUND + QMAX, ROUND - QMAX - 1.0, ALU.min, ALU.max)\
                            .then_inc(clipped, 1)
                    if t.exists(ITEMS):
                        k, g, j = t.index(), t.index(J), t.phase(J)
                        size = CUTS[j][1]
                        at_least(dve, g_read, k + 1)
                        at_least(dve, u_ready, k + 1)
                        start = g * W
                        out = hT[0:size, j, bass.ds(start, W)]
                        dve.scalar_tensor_tensor(out, ubank[t.phase(2)][0:size, 0:W], h_scale[0:size, J + j:J + j + 1],
                                                 silu[t.phase(2)][0:size, :], ALU.mult, ALU.mult).then_inc(h_made, 1)
                    u = t.back(1)
                    if u.exists(ITEMS):
                        k, g, j = u.index(), u.index(J), u.phase(J)
                        size = CUTS[j][1]
                        start = g * W
                        out = hT[0:size, j, bass.ds(start, W)]
                        at_least(dve, h_made, k + 1)
                        dve.tensor_reduce(hm[0:size, bass.ds(k, 1)], out, AX.X, ALU.max, apply_absolute_value=True)\
                            .then_inc(h_top, 1)

                run_steps(dve, step, 2 * J, ITEMS, 1, PER, 1)

        with ExitStack() as part_ctx:
            psp = Space(nc, part_ctx, "fd")
            hmax, htop = psp.sb("hmax", [D, 1]), psp.sb("htop", [1, 1])
            whole = [psp.sb(f"whole{i}", [D, W]) for i in range(J)]
            qh = [psp.sb(f"qh{i}", [D, J, W], BF16) for i in range(2)]
            scaled = psp.sb("scaled", [S, G * D])
            m_bank, top_bank = psp.ps("m_bank"), psp.ps("top_bank")
            ybank = [psp.ps(f"ybank{i}") for i in range(2)]
            (chain, m_ready, m_read, hmax_done, top_ready, scales, rounded, clipped, qh_ready, y_ready, y_read, stored) = [
                psp.sem(n) for n in ("chain", "m_ready", "m_read", "hmax_done", "top_ready", "scales", "rounded", "clipped",
                                     "qh_ready", "y_ready", "y_read", "stored")]
            added, stored_pool = psp.sem("added"), psp.sem("stored_pool")
            block = part_ctx.enter_context(nc.Block())
            ITEMS, PER = GROUPS * J, 2 * J

            @block.tensor
            def _(pe):
                pe.wait_ge(hmax_done, 1)
                pe.transpose(m_bank[0:1, 0:D], hmax[:, :], st.ident[:, :]).then_inc(m_ready, 1)
                pe.wait_ge(m_read, 1)
                pe.matmul(top_bank[:, 0:1], one_row[:, :], htop[:, :], start=True, stop=True).then_inc(top_ready, 1)

                def step(t):
                    u = t.back(3)
                    if u.phase(J) == 2 and u.exists(ITEMS):
                        g, s = u.index(J), u.phase(PER) // J
                        at_least(pe, qh_ready, J * (g + 1))
                        at_least(pe, y_read, g - 1)
                        for b in range(G):
                            for j, (lo, size) in enumerate(CUTS):
                                i = pe.matmul(ybank[s][0:S, b * D:(b + 1) * D], qh[s][0:size, j, b * S:(b + 1) * S],
                                              downT[0:size, j, :], start=(j == 0), stop=(j == J - 1))
                        i.then_inc(y_ready, 1)

                run_steps(pe, step, 0, ITEMS, 4, PER, 1)

            @block.scalar
            def _(act):
                act.wait_ge(scales, 1)

                def step(t):
                    if t.exists(ITEMS):
                        k, g, j = t.index(), t.index(J), t.phase(J)
                        size = CUTS[j][1]
                        start = g * W
                        at_least(act, qh_ready, k - J + 1)
                        act.activation(whole[j][0:size, :], hT[0:size, j, bass.ds(start, W)], ACT.Identity,
                                       bias=round_up[0:size, 0:1], scale=inv_h[0:size, 0:1]).then_inc(rounded, 1)

                run_steps(act, step, 0, ITEMS, 0, PER, 1)

            @block.vector
            def _(dve):
                link = Chain(dve, chain)
                dve.tensor_reduce(hmax[:, :], hm[:, :], AX.X, ALU.max).then_inc(hmax_done, 1)
                dve.wait_ge(m_ready, 1)
                dve.tensor_reduce(htop[:, :], m_bank[0:1, 0:D], AX.X, ALU.max).then_inc(m_read, 1)
                dve.wait_ge(top_ready, 1)
                scales_from(dve, link, top_bank, 1, sx[:, 1:2], inv_h[:, :])
                dve.tensor_scalar(down_row[:, :], down_row[:, :], sx[0:S, 1:2], None, ALU.mult).then_inc(scales, 1)
                dve.wait_ge(scales, 1)

                def step(t):
                    if t.exists(ITEMS):
                        k, j = t.index(), t.phase(J)
                        size = CUTS[j][1]
                        at_least(dve, rounded, k + 1)
                        v = whole[j][0:size, :]
                        dve.tensor_scalar(v, v, ROUND + QMAX, ROUND - QMAX - 1.0, ALU.min, ALU.max).then_inc(clipped, 1)
                    u = t.back(1)
                    if u.exists(ITEMS):
                        k, g, j, s = u.index(), u.index(J), u.phase(J), u.phase(PER) // J
                        size = CUTS[j][1]
                        at_least(dve, clipped, k + 1)
                        at_least(dve, y_ready, g - 1)
                        dve.tensor_scalar(qh[s][0:size, j, :], whole[j][0:size, :], -ROUND, None, ALU.add)\
                            .then_inc(qh_ready, 1)
                    u = t.back(4)
                    if u.phase(J) == 2 and u.exists(ITEMS):
                        g, s = u.index(J), u.phase(PER) // J
                        at_least(dve, y_ready, g + 1)
                        at_least(dve, added, g)
                        dve.tensor_tensor(scaled[:, :].rearrange("p (b d) -> p b d", b=G),
                                          ybank[s][0:S, :].rearrange("p (b d) -> p b d", b=G),
                                          down_row[:, :].rearrange("p (a d) -> p a d", a=1).broadcast_to([S, G, D]),
                                          ALU.mult).then_inc(y_read, 1)
                        dve.wait_ge(y_read, g + 1)
                        first = g * G
                        x = st.xs[:, bass.ds(first, G), :]
                        dve.tensor_tensor(x, scaled[:, :].rearrange("p (b d) -> p b d", b=G), x, ALU.add).then_inc(added, 1)

                run_steps(dve, step, 0, ITEMS, 5, PER, 1)

            def store_places(eng, half, stored):
                with eng.Fori(0, GROUPS) as g:
                    eng.wait_ge(added, g + 1)
                    for b in range(half * G // 2, (half + 1) * G // 2):
                        p = g * G + b
                        n = eng.value_load(st.order[0:1, bass.ds(p, 1)], min_val=0, max_val=NB - 1)
                        eng.dma_start(st.out[bass.ds(n, 1)].rearrange("b s d -> s b d"), st.xs[:, bass.ds(p, 1), :])\
                            .then_inc(stored, 16)
                eng.wait_ge(stored, 16 * NB // 2)

            @block.sync
            def _(sync):
                store_places(sync, 0, stored)

            @block.gpsimd
            def _(pool):
                store_places(pool, 1, stored_pool)


class Stream:
    pass


def rank_sequences(nc, st, ins, causal32):
    with ExitStack() as ctx:
        sp = Space(nc, ctx, "rk")
        sb, sem = sp.sb, sp.sem
        mask8, mask32, far = sb("mask8", [NB, CTX], U8), sb("mask32", [NB, CTX]), sb("far", [NB, CTX])
        table = sb("table", [NB, NB + 2])
        reach, key, rank = sb("reach", [NB, 1]), sb("key", [NB, 1]), sb("rank", [NB, 1])
        diag, above, place, ones = [sb(n, [NB, NB]) for n in ("diag", "above", "place", "ones")]
        number = sb("number", [1, NB])
        bank = sp.ps("bank")
        mask_in, chain, keys_spread, row_ready, place_made, order_ready = [
            sem(n) for n in ("mask_in", "chain", "keys_spread", "row_ready", "place_made", "order_ready")]
        block = ctx.enter_context(nc.Block())

        @block.sync
        def _(sync):
            sync.dma_start(mask8[:, :], ins["mask_BxS2_bk0"]).then_inc(mask_in, 16)

        @block.scalar
        def _(act):
            for dst, name in ((far, "c_far"), (table, "c_table"), (st.ident, "c_ident"), (st.rotT, "c_rotT"),
                              (st.turn, "c_turn"), (st.headmask, "c_headmask"), (causal32, "c_causal")):
                act.dma_start(dst[:], ins[name]).then_inc(st.consts_in, 16)

        @block.tensor
        def _(pe):
            pe.wait_ge(keys_spread, 1)
            pe.matmul(bank[0:NB, 0:NB], ones[:, :], diag[:, :], start=True, stop=True).then_inc(row_ready, 1)
            pe.wait_ge(place_made, 1)
            pe.matmul(bank[0:1, 128:128 + NB], table[:, 0:1], place[:, :], start=True, stop=True)
            pe.matmul(bank[0:S, 256:256 + NB], reach[:, :].broadcast_to([NB, S]), place[:, :], start=True, stop=True)\
                .then_inc(order_ready, 1)

        @block.vector
        def _(dve):
            link = Chain(dve, chain)
            dve.memset(ones[:, :], 1.0)
            dve.wait_ge(mask_in, 16)
            link(dve.tensor_copy(mask32[:, :], mask8[:, :]))
            dve.wait_ge(st.consts_in, 16 * st.n_consts)
            link(dve.tensor_tensor(mask32[:, :], mask32[:, :], far[:, :], ALU.mult))
            link(dve.tensor_reduce(reach[:, :], mask32[:, :], AX.X, ALU.max))
            link(dve.tensor_scalar(key[:, :], reach[:, :], float(NB), None, ALU.mult))
            link(dve.tensor_tensor(key[:, :], key[:, :], table[:, 1:2], ALU.add))
            dve.tensor_scalar(diag[:, :], st.ident[0:NB, 0:NB], key[:, 0:1], None, ALU.mult).then_inc(keys_spread, 1)
            dve.tensor_copy(st.ident_b[:, :], st.ident[:, :])
            dve.tensor_copy(st.causal[:, :, :], causal32[:, :].rearrange("p (a k) -> p a k", a=1)
                            .broadcast_to([S, 4, S]))
            dve.wait_ge(row_ready, 1)
            link(dve.tensor_scalar(above[:, :], bank[0:NB, 0:NB], key[:, 0:1], None, ALU.is_gt))
            link(dve.tensor_reduce(rank[:, :], above[:, :], AX.X, ALU.add))
            dve.tensor_scalar(place[:, :], table[:, 2:NB + 2], rank[:, 0:1], None, ALU.is_equal).then_inc(place_made, 1)
            dve.wait_ge(order_ready, 1)
            dve.tensor_copy(st.reach[:, :], bank[0:S, 256:256 + NB])
            link(dve.tensor_copy(number[:, :], bank[0:1, 128:128 + NB]))
            link(dve.tensor_copy(st.order[:, :], number[:, :]))


def decoder(nc, ins, out):
    with ExitStack() as ctx:
        sp = Space(nc, ctx, "all")
        st = Stream()
        st.xs = sp.sb("xs", [S, NB, D])
        st.stats = sp.sb("stats", [S, NB, 6])
        st.mean = sp.sb("mean", [S, NB])
        st.rstd = sp.sb("rstd", [S, NB])
        st.ident = sp.sb("ident", [D, D])
        st.rotT = sp.sb("rotT", [D, D])
        st.turn = sp.sb("turn", [D, 2, S])
        st.headmask = sp.sb("headmask", [D, D // 8])
        st.ident_b = sp.sb("ident_b", [D, D], BF16)
        st.causal = sp.sb("causal", [S, 4, S], BF16)
        st.consts_in = sp.sem("consts_in")
        st.x_in = [sp.sem(f"x_in{i}") for i in range(3)]
        st.out = out
        causal32 = sp.sb("causal32", [S, S])
        st.order = sp.sb("order", [1, NB], I32)
        st.reach = sp.sb("reach", [S, NB])
        st.n_consts = 7

        st.x = ins["x"]
        rank_sequences(nc, st, ins, causal32)

        attention(nc, st, "a0", True, {n: ins["L0_attn_" + n] for n in ("wq", "bq", "wk", "bk", "wv", "bv", "wo", "bo")})
        cross_attention(nc, st, ins)
        experts(nc, st, ins)
        attention(nc, st, "a1", False, {n: ins["L1_attn_" + n] for n in ("W_qkv", "b_qkv", "W_proj", "b_proj")})
        context_attention(nc, st, ins)
        feed_forward(nc, st, ins)


def _constants():
    hd = 8
    rot = np.zeros((D, D), np.float32)
    for o in range(D):
        d = o % hd
        if d < hd // 2:
            rot[o, o + hd // 2] = -1.0
        else:
            rot[o, o - hd // 2] = 1.0
    freq = (1.0 / np.float32(10000.0) ** (np.arange(0, hd, 2, dtype=np.float32) / np.float32(hd))).astype(np.float32)
    angle = np.arange(S, dtype=np.float32)[:, None] * freq[None, :]
    cos = np.repeat(np.cos(angle), 2, axis=-1).astype(np.float32)
    sin = np.repeat(np.sin(angle), 2, axis=-1).astype(np.float32)
    turn = np.stack([np.tile(cos.T, (D // hd, 1)), np.tile(sin.T, (D // hd, 1))], axis=1)
    headmask = (np.arange(D)[:, None] // hd == np.arange(D // hd)[None, :]).astype(np.float32)
    causal = np.where(np.arange(S)[None, :] <= np.arange(S)[:, None], 0.0, -BIG)
    number = np.arange(NB, dtype=np.float32)[:, None]
    return {
        "c_far": np.tile(CTX - np.arange(CTX, dtype=np.float32), (NB, 1)),
        "c_table": np.concatenate([number, NB - 1 - number, np.tile(number.T, (NB, 1))], axis=1),
        "c_token": np.ascontiguousarray(np.arange(NB * S, dtype=np.float32).reshape(NB, S).T),
        "c_spare": (NB * S + np.arange(32 * D, dtype=np.float32)).reshape(D, 32),
        "c_before": np.triu(np.ones((S, S), np.float32), 1),
        "c_numbers": np.tile(np.concatenate([np.arange(32), D * np.arange(NB * S // D)]).astype(np.float32), (S, 1)),
        "c_ident": np.eye(D, dtype=np.float32),
        "c_rotT": np.ascontiguousarray(rot.T),
        "c_turn": np.ascontiguousarray(turn, dtype=np.float32),
        "c_headmask": headmask,
        "c_pref": np.tile(np.arange(8, 0, -1, dtype=np.float32), (S, 1)),
        "c_causal": causal.astype(np.float32),
    }


def kernel(**inputs):
    import concourse.bacc as bacc
    from concourse.bass_utils import run_bass_kernel_spmd

    nc = bacc.Bacc("TRN2", target_bir_lowering=False, num_devices=1)
    arrays, aps = {}, {}
    for name, value in {**inputs, **_constants()}.items():
        a = np.ascontiguousarray(value)
        arrays[f"in_{name}"] = a
        aps[name] = nc.dram_tensor(f"in_{name}", a.shape, mybir.dt.from_np(a.dtype), kind="ExternalInput").ap()
    out = nc.dram_tensor("out_0", (NB, S, D), F32, kind="ExternalOutput").ap()
    decoder(nc, aps, out)
    r = run_bass_kernel_spmd(nc, [arrays], core_ids=[0])
    return r.results[0]["out_0"]
```
